# Optimizing a Trainium2 kernel written in Bass

```python
import numpy as np
import jax
import jax.numpy as jnp

def _softmax(x, axis=-1):
    return jax.nn.softmax(x, axis=axis)

def _gelu(x):
    return jax.nn.gelu(x, approximate=True)

def _silu(x):
    return jax.nn.silu(x)

def _sigmoid(x):
    return jax.nn.sigmoid(x)

def _layernorm(x, axis=-1, eps=1e-05):
    m = jnp.mean(x, axis=axis, keepdims=True)
    v = jnp.var(x, axis=axis, keepdims=True)
    return (x - m) / jnp.sqrt(v + eps)

def _scatter_add(tgt, idx, src, axis=0):
    return tgt.at[idx].add(src)

def _segment_sum(src, seg, n):
    return jax.ops.segment_sum(src, seg, n)
kernel_name = 'mk_adaln_d2_jaxref_r8_6ec7b6'

def setup_inputs(seed: int=0):
    np.random.seed(seed)
    _w = jnp.asarray

    def _L0_attn_setup():
        import jax, jax.numpy as jnp
        import numpy as np
        EPS = 1.1920929e-07
        NUM_HEADS = 16
        SOFTCAP = 50.0

        def rms_norm(x):
            return x * jax.lax.rsqrt(jnp.mean(x * x, axis=-1, keepdims=True) + EPS)
        key = jax.random.key(seed)
        ks = jax.random.split(key, 5)
        B, S, D = (2, 256, 128)
        x = jax.random.normal(ks[0], (B, S, D), dtype=jnp.float32)
        w_q = jax.random.normal(ks[1], (D, D), dtype=jnp.float32) * 0.02
        w_k = jax.random.normal(ks[2], (D, D), dtype=jnp.float32) * 0.02
        w_v = jax.random.normal(ks[3], (D, D), dtype=jnp.float32) * 0.02
        w_o = jax.random.normal(ks[4], (D, D), dtype=jnp.float32) * 0.02
        return {'x': x, 'w_q': w_q, 'w_k': w_k, 'w_v': w_v, 'w_o': w_o}
    _L0_attn_in = _L0_attn_setup()

    def _L0_ffn_setup():
        import jax, jax.numpy as jnp
        import numpy as np
        HID, FFN, E, K = (128, 512, 8, 2)
        CAP_FACTOR = 1.25
        key = jax.random.key(seed)
        k1, k2, k3, k4 = jax.random.split(key, 4)
        B, T = (4, 256)
        x = jax.random.normal(k1, (B, T, HID), dtype=jnp.float32)
        router_w = jax.random.normal(k2, (E, HID), dtype=jnp.float32) * 0.02
        w1 = jax.random.normal(k3, (E, HID, FFN), dtype=jnp.float32) * 0.02
        w2 = jax.random.normal(k4, (E, FFN, HID), dtype=jnp.float32) * 0.02
        return {'x': x, 'router_w': router_w, 'w1': w1, 'w2': w2}
    _L0_ffn_in = _L0_ffn_setup()
    _L0_c = _w((lambda *s: np.random.randn(*s).astype(np.float32) * 0.05)(32, 128))
    _L0_wmod = _w((lambda *s: np.random.randn(*s).astype(np.float32) * 0.05)(128, 6 * 128) * 128 ** (-0.5))

    def _L1_attn_setup():
        import jax, jax.numpy as jnp
        import numpy as np
        import math
        B, T, C, H = (4, 256, 128, 16)
        HD = C // H
        key = jax.random.key(seed)
        k1, k2, k3 = jax.random.split(key, 3)
        x = jax.random.normal(k1, (B, T, C), dtype=jnp.float32)
        w_attn = jax.random.normal(k2, (C, 3 * C), dtype=jnp.float32) * (1.0 / math.sqrt(C))
        w_proj = jax.random.normal(k3, (C, C), dtype=jnp.float32) * (1.0 / math.sqrt(C))
        return {'x': x, 'w_attn': w_attn, 'w_proj': w_proj}
    _L1_attn_in = _L1_attn_setup()

    def _L1_ffn_setup():
        import jax, jax.numpy as jnp
        import numpy as np
        B, S, H = (2, 128, 128)
        DFF = 256
        E = 8
        TOPK = 2

        def _expert_ffn(x, w1, b1, w2, b2, wg, bg, w3, b3):
            x1 = jnp.einsum('bsh,hf->bsf', x, w1) + b1
            x2 = jnp.einsum('bsh,hf->bsf', x, w2) + b2
            z = x1 * x2
            s = jax.nn.silu(jnp.einsum('bsf,fg->bsg', z, wg) + bg)
            return jnp.einsum('bsg,gh->bsh', s, w3) + b3
        key = jax.random.key(seed)
        ks = jax.random.split(key, 12)
        sc = 0.02
        return {'x': jax.random.normal(ks[0], (B, S, H), jnp.float32), 'gate_w': jax.random.normal(ks[1], (H, E), jnp.float32) * sc, 'gate_b': jnp.zeros((E,), jnp.float32), 'w1': jax.random.normal(ks[2], (E, H, DFF), jnp.float32) * sc, 'b1': jnp.zeros((E, DFF), jnp.float32), 'w2': jax.random.normal(ks[3], (E, H, DFF), jnp.float32) * sc, 'b2': jnp.zeros((E, DFF), jnp.float32), 'wg': jax.random.normal(ks[4], (E, DFF, DFF), jnp.float32) * sc, 'bg': jnp.zeros((E, DFF), jnp.float32), 'w3': jax.random.normal(ks[5], (E, DFF, H), jnp.float32) * sc, 'b3': jnp.zeros((E, H), jnp.float32)}
    _L1_ffn_in = _L1_ffn_setup()
    _L1_c = _w((lambda *s: np.random.randn(*s).astype(np.float32) * 0.05)(32, 128))
    _L1_wmod = _w((lambda *s: np.random.randn(*s).astype(np.float32) * 0.05)(128, 6 * 128) * 128 ** (-0.5))
    _d = {'L0_attn_x': _L0_attn_in['x'], 'L0_attn_w_q': _L0_attn_in['w_q'], 'L0_attn_w_k': _L0_attn_in['w_k'], 'L0_attn_w_v': _L0_attn_in['w_v'], 'L0_attn_w_o': _L0_attn_in['w_o'], 'L0_ffn_router_w': _L0_ffn_in['router_w'], 'L0_ffn_w1': _L0_ffn_in['w1'], 'L0_ffn_w2': _L0_ffn_in['w2'], 'L0_c': _L0_c, 'L0_wmod': _L0_wmod, 'L1_attn_w_attn': _L1_attn_in['w_attn'], 'L1_attn_w_proj': _L1_attn_in['w_proj'], 'L1_ffn_gate_w': _L1_ffn_in['gate_w'], 'L1_ffn_gate_b': _L1_ffn_in['gate_b'], 'L1_ffn_w1': _L1_ffn_in['w1'], 'L1_ffn_b1': _L1_ffn_in['b1'], 'L1_ffn_w2': _L1_ffn_in['w2'], 'L1_ffn_b2': _L1_ffn_in['b2'], 'L1_ffn_wg': _L1_ffn_in['wg'], 'L1_ffn_bg': _L1_ffn_in['bg'], 'L1_ffn_w3': _L1_ffn_in['w3'], 'L1_ffn_b3': _L1_ffn_in['b3'], 'L1_c': _L1_c, 'L1_wmod': _L1_wmod}
    _x0 = _d['L0_attn_x']
    _d['L0_attn_x'] = jax.random.normal(jax.random.fold_in(jax.random.key(seed), 1), (32, 256, 128), dtype=_x0.dtype)
    del _x0
    return _d

def reference(L0_attn_x, L0_attn_w_q, L0_attn_w_k, L0_attn_w_v, L0_attn_w_o, L0_ffn_router_w, L0_ffn_w1, L0_ffn_w2, L0_c, L0_wmod, L1_attn_w_attn, L1_attn_w_proj, L1_ffn_gate_w, L1_ffn_gate_b, L1_ffn_w1, L1_ffn_b1, L1_ffn_w2, L1_ffn_b2, L1_ffn_wg, L1_ffn_bg, L1_ffn_w3, L1_ffn_b3, L1_c, L1_wmod):

    def _L0_attn_ref(x, w_q, w_k, w_v, w_o):
        import jax, jax.numpy as jnp
        import numpy as np
        EPS = 1.1920929e-07
        NUM_HEADS = 16
        SOFTCAP = 50.0

        def rms_norm(x):
            return x * jax.lax.rsqrt(jnp.mean(x * x, axis=-1, keepdims=True) + EPS)
        B, S, D = x.shape
        H = NUM_HEADS
        dk = D // H

        def split_heads(y):
            return y.reshape(B, S, H, dk).transpose(0, 2, 1, 3)
        q = split_heads(x @ w_q.T)
        k = split_heads(x @ w_k.T)
        v = split_heads(x @ w_v.T)
        q = rms_norm(q)
        k = rms_norm(k)
        scores = jnp.einsum('bhqd,bhkd->bhqk', q, k) / jnp.sqrt(jnp.float32(dk))
        scores = jnp.tanh(scores / SOFTCAP) * SOFTCAP
        causal = jnp.tril(jnp.ones((S, S), dtype=bool))
        scores = jnp.where(causal[None, None], scores, -jnp.inf)
        probs = jax.nn.softmax(scores, axis=-1)
        y = jnp.einsum('bhqk,bhkd->bhqd', probs, v)
        y = y.transpose(0, 2, 1, 3).reshape(B, S, D)
        return y @ w_o.T

    def _L0_ffn_ref(x, router_w, w1, w2):
        import jax, jax.numpy as jnp
        import numpy as np
        HID, FFN, E, K = (128, 512, 8, 2)
        CAP_FACTOR = 1.25
        B, T, H = x.shape
        N = B * T
        x_flat = x.reshape(N, H)
        C = max(1, int(CAP_FACTOR * N / E * K))
        logits = x_flat @ router_w.T
        probs = jax.nn.softmax(logits, axis=-1)
        top_v, top_i = jax.lax.top_k(probs, K)
        top_v = top_v / jnp.sum(top_v, axis=-1, keepdims=True)
        out = jnp.zeros_like(x_flat)
        for k in range(K):
            eid = top_i[:, k]
            gate = top_v[:, k]
            onehot = jax.nn.one_hot(eid, E, dtype=jnp.int32)
            pos = jnp.take_along_axis(jnp.cumsum(onehot, axis=0), eid[:, None], axis=1)[:, 0] - 1
            keep = pos < C
            slot = jnp.where(keep, eid * C + pos, E * C)
            buf = jnp.zeros((E * C + 1, H), dtype=x.dtype).at[slot].add(x_flat * keep[:, None].astype(x.dtype))
            expert_in = buf[:E * C].reshape(E, C, H)
            h = jax.nn.gelu(jnp.einsum('ech,ehf->ecf', expert_in, w1), approximate=False)
            y = jnp.einsum('ecf,efh->ech', h, w2)
            tok = y.reshape(E * C, H)[jnp.minimum(slot, E * C - 1)]
            out = out + tok * (gate * keep.astype(x.dtype))[:, None]
        return out.reshape(B, T, H)

    def _L1_attn_ref(x, w_attn, w_proj):
        import jax, jax.numpy as jnp
        import numpy as np
        import math
        B, T, C, H = (4, 256, 128, 16)
        HD = C // H
        b, t, c = x.shape
        qkv = x @ w_attn
        q, k, v = jnp.split(qkv, 3, axis=-1)
        q = q.reshape(b, t, H, HD).transpose(0, 2, 1, 3)
        k = k.reshape(b, t, H, HD).transpose(0, 2, 1, 3)
        v = v.reshape(b, t, H, HD).transpose(0, 2, 1, 3)
        att = jnp.einsum('bhqd,bhkd->bhqk', q, k) * (1.0 / math.sqrt(HD))
        causal = jnp.tril(jnp.ones((t, t), dtype=bool))
        att = jnp.where(causal[None, None, :, :], att, -jnp.inf)
        att = jax.nn.softmax(att, axis=-1)
        y = jnp.einsum('bhqk,bhkd->bhqd', att, v)
        y = y.transpose(0, 2, 1, 3).reshape(b, t, c)
        return y @ w_proj

    def _L1_ffn_ref(x, gate_w, gate_b, w1, b1, w2, b2, wg, bg, w3, b3):
        import jax, jax.numpy as jnp
        import numpy as np
        B, S, H = (2, 128, 128)
        DFF = 256
        E = 8
        TOPK = 2

        def _expert_ffn(x, w1, b1, w2, b2, wg, bg, w3, b3):
            x1 = jnp.einsum('bsh,hf->bsf', x, w1) + b1
            x2 = jnp.einsum('bsh,hf->bsf', x, w2) + b2
            z = x1 * x2
            s = jax.nn.silu(jnp.einsum('bsf,fg->bsg', z, wg) + bg)
            return jnp.einsum('bsg,gh->bsh', s, w3) + b3
        logits = jnp.einsum('bsh,he->bse', x, gate_w) + gate_b
        topv, topi = jax.lax.top_k(logits, TOPK)
        probs = jax.nn.softmax(topv, axis=-1)
        out = jnp.zeros_like(x)
        for e in range(E):
            we = jnp.sum(probs * (topi == e), axis=-1)
            y = _expert_ffn(x, w1[e], b1[e], w2[e], b2[e], wg[e], bg[e], w3[e], b3[e])
            out = out + we[..., None] * y
        return out
    x = L0_attn_x
    mod = (_silu(L0_c) @ L0_wmod).reshape(L0_c.shape[0], 6, 1, -1)
    sa, ca, ga, sb, cb, gb = (mod[:, 0], mod[:, 1], mod[:, 2], mod[:, 3], mod[:, 4], mod[:, 5])
    ga = (2 * (ga >= 0) - 1) * jnp.maximum(jnp.abs(ga), 0.25)
    gb = (2 * (gb >= 0) - 1) * jnp.maximum(jnp.abs(gb), 0.25)
    h = _layernorm(x, axis=-1) * (1 + ca) + sa
    x = x + ga * _L0_attn_ref(h, L0_attn_w_q, L0_attn_w_k, L0_attn_w_v, L0_attn_w_o)
    h = _layernorm(x, axis=-1) * (1 + cb) + sb
    x = x + gb * _L0_ffn_ref(h, L0_ffn_router_w, L0_ffn_w1, L0_ffn_w2)
    mod = (_silu(L1_c) @ L1_wmod).reshape(L1_c.shape[0], 6, 1, -1)
    sa, ca, ga, sb, cb, gb = (mod[:, 0], mod[:, 1], mod[:, 2], mod[:, 3], mod[:, 4], mod[:, 5])
    ga = (2 * (ga >= 0) - 1) * jnp.maximum(jnp.abs(ga), 0.25)
    gb = (2 * (gb >= 0) - 1) * jnp.maximum(jnp.abs(gb), 0.25)
    h = _layernorm(x, axis=-1) * (1 + ca) + sa
    x = x + ga * _L1_attn_ref(h, L1_attn_w_attn, L1_attn_w_proj)
    h = _layernorm(x, axis=-1) * (1 + cb) + sb
    x = x + gb * _L1_ffn_ref(h, L1_ffn_gate_w, L1_ffn_gate_b, L1_ffn_w1, L1_ffn_b1, L1_ffn_w2, L1_ffn_b2, L1_ffn_wg, L1_ffn_bg, L1_ffn_w3, L1_ffn_b3)
    return x

_drawn_inputs = setup_inputs


def setup_inputs(seed=0):
    import zlib

    import numpy as np

    out = dict(_drawn_inputs(seed))
    spreads = {'L1_ffn_gate_b': (0.0, 0.8),
     'L1_ffn_b1': (0.0, 0.8),
     'L1_ffn_b2': (0.0, 0.8),
     'L1_ffn_bg': (0.0, 0.8),
     'L1_ffn_b3': (0.0, 1.512)}
    factors = {'L0_attn_w_q': 8.0,
     'L0_attn_w_k': 8.0,
     'L0_attn_w_v': 8.0,
     'L0_attn_w_o': 8.0,
     'L0_ffn_router_w': 6.728,
     'L0_ffn_w1': 5.963,
     'L0_ffn_w2': 5.902,
     'L0_c': 5.645,
     'L0_wmod': 5.645,
     'L1_ffn_gate_w': 3.779,
     'L1_ffn_w1': 8.0,
     'L1_ffn_w2': 8.0,
     'L1_ffn_wg': 8.0,
     'L1_ffn_w3': 8.0}
    for name, (base, spread) in spreads.items():
        noise = np.random.default_rng([zlib.crc32(name.encode()), seed]).standard_normal(out[name].shape)
        drawn = base * np.exp(spread * noise) if base else spread * noise
        out[name] = jnp.asarray(drawn.astype(out[name].dtype))
    for name, factor in factors.items():
        out[name] = (out[name] * factor).astype(out[name].dtype)
    return out
```

```python
import concourse.bass as bass
from concourse import mybir
from contextlib import ExitStack

NB, S, D, H, HD = 32, 256, 128, 16, 8
P = 128
TB = S // P
NT = NB * TB
N = NB * S
E = 8
ST = 256
NJ = (2 * N + E * (ST - 1)) // ST
HI = NJ * ST // P
CAP = int(1.25 * N / E * 2)
FF0, FF1 = 512, 256
EPS, QK_EPS = 1e-5, 1.1920929e-07
SOFTCAP = 50.0
QK_SCALE = HD ** -0.5
SLOT = (32, 64)
MAGIC = 0x5F3759DF
MASKED = -1e30
EMPTY = 1 << 20


class Batch:

    def __init__(self, half, parity):
        self.half, self.parity = half, parity

    def index(self, factor=1, offset=0):
        return self.half * (2 * factor) + (self.parity * factor + offset)

    def next(self):
        return Batch(self.half + self.parity, 1 - self.parity)

    def prev(self):
        return Batch(self.half - (1 - self.parity), 1 - self.parity)


class Tile:

    def __init__(self, quarter, phase):
        self.quarter, self.phase = quarter, phase

    def index(self, factor=1, offset=0):
        return self.quarter * (4 * factor) + (self.phase * factor + offset)

    def ahead(self, n):
        return Tile(self.quarter + (self.phase + n) // 4, (self.phase + n) % 4)


def wait(eng, sem, value):
    if not isinstance(value, int) or value > 0:
        eng.wait_ge(sem, value)


def passed(eng, counter):
    eng.sem_inc(counter, 1)


class Chain:

    def __init__(self, eng, sem, steps, turn):
        self.eng, self.sem, self.steps, self.turn, self.n = eng, sem, steps, turn, 0

    def link(self, *instructions):
        for ins in instructions:
            ins.then_inc(self.sem, 1)
        self.n += len(instructions)
        assert self.n <= self.steps, self.n
        self.eng.wait_ge(self.sem, self.turn(self.steps, self.n))

    def end(self):
        assert self.n == self.steps, (self.n, self.steps)


def adaln_kernel(nc, x, c_t, wmod, wqkv, wo, router, gate_b, exp0, exp1, out):
    f32, bf16, f16, i32 = (mybir.dt.float32, mybir.dt.bfloat16, mybir.dt.float16, mybir.dt.int32)
    ALU, ACT, AX = mybir.AluOpType, mybir.ActivationFunctionType, mybir.AxisListType
    ds = bass.ds
    W_E = (exp0.shape[2], exp1.shape[2])

    with ExitStack() as ctx:
        def sb(name, shape, dt=f32):
            return ctx.enter_context(nc.sbuf_tensor(name, shape, dt))

        def sem(name):
            return ctx.enter_context(nc.semaphore(name))

        def dram(name, shape, dt=f32):
            return nc.dram_tensor(name, shape, dt, kind="Internal").ap()

        mod_dram = dram("mod_dram", [2 * NB, 6 * D])
        h_dram = [dram(f"h_dram{l}", [N, D]) for l in range(2)]
        y_dram = [dram(f"y_dram{l}", [2 * N, D]) for l in range(2)]

        X = sb("X", [P, NT * D])
        Xt = X[:, :]
        LG = [sb(f"LG{l}", [P, NT * E]) for l in range(2)]
        G = [sb(f"G{l}", [P, 2 * NT]) for l in range(2)]
        wqkv_sb = sb("wqkv_sb", [P, 2, 3 * D])
        wo_sb = sb("wo_sb", [P, 2, D])
        router_sb = sb("router_sb", [P, 2, E])
        gate_b_sb = sb("gate_b_sb", [P, E])
        identf = sb("identf", [P, P])
        identb = sb("identb", [P, P], bf16)
        identh = sb("identh", [P, P], f16)
        causal = sb("causal", [P, P], bf16)
        ps = ctx.enter_context(nc.psum_tensor("ps", [P, 8, 512], f32))

        modF = [sb(f"modF{i}", [P, 2 * D]) for i in range(2)]
        modB = [sb(f"modB{i}", [P, 3 * D]) for i in range(2)]
        modG = [sb(f"modG{i}", [P, D]) for i in range(2)]
        yin = [sb(f"yin{i}", [P, 2, 2, D]) for i in range(2)]
        ycomb = sb("ycomb", [P, 2, D])
        stF = sb("stF", [P, 2, 6])
        mvF = sb("mvF", [P, 2, 2])
        nwF = sb("nwF", [P, 4, 64])
        hF = [sb(f"hF{i}", [P, 2, D]) for i in range(2)]
        hT = sb("hT", [P, 2, D])
        qkv = [sb(f"qkv{i}", [P, 2, 3 * D]) for i in range(2)]
        qk2 = sb("qk2", [P, 512])
        qk3 = sb("qk3", [P, 512])
        pieces = sb("pieces", [P, 3, 512], bf16)
        ms = sb("ms", [P, 64])
        Qx = sb("Qx", [P, 2 * H * 64], bf16)
        Kx = sb("Kx", [P, 2 * H * 64], bf16)
        QT = [sb(f"QT{i}", [P, 8 * S], bf16) for i in range(2)]
        QTa = sb("QTa", [P, 8 * S], bf16)
        KT = [sb(f"KT{i}", [P, 2 * 8 * S], bf16) for i in range(2)]
        Vx = [sb(f"Vx{i}", [P, 2, H, 32]) for i in range(2)]
        tanh = [sb(f"tanh{i}", [P, 1024]) for i in range(2)]
        probs_all = sb("probs_all", [P, 2 * 3072])
        probs = [probs_all[:, i * 3072:(i + 1) * 3072] for i in range(2)]
        oT = [sb(f"oT{i}", [P, 1024]) for i in range(2)]
        rec = sb("rec", [P, 2, H])
        y = sb("y", [P, 2, D])
        yT = sb("yT", [P, 2, D])
        attn = sb("attn", [P, 2, D])
        stB = sb("stB", [P, 2, 6])
        mvB = sb("mvB", [P, 2, 2])
        nwB = sb("nwB", [P, 4, 2])
        hB = [sb(f"hB{i}", [P, 2, D]) for i in range(2)]
        h2T = sb("h2T", [P, 2, D])
        mxr = sb("mxr", [P, 4, 2 * H])

        iota_i = sb("iota_i", [P, 2 * NT + HI + NJ + 3 * E], i32)
        iota_f = sb("iota_f", [P, 2 * NT + HI + NJ + 3 * E])
        lane, block_no, tile_no, expert_no, row_no, pair_no = (
            iota_f[:, 0:P], iota_f[:, P:P + HI], iota_f[:, P + HI:P + HI + NJ],
            iota_f[:, P + HI + NJ:P + HI + NJ + E], iota_f[:, P + HI + NJ + E:P + HI + NJ + E + 1], iota_f[:, 0:P])
        lane_b, block_b = sb("lane_b", [P, P], bf16), sb("block_b", [P, HI], bf16)
        pair_base = sb("pair_base", [P, 2 * NT])
        before = sb("before", [P, P], bf16)
        onesb = sb("onesb", [P, P], bf16)
        chosen = sb("chosen", [P, 2, E, NT], bf16)
        rt = [tanh[0], tanh[1], oT[0], oT[1], QTa[:, :].bitcast(f32)]
        small = sb("small", [P, 8, 2 * E])
        top = sb("top", [P, 6, NT])
        slots = sb("slots", [P, 5, 2 * NT])
        eid = sb("eid", [P, NJ], i32)
        permA = [sb(f"permA{i}", [P, 8, P], bf16) for i in range(2)]
        permB = [sb(f"permB{i}", [P, 8, 2, HI], bf16) for i in range(2)]
        inv = sb("inv", [P, 4, HI])
        gat_i, sca_i = sb("gat_i", [P, HI], i32), sb("sca_i", [P, HI], i32)

        we = [probs_all[:, i * 1536:i * 1536 + max(W_E)] for i in range(4)]
        idx = [sb(f"idx{i}", [P, 4], i32) for i in range(4)]
        xg = [sb(f"xg{i}", [P, 2, D]) for i in range(4)]
        xT = [sb(f"xT{i}", [P, ST]) for i in range(2)]
        hid = tanh
        hz = [oT[i][:, 0:512] for i in range(2)]
        yo = [sb(f"yo{i}", [P, 2, D]) for i in range(4)]

        setup_dma, setup_pool, setup_pe, setup_dve, setup_act = (
            sem("setup_dma"), sem("setup_pool"), sem("setup_pe"), sem("setup_dve"), sem("setup_act"))
        mod_stored, x_loaded = sem("mod_stored"), [sem("x_loaded0"), sem("x_loaded1")]

        final_dve = sem("final_dve")
        final_used, final_in, stored = sem("final_used"), [sem("final_in0"), sem("final_in1")], sem("stored")
        dve_passed, pool_passed = sem("dve_passed"), sem("pool_passed")

        L = [{}, {}]
        for l in range(2):
            names = {}
            own = (("qk_psum", "tanh_done", "hidden_ready"),
                   ("slots_act", "tq_psum", "tk_psum", "qa_ready", "k_ready", "max_psum", "max_done", "m_ready",
                    "up_act", "z_ready", "mid_psum", "s_ready"))[l]
            for name in own + ("front_dve", "front_pool", "xn_ready", "h_ready", "hT_psum", "hT_ready", "qkv_psum",
                               "qkv_ready", "slots_ready", "qk_ready", "v_ready", "score_psum", "exp_done", "masked",
                               "pv_psum", "o_ready", "ot_psum", "y_ready", "yT_psum", "yT_ready", "proj_psum",
                               "back_dve", "x1_ready", "back_pool", "xn2_ready", "h2_ready", "h2T_psum", "h2T_ready",
                               "router_psum", "logits_ready",
                               "route_dve", "gate_in", "gate_exp", "onehot_ready", "prefix_psum", "perm_ready",
                               "perm_used", "index_ready", "index_copied", "xT_psum", "xT_ready", "up_psum",
                               "down_psum", "y_out"):
                names[name] = sem(f"{name}{l}")
            for name, n in (("modF_in", 2), ("modB_in", 2), ("h2_out", 2), ("weights_in", 4), ("gathered", 4), ("scattered", 4)):
                names[name] = [sem(f"{name}{l}{i}") for i in range(n)]
            L[l] = names
        L[1]["y_in"] = [sem(f"y_in{i}") for i in range(2)]

        FRONT = (37, 35)
        BACK = 19
        QK_STEPS = (5, 1)
        PIECES_DONE = 27
        PIECES = ((0, 0, 3), (1, 3 * HD, 2), (2, 5 * HD, 1))
        BIAS = 1280
        ROUTE = (64, 64)

        block = ctx.enter_context(nc.Block())

        def steps(eng, first, step):
            first(Batch(0, 0))
            step(Batch(0, 0), True, False)
            step(Batch(0, 1), True, True)
            step(Batch(1, 0), True, True)
            with eng.Fori(1, NB // 2 - 1) as i:
                step(Batch(i, 1), True, True)
                step(Batch(i + 1, 0), True, True)
            step(Batch(NB // 2 - 1, 1), False, True)
            step(Batch(NB // 2, 0), False, None)

        def tiles(eng, before_first, step):
            before_first()
            step(Tile(0, 0), True, True, True, False)
            for r in range(1, 5):
                step(Tile(r // 4, r % 4), True, True, True, True)
            with eng.Fori(1, (NJ - 3) // 4) as i:
                for r in range(1, 5):
                    step(Tile(i + r // 4, r % 4), True, True, True, True)
            step(Tile(NJ // 4, (NJ - 2) % 4), True, False, True, True)
            step(Tile(NJ // 4, (NJ - 1) % 4), False, False, True, True)
            step(Tile(NJ // 4, NJ % 4), False, False, False, True)

        def flags(front, back):
            return front, back is not None, back is not False

        def heads(l):
            return P // SLOT[l]

        def chunk_blocks(c):
            half, kind = c // 3, c % 3
            if kind < 2:
                return [(i * S, S, half * 8 + kind * 4 + i, 0, 0) for i in range(4)]
            return [(i * P, P, half * 8 + i, 1, P) for i in range(8)]

        @block.sync
        def _(sp):
            sp.dma_start(wqkv_sb[:, :, :], wqkv.rearrange("l p n -> p l n")).then_inc(setup_dma, 16)
            sp.dma_start(wo_sb[:, :, :], wo.rearrange("l p n -> p l n")).then_inc(setup_dma, 16)
            sp.dma_start(router_sb[:, :, :], router.rearrange("l p n -> p l n")).then_inc(setup_dma, 16)
            sp.dma_start(gate_b_sb[:, :], gate_b).then_inc(setup_dma, 16)
            sp.dma_start(probs[0][:, 0:1536].rearrange("p (l n) -> p l n", l=2),
                         wmod.rearrange("l p n -> p l n")).then_inc(setup_dma, 16)
            sp.dma_start(tanh[0][:, 0:2 * NB].rearrange("p (l n) -> p l n", l=2),
                         c_t.rearrange("l p n -> p l n")).then_inc(setup_dma, 16)
            sp.wait_ge(setup_dve, 12)
            for l in range(2):
                sp.dma_start(mod_dram[l * NB:(l + 1) * NB, :], probs[1][0:NB, l * 768:(l + 1) * 768]).then_inc(mod_stored, 16)
            sp.wait_ge(mod_stored, 32)

            def rows(l, b, first, n):
                return mod_dram[ds(b.index(1, l * NB), 1), first:first + n].to_broadcast([P, n])

            for l in range(2):
                q = L[l]

                def front_loads(b):
                    wait(sp, q["h_ready"], b.index(1, -1))
                    if l == 0:
                        sp.dma_start(Xt[:, ds(b.index(S), S)].rearrange("p (t c) -> p t c", t=2),
                                     x[ds(b.index(S), S), :].rearrange("(t p) c -> p t c", p=P)).then_inc(x_loaded[b.parity], 16)
                    else:
                        wait(sp, q["h_ready"], b.index(1, -1))
                        for k in range(2):
                            sp.dma_start(yin[b.parity][:, k, :, :],
                                         y_dram[0][ds(b.index(S, k * N), S), :].rearrange("(t p) c -> p t c", p=P)).then_inc(q["y_in"][b.parity], 16)
                        sp.dma_start(modG[b.parity][:, :], rows(0, b, 5 * D, D)).then_inc(q["y_in"][b.parity], 16)
                    sp.dma_start(modF[b.parity][:, :], rows(l, b, 0, 2 * D)).then_inc(q["modF_in"][b.parity], 16)

                def back_loads(b):
                    wait(sp, q["h2_ready"], b.index(1, -1))
                    sp.dma_start(modB[b.parity][:, :], rows(l, b, 2 * D, 3 * D)).then_inc(q["modB_in"][b.parity], 16)

                def back_stores(b):
                    sp.wait_ge(q["h2_ready"], b.index(1, 1))
                    sp.dma_start(h_dram[l][ds(b.index(S), S), :].rearrange("(t p) c -> p t c", p=P),
                                 hB[b.parity][:, :, :]).then_inc(q["h2_out"][b.parity], 16)

                def step(b, front, back):
                    f, a, k = flags(front, back)
                    if a:
                        back_loads(b)
                    if f:
                        front_loads(b.next())
                    if k:
                        back_stores(b.prev())

                steps(sp, front_loads, step)
                for i in range(2):
                    sp.wait_ge(q["h2_out"][i], 16 * (NB // 2))
                exp = (exp0, exp1)[l]
                sp.wait_ge(q["index_ready"], 2)

                def weights(j):
                    wait(sp, q["y_out"], j.index(1, -3))
                    e = sp.value_load(eid[0:1, ds(j.index(), 1)], min_val=0, max_val=E - 1)
                    sp.dma_start(we[j.phase][:, 0:W_E[l]], exp[ds(e, 1), :, :].rearrange("e p n -> p (e n)")).then_inc(q["weights_in"][j.phase], 16)

                def w_first():
                    weights(Tile(0, 0))
                    weights(Tile(0, 1))

                def w_step(j, up, transposed, mid, down):
                    if transposed:
                        weights(j.ahead(2))

                tiles(sp, w_first, w_step)
                for r in range(4):
                    sp.wait_ge(q["scattered"][r], 32 * len(range(r, NJ, 4)))

            q = L[1]

            def final_loads(b):
                wait(sp, final_used, b.index(1, -1))
                for k in range(2):
                    sp.dma_start(yin[b.parity][:, k, :, :],
                                 y_dram[1][ds(b.index(S, k * N), S), :].rearrange("(t p) c -> p t c", p=P)).then_inc(final_in[b.parity], 16)
                sp.dma_start(modG[b.parity][:, :], rows(1, b, 5 * D, D)).then_inc(final_in[b.parity], 16)

            def store(b):
                sp.wait_ge(final_used, b.index(1, 1))
                sp.dma_start(out[ds(b.index(S), S), :].rearrange("(t p) c -> p t c", p=P),
                             Xt[:, ds(b.index(S), S)].rearrange("p (t c) -> p t c", t=2)).then_inc(stored, 16)

            final_loads(Batch(0, 0))
            final_loads(Batch(0, 1))
            with sp.Fori(0, NB // 2 - 1) as i:
                for p in range(2):
                    final_loads(Batch(i + 1, p))
                    store(Batch(i, p))
            for p in range(2):
                store(Batch(NB // 2 - 1, p))
            sp.wait_ge(stored, 16 * NB)


        @block.gpsimd
        def _(pool):
            def one(ins):
                ins.then_inc(setup_pool, 1)

            one(nc.gpsimd.memset(identf[:, :], 0.0))
            one(nc.gpsimd.memset(identb[:, :], 0.0))
            one(nc.gpsimd.memset(identh[:, :], 0.0))
            one(nc.gpsimd.memset(causal[:, :], 0.0))
            pool.wait_ge(setup_pool, 4)
            for m in (identf, identb, identh):
                one(nc.gpsimd.affine_select(out=m[:, :], in_=m[:, :], compare_op=ALU.not_equal, fill=1.0,
                                            base=0, pattern=[[-1, P]], channel_multiplier=1))
            one(nc.gpsimd.affine_select(out=causal[:, :], in_=causal[:, :], compare_op=ALU.is_ge, fill=MASKED,
                                        base=0, pattern=[[-1, P]], channel_multiplier=1))
            for i in range(2):
                one(nc.gpsimd.memset(Vx[i][:, :, :, :], 0.0))
                one(nc.gpsimd.memset(KT[i][:, :].bitcast(f32), 0.0))
            one(nc.gpsimd.memset(Qx[:, :].bitcast(f32), 0.0))
            one(nc.gpsimd.memset(Kx[:, :].bitcast(f32), 0.0))
            pool.wait_ge(setup_pool, 14)
            for i in range(2):
                one(nc.gpsimd.memset(Vx[i][:, :, :, HD:HD + 1], 1.0))
            one(nc.gpsimd.iota(iota_i[:, 0:P], [[1, P]], base=0, channel_multiplier=0))
            one(nc.gpsimd.iota(iota_i[:, P:P + HI], [[1, HI]], base=0, channel_multiplier=0))
            one(nc.gpsimd.iota(iota_i[:, P + HI:P + HI + NJ], [[1, NJ]], base=0, channel_multiplier=0))
            one(nc.gpsimd.iota(iota_i[:, P + HI + NJ:P + HI + NJ + E], [[1, E]], base=-E, channel_multiplier=0))
            one(nc.gpsimd.iota(iota_i[:, P + HI + NJ + E:P + HI + NJ + 2 * E], [[0, E]], base=1, channel_multiplier=1))
            one(nc.gpsimd.memset(onesb[:, :], 1.0))
            one(nc.gpsimd.memset(before[:, :], 1.0))
            pool.wait_ge(setup_pool, 23)
            one(nc.gpsimd.affine_select(out=before[:, :], in_=before[:, :], compare_op=ALU.is_gt, fill=0.0,
                                        base=0, pattern=[[1, P]], channel_multiplier=-1))
            pool.wait_ge(setup_pool, 24)

            for l in range(2):
                q = L[l]

                def front(b):
                    pool.wait_ge(q["xn_ready"], b.index(2, 2))
                    pool.wait_ge(q["modF_in"][b.parity], b.half * 16 + 16)
                    c = Chain(pool, q["front_pool"], 1, b.index)
                    for_all = hF[b.parity][:, :, :]
                    c.link(nc.gpsimd.tensor_tensor(for_all, for_all, modF[b.parity][:, D:2 * D].unsqueeze(1).to_broadcast([P, 2, D]), ALU.mult))
                    nc.gpsimd.tensor_tensor(for_all, for_all, modF[b.parity][:, 0:D].unsqueeze(1).to_broadcast([P, 2, D]),
                                            ALU.add).then_inc(q["h_ready"], 1)
                    c.end()

                def values(b):
                    pool.wait_ge(q["qkv_ready"], b.index(2, 2))
                    wait(pool, q["pv_psum"], b.index(2, -2))
                    passed(pool, pool_passed)
                    nc.gpsimd.tensor_copy(Vx[b.parity][:, :, :, 0:HD],
                                          qkv[b.parity][:, :, 2 * D:3 * D].rearrange("p t (h d) -> p t h d", h=H)).then_inc(q["v_ready"], 1)

                def mask(b, c):
                    pool.wait_ge(q["exp_done"], b.index(6, c + 1))
                    half, kind = c // 3, c % 3
                    v = probs[half][:, kind * 1024:(kind + 1) * 1024]
                    v = v.rearrange("p (h n) -> p h n", h=4 if kind < 2 else 8)[:, :, 0:P]
                    passed(pool, pool_passed)
                    nc.gpsimd.affine_select(out=v, in_=v, compare_op=ALU.is_ge, fill=0.0, base=0,
                                            pattern=[[0, v.shape[1]], [1, P]], channel_multiplier=-1).then_inc(q["masked"], 1)

                def back(b):
                    pool.wait_ge(q["xn2_ready"], b.index(2, 2))
                    c = Chain(pool, q["back_pool"], 1, b.index)
                    v = hB[b.parity][:, :, :]
                    c.link(nc.gpsimd.tensor_tensor(v, v, modB[b.parity][:, 2 * D:3 * D].unsqueeze(1).to_broadcast([P, 2, D]), ALU.mult))
                    nc.gpsimd.tensor_tensor(v, v, modB[b.parity][:, D:2 * D].unsqueeze(1).to_broadcast([P, 2, D]),
                                            ALU.add).then_inc(q["h2_ready"], 1)
                    c.end()

                def first(b):
                    front(b)
                    values(b)

                def step(b, front_, back_):
                    f, a, k = flags(front_, back_)
                    if f:
                        front(b.next())
                    if a:
                        mask(b, 0)
                        mask(b, 1)
                    if f:
                        values(b.next())
                    if a:
                        mask(b, 2)
                        mask(b, 3)
                    if k:
                        back(b.prev())
                    if a:
                        mask(b, 4)
                        mask(b, 5)

                steps(pool, first, step)
                pool.wait_ge(q["index_ready"], 2)
                for i in range(2):
                    pool.wait_ge(q["h2_out"][i], 16 * (NB // 2))

                def gather(j):
                    wait(pool, q["xT_psum"], j.index(1, -3))
                    wait(pool, q["scattered"][j.phase], j.quarter * 32)
                    passed(pool, pool_passed)
                    nc.gpsimd.tensor_copy(idx[j.phase][:, 0:2], gat_i[:, ds(j.index(2), 2)]).then_inc(q["index_copied"], 1)
                    nc.gpsimd.tensor_copy(idx[j.phase][:, 2:4], sca_i[:, ds(j.index(2), 2)]).then_inc(q["index_copied"], 1)
                    pool.wait_ge(q["index_copied"], j.index(2, 2))
                    passed(pool, pool_passed)
                    for s_ in range(2):
                        nc.gpsimd.indirect_dma_start(
                            out=xg[j.phase][:, s_, :], out_offset=None, in_=h_dram[l][:, :],
                            in_offset=bass.IndirectOffsetOnAxis(idx[j.phase][:, s_:s_ + 1], 0)).then_inc(q["gathered"][j.phase], 16)

                def scatter(j):
                    pool.wait_ge(q["y_out"], j.index(1, 1))
                    passed(pool, pool_passed)
                    for s_ in range(2):
                        nc.gpsimd.indirect_dma_start(
                            out=y_dram[l][:, :], out_offset=bass.IndirectOffsetOnAxis(idx[j.phase][:, 2 + s_:3 + s_], 0),
                            in_=yo[j.phase][:, s_, :], in_offset=None,
                            bounds_check=2 * N - 1, oob_is_err=False).then_inc(q["scattered"][j.phase], 16)

                def g_first():
                    for r in range(2):
                        gather(Tile(0, r))

                def g_step(j, up, transposed, mid, down):
                    if transposed:
                        gather(j.ahead(2))
                    if down:
                        scatter(Tile(j.quarter, j.phase - 1) if j.phase else Tile(j.quarter - 1, 3))

                if l == 0:
                    pool.wait_ge(q["logits_ready"], NB)
                    for v in (KT[0], KT[1], Qx, Kx):
                        one(nc.gpsimd.memset(v[:, :].bitcast(f32), 0.0))
                    pool.wait_ge(setup_pool, 28)
                    for piece in range(3):
                        at = 6 * HD + piece
                        one(nc.gpsimd.memset(Kx[:, :].rearrange("p (h n) -> p h n", n=64)[:, :, at:at + 1], 1.0))

                tiles(pool, g_first, g_step)

        @block.scalar
        def _(act):
            act.wait_ge(setup_dma, 96)
            nc.scalar.activation(tanh[1][:, 0:2 * NB], tanh[0][:, 0:2 * NB], ACT.Silu).then_inc(setup_act, 1)

            for l in range(2):
                q = L[l]

                def copy_h(b):
                    act.wait_ge(q["hT_psum"], b.index(1, 1))
                    wait(act, q["qkv_psum"], b.index(2, 0))
                    nc.scalar.activation(hT[:, :, :], ps[:, 4, 0:S].rearrange("p (t c) -> p t c", t=2), ACT.Copy).then_inc(q["hT_ready"], 1)

                def copy_qkv(b):
                    wait(act, q["slots_ready"], b.index(1, -1))
                    wait(act, q["v_ready"], b.index(1, -1))
                    for t in range(2):
                        act.wait_ge(q["qkv_psum"], b.index(2, t + 1))
                        nc.scalar.activation(qkv[b.parity][:, t, :], ps[:, 4 + t, 0:3 * D], ACT.Copy).then_inc(q["qkv_ready"], 1)

                def fill_q(b):
                    act.wait_ge(q["front_dve"], b.index(FRONT[1], PIECES_DONE))
                    v = Qx[:, :].rearrange("p (th n) -> p th n", n=64)
                    wait(act, q["tq_psum"], b.index(2, 0))
                    for piece, at, n in PIECES:
                        src = pieces[:, piece, :].rearrange("p (t q) -> p t q", t=2)[:, :, 0:P]
                        for t in range(2):
                            nc.scalar.activation(
                                v[:, t * H:(t + 1) * H, at:at + n * HD].rearrange("p h (s d) -> p h s d", s=n),
                                src[:, t, :].rearrange("p (h d) -> p h d", h=H).unsqueeze(2).to_broadcast([P, H, n, HD]),
                                ACT.Copy).then_inc(q["slots_act"], 1)

                def softmax(b, c):
                    act.wait_ge(q["score_psum"], b.index(6, c + 1))
                    src = ps[:, 2 * (c % 2):2 * (c % 2) + 2, :].rearrange("p a b -> p (a b)")
                    half, kind = c // 3, c % 3
                    dst = probs[half][:, kind * 1024:(kind + 1) * 1024]
                    wait(act, q["pv_psum"], b.index(2, half - 1))
                    if l == 0:
                        wait(act, q["exp_done"], b.index(6, c - 1))
                        nc.scalar.activation(tanh[c % 2][:, :], src, ACT.Tanh, scale=QK_SCALE / SOFTCAP).then_inc(q["tanh_done"], 1)
                        act.wait_ge(q["tanh_done"], b.index(6, c + 1))
                        nc.scalar.activation(dst, tanh[c % 2][:, :], ACT.Exp, scale=SOFTCAP).then_inc(q["exp_done"], 1)
                    else:
                        nc.scalar.activation(dst, src, ACT.Exp, scale=QK_SCALE).then_inc(q["exp_done"], 1)

                def copy_o(b, half):
                    act.wait_ge(q["pv_psum"], b.index(2, half + 1))
                    wait(act, q["ot_psum"], b.index(2, -2))
                    nc.scalar.activation(oT[b.parity][:, half * 512:(half + 1) * 512], ps[:, 6, :], ACT.Copy).then_inc(q["o_ready"], 1)

                def copy_y(b):
                    act.wait_ge(q["yT_psum"], b.index(1, 1))
                    wait(act, q["proj_psum"], b.index(1, 0))
                    nc.scalar.activation(yT[:, :, :], ps[:, 7, 0:S].rearrange("p (t c) -> p t c", t=2), ACT.Copy).then_inc(q["yT_ready"], 1)

                def copy_h2(b):
                    act.wait_ge(q["h2T_psum"], b.index(1, 1))
                    wait(act, q["router_psum"], b.index(1, 0))
                    nc.scalar.activation(h2T[:, :, :], ps[:, 7, 0:S].rearrange("p (t c) -> p t c", t=2), ACT.Copy).then_inc(q["h2T_ready"], 1)

                def first(b):
                    copy_h(b)
                    copy_qkv(b)
                    if l == 1:
                        fill_q(b)

                def step(b, front, back):
                    f, a, k = flags(front, back)
                    if a:
                        softmax(b, 0)
                    if k:
                        copy_o(b.prev(), 1)
                    if f:
                        copy_h(b.next())
                    if a:
                        softmax(b, 1)
                    if f:
                        copy_qkv(b.next())
                    if a:
                        softmax(b, 2)
                    if k:
                        copy_y(b.prev())
                    if a:
                        softmax(b, 3)
                    if f and l == 1:
                        fill_q(b.next())
                    if a:
                        copy_o(b, 0)
                        softmax(b, 4)
                    if k:
                        copy_h2(b.prev())
                    if a:
                        softmax(b, 5)

                steps(act, first, step)
                act.wait_ge(q["gate_in"], 1)
                nc.scalar.activation(top[:, 5, :], top[:, 4, :], ACT.Exp).then_inc(q["gate_exp"], 1)

                def pair(j):
                    return ps[:, 2 + 2 * (j.phase % 2):4 + 2 * (j.phase % 2), :].rearrange("p a b -> p (a b)")

                def a_step(j, up, transposed, mid, down):
                    if l == 0:
                        if up:
                            hidden(j.ahead(1))
                    else:
                        if up:
                            biased(j.ahead(1))
                        if mid:
                            gated(j)

                def hidden(j):
                    act.wait_ge(q["up_psum"], j.index(1, 1))
                    wait(act, q["down_psum"], j.index(1, -1))
                    nc.scalar.activation(hid[j.phase % 2][:, :], pair(j), ACT.Gelu).then_inc(q["hidden_ready"], 1)

                def biased(j):
                    act.wait_ge(q["up_psum"], j.index(1, 1))
                    wait(act, q["z_ready"], j.index(2, -2))
                    w = we[j.phase]
                    for f in range(2):
                        nc.scalar.activation(hid[j.phase % 2][:, f * ST:(f + 1) * ST], pair(j)[:, f * ST:(f + 1) * ST], ACT.Identity,
                                             bias=w[:, BIAS + f:BIAS + f + 1]).then_inc(q["up_act"], 1)

                def gated(j):
                    act.wait_ge(q["mid_psum"], j.index(1, 1))
                    wait(act, q["down_psum"], j.index(1, -1))
                    w = we[j.phase]
                    for f in range(2):
                        nc.scalar.activation(hid[j.phase % 2][:, 512 + f * ST:512 + (f + 1) * ST], ps[:, 6, f * ST:(f + 1) * ST], ACT.Silu,
                                             bias=w[:, BIAS + 4 + f:BIAS + 5 + f]).then_inc(q["s_ready"], 1)

                tiles(act, (lambda: hidden(Tile(0, 0))) if l == 0 else (lambda: biased(Tile(0, 0))), a_step)

        @block.tensor
        def _(pe):
            pe.wait_ge(setup_pool, 16)
            pe.wait_ge(setup_act, 1)
            for l in range(2):
                sc = tanh[1][:, l * NB:(l + 1) * NB]
                wm = probs[0][:, l * 768:(l + 1) * 768]
                nc.tensor.matmul(ps[0:NB, 2 * l, :], sc, wm[:, 0:512], start=True, stop=True)
                nc.tensor.matmul(ps[0:NB, 2 * l + 1, 0:256], sc, wm[:, 512:768], start=True, stop=True).then_inc(setup_pe, 1)
            pe.wait_ge(setup_dve, 12)
            for l in range(2):
                q = L[l]
                nh = heads(l)
                ng = H // nh
                dt = f16 if l == 0 else bf16
                ident = identh if l == 0 else identb

                def transposed_h(b):
                    pe.wait_ge(q["h_ready"], b.index(1, 1))
                    wait(pe, q["qk_ready"], b.index(QK_STEPS[l], 0))
                    for t in range(2):
                        last = nc.tensor.transpose(ps[:, 4, t * P:(t + 1) * P], hF[b.parity][:, t, :], identf[:, :])
                    last.then_inc(q["hT_psum"], 1)

                def qkv_products(b):
                    pe.wait_ge(q["hT_ready"], b.index(1, 1))
                    for t in range(2):
                        nc.tensor.matmul(ps[:, 4 + t, 0:3 * D], hT[:, t, :], wqkv_sb[:, l, :], start=True, stop=True).then_inc(q["qkv_psum"], 1)

                def transposed_qk(b):
                    pe.wait_ge(q["slots_ready"], b.index(1, 1))
                    for i, src in enumerate((Qx, Kx)):
                        v = src[:, 0:2 * H * SLOT[l]].bitcast(dt)
                        dst = ps[:, 4 + i, :].bitcast(dt)
                        for g in range(ng):
                            for t in range(2):
                                at = (t * H + g * nh) * SLOT[l]
                                last = nc.tensor.transpose(dst[:, g * S + t * P:g * S + (t + 1) * P], v[:, at:at + P], ident[:, :])
                        last.then_inc(q["qk_psum"], 1)

                def slots_transposed(b, src, first, done):
                    v = src[:, 0:2 * H * SLOT[1]]
                    dst = ps[:, 4:6, :].rearrange("p a b -> p (a b)").bitcast(bf16)
                    for g in range(ng):
                        for t in range(2):
                            at = (t * H + g * nh) * SLOT[1]
                            last = nc.tensor.transpose(dst[:, g * S + t * P:g * S + (t + 1) * P], v[:, at:at + P], ident[:, :])
                    last.then_inc(done, 1)

                def transposed_q(b):
                    pe.wait_ge(q["slots_act"], b.index(6, 6))
                    slots_transposed(b, Qx, 0, q["tq_psum"])

                def transposed_k(b):
                    pe.wait_ge(q["slots_ready"], b.index(1, 1))
                    pe.wait_ge(q["qa_ready"], b.index(1, 1))
                    slots_transposed(b, Kx, 0, q["tk_psum"])

                def max_scores(b, m):
                    bank = 4 + m % 2
                    if m < 2:
                        pe.wait_ge(q["k_ready"], b.index(2, 2))
                    else:
                        pe.wait_ge(q["max_done"], b.index(12, m - 1))
                    kv = KT[b.parity][:, :]
                    if m < 8:
                        blocks = [(i * S, S, 2 * m + i, 1) for i in range(2)]
                    else:
                        blocks = [(i * P, P, 4 * (m - 8) + i, 0) for i in range(4)]
                    for col, n, h, qt in blocks:
                        g, i = h // nh, h % nh
                        nc.tensor.matmul(ps[:, bank, col:col + n], QTa[:, g * S + qt * P:g * S + qt * P + P],
                                         kv[:, (i * ng + g) * S:(i * ng + g) * S + n], start=True, stop=False)
                        last = nc.tensor.matmul(ps[:, bank, col + n - P:col + n], identb[:, :], causal[:, :], start=False, stop=True)
                    last.then_inc(q["max_psum"], 1)

                def transposed_qm(b):
                    pe.wait_ge(q["m_ready"], b.index(1, 1))
                    slots_transposed(b, Qx, 0, q["tq_psum"])

                def scores(b, c):
                    wait(pe, q["tanh_done"] if l == 0 else q["exp_done"], b.index(6, c - 1))
                    if c == 0:
                        pe.wait_ge(q["qk_ready"], b.index(QK_STEPS[l], QK_STEPS[l]))
                    flat = ps[:, 2 * (c % 2):2 * (c % 2) + 2, :].rearrange("p a b -> p (a b)")
                    qv, kv = QT[b.parity][:, 0:ng * S].bitcast(dt), KT[b.parity][:, 0:nh * ng * S].bitcast(dt)
                    for col, n, h, kt, q0 in chunk_blocks(c):
                        g, i = h // nh, h % nh
                        last = nc.tensor.matmul(flat[:, col:col + n],
                                                kv[:, (i * ng + g) * S + kt * P:(i * ng + g) * S + kt * P + P],
                                                qv[:, g * S + q0:g * S + q0 + n], start=True, stop=True)
                    last.then_inc(q["score_psum"], 1)

                def values(b, half):
                    pe.wait_ge(q["masked"], b.index(6, 3 * (half + 1)))
                    if half == 0:
                        pe.wait_ge(q["v_ready"], b.index(1, 1))
                    wait(pe, q["o_ready"], b.index(2, half))
                    pr = probs[half]
                    for g in range(2):
                        for kt in range(2):
                            for i in range(4):
                                h = half * 8 + g * 4 + i
                                o = ps[32 * i:32 * i + 32, 6, g * S:(g + 1) * S]
                                v = Vx[b.parity][:, kt, h, :]
                                if kt == 0:
                                    nc.tensor.matmul(o, v, pr[:, g * 1024 + i * S:g * 1024 + (i + 1) * S], start=True, stop=False)
                                else:
                                    last = nc.tensor.matmul(o[:, P:S], v, pr[:, 2048 + (g * 4 + i) * P:2048 + (g * 4 + i + 1) * P],
                                                            start=False, stop=True)
                    last.then_inc(q["pv_psum"], 1)

                def transposed_o(b, t):
                    pe.wait_ge(q["o_ready"], b.index(2, 2))
                    if t == 0:
                        wait(pe, q["logits_ready"], b.index(1, 0))
                    else:
                        pe.wait_ge(q["y_ready"], b.index(2, 1))
                    for g in range(4):
                        last = nc.tensor.transpose(ps[:, 7, g * P:(g + 1) * P], oT[b.parity][:, g * S + t * P:g * S + (t + 1) * P], identf[:, :])
                    last.then_inc(q["ot_psum"], 1)

                def transposed_y(b):
                    pe.wait_ge(q["y_ready"], b.index(2, 2))
                    for t in range(2):
                        last = nc.tensor.transpose(ps[:, 7, t * P:(t + 1) * P], y[:, t, :], identf[:, :])
                    last.then_inc(q["yT_psum"], 1)

                def projection(b):
                    pe.wait_ge(q["yT_ready"], b.index(1, 1))
                    for t in range(2):
                        last = nc.tensor.matmul(ps[:, 7, S + t * P:S + (t + 1) * P], yT[:, t, :], wo_sb[:, l, :], start=True, stop=True)
                    last.then_inc(q["proj_psum"], 1)

                def transposed_h2(b):
                    pe.wait_ge(q["h2_ready"], b.index(1, 1))
                    for t in range(2):
                        last = nc.tensor.transpose(ps[:, 7, t * P:(t + 1) * P], hB[b.parity][:, t, :], identf[:, :])
                    last.then_inc(q["h2T_psum"], 1)

                def router_logits(b):
                    pe.wait_ge(q["h2T_ready"], b.index(1, 1))
                    for t in range(2):
                        last = nc.tensor.matmul(ps[:, 7, S + t * E:S + (t + 1) * E], h2T[:, t, :], router_sb[:, l, :], start=True, stop=True)
                    last.then_inc(q["router_psum"], 1)

                def first(b):
                    transposed_h(b)
                    qkv_products(b)
                    if l == 0:
                        transposed_qk(b)
                    else:
                        transposed_q(b)
                        transposed_k(b)
                        for m in range(12):
                            max_scores(b, m)
                        transposed_qm(b)

                def step(b, front, back):
                    f, a, k = flags(front, back)
                    if a:
                        scores(b, 0)
                        scores(b, 1)
                    if k:
                        values(b.prev(), 1)
                    if f:
                        transposed_h(b.next())
                    if k:
                        transposed_o(b.prev(), 0)
                    if a:
                        scores(b, 2)
                    if f:
                        qkv_products(b.next())
                    if k:
                        transposed_o(b.prev(), 1)
                    if a:
                        scores(b, 3)
                        values(b, 0)
                    if k:
                        transposed_y(b.prev())
                    if a:
                        scores(b, 4)
                    if k:
                        projection(b.prev())
                    if f and l == 0:
                        transposed_qk(b.next())
                    if f and l == 1:
                        transposed_q(b.next())
                        transposed_k(b.next())
                    if a:
                        scores(b, 5)
                    if f and l == 1:
                        for m in range(12):
                            max_scores(b.next(), m)
                    if k:
                        transposed_h2(b.prev())
                        router_logits(b.prev())
                    if f and l == 1:
                        transposed_qm(b.next())

                steps(pe, first, step)
                pe.wait_ge(q["onehot_ready"], 2)
                for k in range(2):
                    rhs = chosen[:, k, :, :].rearrange("p e t -> p (e t)")
                    nc.tensor.matmul(ps[:, k, :], before[:, :], rhs, start=True, stop=True)
                    nc.tensor.matmul(ps[:, 2 + k, :], onesb[:, :], rhs, start=True, stop=True).then_inc(q["prefix_psum"], 1)

                def invert(g, start, stop):
                    pe.wait_ge(q["perm_ready"], g.index(1, 1))
                    a_, b_ = permA[g.parity], permB[g.parity]
                    for r in range(8):
                        last = nc.tensor.matmul(ps[:, 4, 0:2 * HI], a_[:, r, :], b_[:, r, :, :].rearrange("p a b -> p (a b)"),
                                                start=start and r == 0, stop=stop and r == 7)
                    last.then_inc(q["perm_used"], 1)

                groups = 2 * NT // 8
                invert(Batch(0, 0), True, False)
                invert(Batch(0, 1), False, False)
                with pe.Fori(1, groups // 2 - 1) as i:
                    invert(Batch(i, 0), False, False)
                    invert(Batch(i, 1), False, False)
                invert(Batch(groups // 2 - 1, 0), False, False)
                invert(Batch(groups // 2 - 1, 1), False, True)

                def pair(j):
                    return ps[:, 2 + 2 * (j.phase % 2):4 + 2 * (j.phase % 2), :].rearrange("p a b -> p (a b)")

                def transposed_x(j):
                    pe.wait_ge(q["gathered"][j.phase], j.quarter * 32 + 32)
                    wait(pe, q["xT_ready"], j.index(1, -1))
                    for s_ in range(2):
                        last = nc.tensor.transpose(ps[:, j.phase % 2, s_ * P:(s_ + 1) * P], xg[j.phase][:, s_, :], identf[:, :])
                    last.then_inc(q["xT_psum"], 1)

                def up_products(j):
                    pe.wait_ge(q["xT_ready"], j.index(1, 1))
                    pe.wait_ge(q["weights_in"][j.phase], j.quarter * 16 + 16)
                    if l == 0:
                        wait(pe, q["hidden_ready"], j.index(1, -1))
                    else:
                        wait(pe, q["z_ready"], j.index(2, -2))
                    o = pair(j)
                    for f in range(4):
                        last = nc.tensor.matmul(o[:, f * ST:(f + 1) * ST], we[j.phase][:, f * P:(f + 1) * P], xT[j.phase % 2][:, :],
                                                start=True, stop=True)
                    last.then_inc(q["up_psum"], 1)

                def mid_products(j):
                    pe.wait_ge(q["z_ready"], j.index(2, 2))
                    wait(pe, q["s_ready"], j.index(2, 0))
                    for g in range(2):
                        for f in range(2):
                            at = 512 + f * FF1 + g * P
                            last = nc.tensor.matmul(ps[:, 6, g * ST:(g + 1) * ST], we[j.phase][:, at:at + P],
                                                    hz[j.phase % 2][:, f * ST:(f + 1) * ST], start=f == 0, stop=f == 1)
                    last.then_inc(q["mid_psum"], 1)

                def down_products(j):
                    if l == 0:
                        pe.wait_ge(q["hidden_ready"], j.index(1, 1))
                    else:
                        pe.wait_ge(q["s_ready"], j.index(2, 2))
                    wait(pe, q["y_out"], j.index(1, 0))
                    bank = 6 + j.phase % 2 if l == 0 else 7
                    nf, w0, h0 = (4, 512, 0) if l == 0 else (2, 1024, 512)
                    for s_ in range(2):
                        for f in range(nf):
                            last = nc.tensor.matmul(ps[:, bank, s_ * P:(s_ + 1) * P],
                                                    hid[j.phase % 2][:, h0 + f * ST + s_ * P:h0 + f * ST + (s_ + 1) * P],
                                                    we[j.phase][:, w0 + f * P:w0 + (f + 1) * P], start=f == 0, stop=f == nf - 1)
                    last.then_inc(q["down_psum"], 1)

                def p_first():
                    transposed_x(Tile(0, 0))
                    up_products(Tile(0, 0))
                    transposed_x(Tile(0, 1))

                def p_step(j, up, transposed, mid, down):
                    if up:
                        up_products(j.ahead(1))
                    if transposed:
                        transposed_x(j.ahead(2))
                    if mid and l == 1:
                        mid_products(j)
                    if down:
                        down_products(Tile(j.quarter, j.phase - 1) if j.phase else Tile(j.quarter - 1, 3))

                tiles(pe, p_first, p_step)

        @block.vector
        def _(dve):
            V = nc.vector
            m = probs[1][0:NB, 0:1536].rearrange("p (l s c) -> p l s c", l=2, s=6)
            tmp = probs[1][0:NB, 2048:2048 + 512].rearrange("p (l s c) -> p l s c", l=2, s=2)
            n = 0

            def link(ins):
                nonlocal n
                ins.then_inc(setup_dve, 1)
                n += 1
                dve.wait_ge(setup_dve, n)

            dve.wait_ge(setup_pe, 2)
            for l in range(2):
                link(V.tensor_copy(probs[1][0:NB, l * 768:(l + 1) * 768],
                                   ps[0:NB, 2 * l:2 * l + 2, :].rearrange("p a b -> p (a b)")[:, 0:768]))
            for l in range(2):
                sc = m[:, l, 1:5:3, :]
                link(V.tensor_scalar(sc, sc, 1.0, None, ALU.add))
                g = m[:, l, 2:6:3, :]
                sign = tmp[:, l, :, :]
                link(V.tensor_scalar(sign, g, 0.0, 2.0, ALU.is_ge, ALU.mult))
                link(V.tensor_scalar(sign, sign, 1.0, None, ALU.subtract))
                link(V.scalar_tensor_tensor(g, g, -1.0, g, ALU.mult, ALU.max))
                link(V.scalar_tensor_tensor(g, g, 0.25, sign, ALU.max, ALU.mult))

            def rsqrt(c, src, k, eps, work):
                r, v, i0, a = work
                c.link(V.tensor_scalar(v, src, k, eps, ALU.mult, ALU.add))
                c.link(V.tensor_scalar(i0.bitcast(i32), v.bitcast(i32), 1, None, ALU.arith_shift_right))
                c.link(V.tensor_scalar(r.bitcast(i32), i0.bitcast(i32), -1.0, float(MAGIC), ALU.mult, ALU.add))
                for _ in range(3):
                    c.link(V.tensor_tensor(a, r, r, ALU.mult))
                    c.link(V.scalar_tensor_tensor(a, a, -0.5, v, ALU.mult, ALU.mult))
                    c.link(V.scalar_tensor_tensor(r, a, 1.5, r, ALU.add, ALU.mult))

            def combine(c, b, gates, last=None):
                y0, y1 = yin[b.parity][:, 0], yin[b.parity][:, 1]
                gate = [[gates[:, ds(b.index(2, k * NT + t), 1)] for t in range(2)] for k in range(2)]
                c.link(*[V.tensor_scalar(ycomb[:, t, :], y0[:, t, :], gate[0][t], None, ALU.mult) for t in range(2)])
                c.link(*[V.scalar_tensor_tensor(ycomb[:, t, :], y1[:, t, :], gate[1][t], ycomb[:, t, :], ALU.mult, ALU.add) for t in range(2)])
                c.link(V.tensor_tensor(ycomb[:, :, :], ycomb[:, :, :], modG[b.parity][:, :].unsqueeze(1).to_broadcast([P, 2, D]), ALU.mult))
                xb = Xt[:, ds(b.index(S), S)]
                ins = V.tensor_tensor(xb, xb, ycomb[:, :, :].rearrange("p t c -> p (t c)"), ALU.add)
                if last is None:
                    c.link(ins)
                else:
                    ins.then_inc(last, 1)

            dve.wait_ge(setup_pool, 24)
            link(V.tensor_copy(iota_f[:, 0:P + HI + NJ + 2 * E], iota_i[:, 0:P + HI + NJ + 2 * E]))
            link(V.tensor_copy(lane_b[:, :], lane))
            link(V.tensor_copy(block_b[:, :], block_no))
            link(V.tensor_scalar(pair_base[:, :], lane, float(P), None, ALU.mult))

            for l in range(2):
                q = L[l]
                nh = heads(l)
                ng = H // nh
                dt = f16 if l == 0 else bf16

                def normalize(c, b, at, st, mv, nw, dst, done, free, free_at):
                    passed(dve, dve_passed)
                    c.link(*[V.bn_stats(st[:, t, :], Xt[:, ds(b.index(S, t * D), D)]) for t in range(2)])
                    passed(dve, dve_passed)
                    c.link(*[V.bn_aggr(mv[:, t, :], st[:, t, :]) for t in range(2)])
                    w = [nw[:, i, 0:2] for i in range(4)]
                    rsqrt(c, mv[:, :, 1], 1.0, EPS, w)
                    wait(dve, free, free_at)
                    for t in range(2):
                        V.tensor_scalar(dst[:, t, :], Xt[:, ds(b.index(S, t * D), D)], mv[:, t, 0:1], w[0][:, t:t + 1],
                                        ALU.subtract, ALU.mult).then_inc(done, 1)

                chain = {}

                def front_norm(b):
                    c = chain["f"] = Chain(dve, q["front_dve"], FRONT[l], b.index)
                    if l == 0:
                        dve.wait_ge(x_loaded[b.parity], b.half * 16 + 16)
                    else:
                        dve.wait_ge(q["y_in"][b.parity], b.half * 48 + 48)
                        combine(c, b, G[0])
                    normalize(c, b, 0, stF, mvF, nwF, hF[b.parity], q["xn_ready"], q["hT_psum"], b.index(1, -1))

                def front_slots(b):
                    c = chain["f"]
                    dve.wait_ge(q["qkv_ready"], b.index(2, 2))
                    qk = qkv[b.parity][:, :, 0:2 * D]
                    v2 = lambda t: t[:, :].rearrange("p (t n) -> p t n", t=2)
                    if l == 0:
                        c.link(V.tensor_tensor(v2(qk2), qk, qk, ALU.mult))
                        c.link(V.reduce_sum(ms[:, :], qk2[:, :].rearrange("p (h d) -> p h d", d=HD), AX.X))
                        w = [nwF[:, i, :] for i in range(4)]
                        rsqrt(c, ms[:, :], 1.0 / HD, QK_EPS, w)
                        c.link(V.tensor_tensor(qk2[:, :].rearrange("p (t h d) -> p t h d", t=2, d=HD),
                                               qk.rearrange("p t (h d) -> p t h d", d=HD),
                                               w[0].rearrange("p (t h) -> p t h", t=2).unsqueeze(3).to_broadcast([P, 2, 2 * H, HD]), ALU.mult))
                        wait(dve, q["qk_psum"], b.index(2, 0))
                        s = qk2[:, :].rearrange("p (t s h d) -> p t s h d", t=2, s=2, h=H)
                        xs = [t_[:, 0:2 * H * SLOT[0]].bitcast(f16).rearrange("p (t h n) -> p t h n", t=2, h=H) for t_ in (Qx, Kx)]
                        c.link(*[V.tensor_copy(xs[i][:, :, :, 0:HD], s[:, :, i]) for i in range(2)])
                        low = (2 * HD, HD)
                        high = (HD, 2 * HD)
                        for i in range(2):
                            V.tensor_tensor(xs[i][:, :, :, low[i]:low[i] + HD], s[:, :, i], xs[i][:, :, :, 0:HD], ALU.subtract).then_inc(q["front_dve"], 1)
                        for i in range(2):
                            V.tensor_copy(xs[i][:, :, :, high[i]:high[i] + HD], xs[i][:, :, :, 0:HD]).then_inc(q["front_dve"], 1)
                        c.n += 4
                        dve.wait_ge(q["front_dve"], b.index(FRONT[l], c.n))
                        V.memset(nwF[:, 1, 0:1], 0.0).then_inc(q["slots_ready"], 1)
                        c.end()
                    else:
                        pc = [v2(pieces[:, i, :]) for i in range(3)]
                        wait(dve, q["slots_act"], b.index(6, 0))
                        c.link(V.tensor_copy(pc[0], qk))
                        c.link(V.tensor_tensor(v2(qk2), qk, pc[0], ALU.subtract))
                        c.link(V.tensor_copy(pc[1], v2(qk2)))
                        c.link(V.tensor_tensor(v2(qk3), v2(qk2), pc[1], ALU.subtract))
                        c.link(V.tensor_copy(pc[2], v2(qk3)))
                        assert c.n == PIECES_DONE
                        wait(dve, q["tk_psum"], b.index(1, 0))
                        for at, piece in enumerate((0, 1, 2, 0, 1, 0)):
                            last = V.tensor_copy(Kx[:, :].rearrange("p (t h n) -> p t h n", t=2, h=H)[:, :, :, at * HD:(at + 1) * HD],
                                                 pieces[:, piece, :].rearrange("p (t s h d) -> p t s h d", t=2, s=2, h=H)[:, :, 1])
                        last.then_inc(q["slots_ready"], 1)

                def front_copies(b):
                    words = ng * S // 2
                    if l == 1:
                        return front_maxima(b)
                    dve.wait_ge(q["qk_psum"], b.index(2, 1))
                    wait(dve, q["score_psum"], b.index(6, -6))
                    V.tensor_copy(QT[b.parity][:, 0:ng * S].bitcast(i32), ps[:, 4, 0:words].bitcast(i32)).then_inc(q["qk_ready"], 1)
                    dve.wait_ge(q["qk_psum"], b.index(2, 2))
                    n = SLOT[l]
                    for i in range(nh):
                        V.tensor_copy(KT[b.parity][i * n:(i + 1) * n, i * ng * S:(i + 1) * ng * S].bitcast(i32),
                                      ps[i * n:(i + 1) * n, 5, 0:words].bitcast(i32)).then_inc(q["qk_ready"], 1)

                def front_maxima(b):
                    c = chain["f"]
                    both = ps[:, 4:6, :].rearrange("p a b -> p (a b)").bitcast(i32)
                    dve.wait_ge(q["tq_psum"], b.index(2, 1))
                    wait(dve, q["max_psum"], b.index(12, 0))
                    V.tensor_copy(QTa[:, :].bitcast(i32), both).then_inc(q["qa_ready"], 1)
                    dve.wait_ge(q["tk_psum"], b.index(1, 1))
                    wait(dve, q["score_psum"], b.index(6, -6))
                    n = SLOT[1]
                    for i in range(2):
                        V.tensor_copy(KT[b.parity][i * n:(i + 1) * n, i * ng * S:(i + 1) * ng * S].bitcast(i32),
                                      both[i * n:(i + 1) * n, :]).then_inc(q["k_ready"], 1)
                    for m in range(12):
                        dve.wait_ge(q["max_psum"], b.index(12, m + 1))
                        bank = ps[:, 4 + m % 2, :]
                        if m < 8:
                            ins = V.reduce_max(mxr[:, 0, H + 2 * m:H + 2 * m + 2], bank.rearrange("p (h n) -> p h n", h=2), AX.X)
                        else:
                            ins = V.reduce_max(mxr[:, 0, 4 * (m - 8):4 * (m - 8) + 4], bank.rearrange("p (h n) -> p h n", h=4), AX.X)
                        ins.then_inc(q["max_done"], 1)
                    dve.wait_ge(q["max_done"], b.index(12, 12))
                    piece = [Qx[:, :].rearrange("p (h n) -> p h n", n=64)[:, :, 6 * HD + i] for i in range(3)]
                    c.link(V.tensor_scalar(mxr[:, 1, :], mxr[:, 0, :], -1.0, None, ALU.mult))
                    for i in range(2):
                        c.link(V.tensor_copy(piece[i], mxr[:, 1 + i, :]))
                        c.link(V.tensor_tensor(mxr[:, 2 + i, :], mxr[:, 1 + i, :], piece[i], ALU.subtract))
                    V.tensor_copy(piece[2], mxr[:, 3, :]).then_inc(q["m_ready"], 1)
                    dve.wait_ge(q["tq_psum"], b.index(2, 2))
                    V.tensor_copy(QT[b.parity][:, :].bitcast(i32), both).then_inc(q["qk_ready"], 1)
                    for i in range(3):
                        V.memset(piece[i], 0.0).then_inc(q["front_dve"], 1)
                    c.n += 3
                    dve.wait_ge(q["front_dve"], b.index(FRONT[1], c.n))
                    c.end()

                def back_values(b, t):
                    if t == 0:
                        chain["b"] = Chain(dve, q["back_dve"], BACK, b.index)
                        wait(dve, q["yT_psum"], b.index(1, 0))
                    c = chain["b"]
                    dve.wait_ge(q["ot_psum"], b.index(2, t + 1))
                    o = ps[:, 7, :].rearrange("p (h n) -> p h n", n=32)
                    c.link(V.reciprocal(rec[:, t, :], o[:, :, HD]))
                    V.tensor_tensor(y[:, t, :].rearrange("p (h d) -> p h d", d=HD), o[:, :, 0:HD],
                                    rec[:, t, :].unsqueeze(2).to_broadcast([P, H, HD]), ALU.mult).then_inc(q["y_ready"], 1)

                def back_residual(b):
                    c = chain["b"]
                    dve.wait_ge(q["proj_psum"], b.index(1, 1))
                    dve.wait_ge(q["modB_in"][b.parity], b.half * 16 + 16)
                    c.link(V.tensor_tensor(attn[:, :, :], ps[:, 7, S:2 * S].rearrange("p (t c) -> p t c", t=2),
                                           modB[b.parity][:, 0:D].unsqueeze(1).to_broadcast([P, 2, D]), ALU.mult))
                    xb = Xt[:, ds(b.index(S), S)]
                    V.tensor_tensor(xb, xb, attn[:, :, :].rearrange("p t c -> p (t c)"), ALU.add).then_inc(q["x1_ready"], 1)
                    dve.wait_ge(q["x1_ready"], b.index(1, 1))
                    hb = hB[b.parity]
                    wait(dve, q["h2_out"][b.parity], b.half * 16)
                    normalize(c, b, 0, stB, mvB, nwB, hb, q["xn2_ready"], q["h2T_psum"], b.index(1, -1))
                    c.end()

                def back_logits(b):
                    dve.wait_ge(q["router_psum"], b.index(1, 1))
                    V.tensor_copy(LG[l][:, ds(b.index(2 * E), 2 * E)], ps[:, 7, S:S + 2 * E]).then_inc(q["logits_ready"], 1)

                def first(b):
                    front_norm(b)
                    front_slots(b)
                    front_copies(b)

                def step(b, front, back):
                    f, a, k = flags(front, back)
                    if f:
                        front_norm(b.next())
                    if k:
                        back_values(b.prev(), 0)
                        back_values(b.prev(), 1)
                    if f:
                        front_slots(b.next())
                    if k:
                        back_residual(b.prev())
                    if f:
                        front_copies(b.next())
                    if k:
                        back_logits(b.prev())

                steps(dve, first, step)
                dve.wait_ge(q["logits_ready"], NB)

                c = Chain(dve, q["route_dve"], ROUTE[l], lambda steps_, n_: n_)
                te = lambda v: v.rearrange("p (t e) -> p t e", e=E)
                w = [te(rt[i][:, 0:NT * E]) for i in range(5)]
                lg = te(LG[l][:, :])
                tb = lambda v: v.unsqueeze(2).to_broadcast([P, NT, E])
                eb = lambda v: v.unsqueeze(1).to_broadcast([P, NT, E])
                if l == 1:
                    c.link(V.tensor_tensor(lg, lg, eb(gate_b_sb[:, :]), ALU.add))
                for k in range(2):
                    c.link(V.reduce_max(top[:, k, :], lg, AX.X))
                    c.link(V.tensor_tensor(w[0], lg, tb(top[:, k, :]), ALU.is_equal))
                    c.link(V.tensor_tensor(w[0], w[0], eb(expert_no), ALU.mult))
                    c.link(V.tensor_reduce(top[:, 2 + k, :], w[0], AX.X, ALU.min))
                    c.link(V.tensor_tensor(w[1 + k], eb(expert_no), tb(top[:, 2 + k, :]), ALU.is_equal))
                    V.tensor_copy(chosen[:, k, :, :].rearrange("p e t -> p t e"), w[1 + k]).then_inc(q["onehot_ready"], 1)
                    if k == 0:
                        c.link(V.scalar_tensor_tensor(lg, w[1], -3.0e38, lg, ALU.mult, ALU.add))
                V.tensor_tensor(top[:, 4, :], top[:, 1, :], top[:, 0, :], ALU.subtract).then_inc(q["gate_in"], 1)
                dve.wait_ge(q["gate_exp"], 1)
                g0, g1 = G[l][:, 0:NT], G[l][:, NT:2 * NT]
                c.link(V.tensor_scalar(g1, top[:, 5, :], 1.0, None, ALU.add))
                c.link(V.reciprocal(g0, g1))
                c.link(V.tensor_tensor(g1, top[:, 5, :], g0, ALU.mult))

                c.link(V.memset(rt[3][:, :], 1.0))
                c.link(V.memset(rt[3][:, :].rearrange("p (g t) -> p g t", t=NT)[:, :, 0:1], 0.0))
                dve.wait_ge(q["prefix_psum"], 2)
                c.link(V.tensor_copy(rt[2][:, :], ps[:, 2:4, :].rearrange("p a b -> p (a b)")))
                c.link(V.tensor_tensor_scan(rt[1][:, :], rt[3][:, :], rt[2][:, :], 0.0, ALU.mult, ALU.add))
                c.link(V.tensor_tensor(rt[0][:, :], rt[1][:, :], rt[2][:, :], ALU.subtract))
                c.link(V.tensor_tensor(rt[0][:, :], rt[0][:, :], ps[:, 0:2, :].rearrange("p a b -> p (a b)"), ALU.add))
                count = small[:, 0, :]
                ket = lambda v: v.rearrange("p (k e t) -> p k e t", k=2, e=E)
                oh = chosen[:, :, :, :].rearrange("p k e t -> p (k e t)")
                kt = lambda v: v.rearrange("p (k t) -> p k t", k=2)
                if l == 0:
                    c.link(V.tensor_tensor(rt[4][:, :], rt[0][:, :], oh, ALU.mult))
                    c.link(V.reduce_sum(kt(slots[:, 0, :]), ket(rt[4][:, :]).rearrange("p k e t -> p k t e"), AX.X))
                    c.link(V.tensor_scalar(slots[:, 0, :], slots[:, 0, :], float(CAP), None, ALU.is_lt))
                    c.link(V.tensor_tensor(G[0][:, :], G[0][:, :], slots[:, 0, :], ALU.mult))
                c.link(V.tensor_copy(count, rt[1][:, :].rearrange("p (g t) -> p g t", t=NT)[:, :, NT - 1]))
                n_e, n_i, tiles_f, ends, base = (small[:, 1, 0:E], small[:, 2, 0:E].bitcast(i32), small[:, 3, 0:E],
                                                 small[:, 4, 0:E], small[:, 5, :])
                c.link(V.tensor_tensor(n_e, count[:, 0:E], count[:, E:2 * E], ALU.add))
                c.link(V.tensor_scalar(n_e, n_e, float(ST - 1), None, ALU.add))
                c.link(V.tensor_copy(n_i, n_e))
                c.link(V.tensor_scalar(n_i, n_i, ST.bit_length() - 1, None, ALU.arith_shift_right))
                c.link(V.tensor_copy(tiles_f, n_i))
                c.link(V.memset(small[:, 6, 0:E], 1.0))
                c.link(V.tensor_tensor_scan(ends, small[:, 6, 0:E], tiles_f, 0.0, ALU.mult, ALU.add))
                c.link(V.tensor_tensor(base[:, 0:E], ends, tiles_f, ALU.subtract))
                c.link(V.tensor_scalar(base[:, 0:E], base[:, 0:E], float(ST), None, ALU.mult))
                c.link(V.tensor_tensor(base[:, E:2 * E], base[:, 0:E], count[:, 0:E], ALU.add))
                c.link(V.tensor_tensor(rt[0][:, :].rearrange("p (g t) -> p g t", t=NT), rt[0][:, :].rearrange("p (g t) -> p g t", t=NT),
                                       base.unsqueeze(2).to_broadcast([P, 2 * E, NT]), ALU.add))
                c.link(V.tensor_tensor(rt[4][:, :], rt[0][:, :], oh, ALU.mult))
                c.link(V.reduce_sum(kt(slots[:, 0, :]), ket(rt[4][:, :]).rearrange("p k e t -> p k t e"), AX.X))
                slot_i, part_i = slots[:, 1, :].bitcast(i32), slots[:, 2, :].bitcast(i32)
                c.link(V.tensor_copy(slot_i, slots[:, 0, :]))
                c.link(V.tensor_scalar(part_i, slot_i, P - 1, None, ALU.bitwise_and))
                c.link(V.tensor_copy(slots[:, 3, :], part_i))
                c.link(V.tensor_scalar(part_i, slot_i, P.bit_length() - 1, None, ALU.arith_shift_right))
                c.link(V.tensor_copy(slots[:, 4, :], part_i))
                v = rt[4][:, 0:NJ * E].rearrange("p (j e) -> p j e", e=E)
                c.link(V.tensor_tensor(v, ends.unsqueeze(1).to_broadcast([P, NJ, E]), tile_no.unsqueeze(2).to_broadcast([P, NJ, E]), ALU.is_le))
                c.link(V.reduce_sum(inv[:, 0, 0:NJ], v, AX.X))
                c.link(V.tensor_scalar(inv[:, 0, 0:NJ], inv[:, 0, 0:NJ], float(E - 1), None, ALU.min))
                V.tensor_copy(eid[:, :], inv[:, 0, 0:NJ]).then_inc(q["index_ready"], 1)

                def factors(g):
                    wait(dve, q["perm_used"], g.index(1, -1))
                    for r in range(8):
                        at = g.index(8, r)
                        low_, high_ = slots[:, 3, ds(at, 1)], slots[:, 4, ds(at, 1)]
                        V.tensor_scalar(permA[g.parity][:, r, :], lane_b[:, :], low_, None, ALU.is_equal)
                        V.tensor_scalar(permB[g.parity][:, r, 0, :], block_b[:, :], high_, row_no, ALU.is_equal, ALU.mult)
                        last = V.tensor_scalar(permB[g.parity][:, r, 1, :], block_b[:, :], high_, pair_base[:, ds(at, 1)], ALU.is_equal, ALU.mult)
                    last.then_inc(q["perm_ready"], 1)

                factors(Batch(0, 0))
                factors(Batch(0, 1))
                with dve.Fori(1, NT // 8) as i:
                    factors(Batch(i, 0))
                    factors(Batch(i, 1))
                dve.wait_ge(q["perm_used"], NT // 4)
                c.link(V.tensor_copy(inv[:, 0:2, :], ps[:, 4, 0:2 * HI].rearrange("p (a b) -> p a b", a=2)))
                c.link(V.tensor_tensor(inv[:, 0, :], inv[:, 0, :], inv[:, 1, :], ALU.add))
                c.link(V.tensor_scalar(inv[:, 1, :], inv[:, 0, :], 0.0, float(EMPTY), ALU.is_equal, ALU.mult))
                c.link(V.tensor_scalar(inv[:, 2, :], inv[:, 0, :], 1.0, 0.0, ALU.subtract, ALU.max))
                c.link(V.scalar_tensor_tensor(inv[:, 1, :], inv[:, 2, :], 0.0, inv[:, 1, :], ALU.add, ALU.add))
                c.link(V.tensor_copy(sca_i[:, :], inv[:, 1, :]))
                c.link(V.tensor_copy(gat_i[:, :], inv[:, 2, :]))
                V.tensor_scalar(gat_i[:, :], gat_i[:, :], N - 1, None, ALU.bitwise_and).then_inc(q["index_ready"], 1)
                assert c.n <= ROUTE[l], c.n

                def copy_x(j):
                    dve.wait_ge(q["xT_psum"], j.index(1, 1))
                    wait(dve, q["up_psum"], j.index(1, -1))
                    V.tensor_copy(xT[j.phase % 2][:, :], ps[:, j.phase % 2, 0:ST]).then_inc(q["xT_ready"], 1)

                def product(j):
                    dve.wait_ge(q["up_act"], j.index(2, 2))
                    wait(dve, q["mid_psum"], j.index(1, -1))
                    up = ps[:, 2 + 2 * (j.phase % 2):4 + 2 * (j.phase % 2), :].rearrange("p a b -> p (a b)")
                    for f in range(2):
                        V.scalar_tensor_tensor(hz[j.phase % 2][:, f * ST:(f + 1) * ST], up[:, 512 + f * ST:512 + (f + 1) * ST],
                                               we[j.phase][:, BIAS + 2 + f:BIAS + 3 + f], hid[j.phase % 2][:, f * ST:(f + 1) * ST],
                                               ALU.add, ALU.mult).then_inc(q["z_ready"], 1)

                def copy_y(j):
                    dve.wait_ge(q["down_psum"], j.index(1, 1))
                    wait(dve, q["scattered"][j.phase], j.quarter * 32)
                    if l == 0:
                        ins = V.tensor_copy(yo[j.phase][:, :, :], ps[:, 6 + j.phase % 2, 0:2 * P].rearrange("p (s c) -> p s c", s=2))
                    else:
                        ins = V.tensor_tensor(yo[j.phase][:, :, :], ps[:, 7, 0:2 * P].rearrange("p (s c) -> p s c", s=2),
                                              we[j.phase][:, BIAS + 6:BIAS + 6 + D].unsqueeze(1).to_broadcast([P, 2, D]), ALU.add)
                    ins.then_inc(q["y_out"], 1)

                def v_first():
                    copy_x(Tile(0, 0))
                    if l == 1:
                        product(Tile(0, 0))
                    copy_x(Tile(0, 1))

                def v_step(j, up, transposed, mid, down):
                    if transposed:
                        copy_x(j.ahead(2))
                    if up and l == 1:
                        product(j.ahead(1))
                    if down:
                        copy_y(Tile(j.quarter, j.phase - 1) if j.phase else Tile(j.quarter - 1, 3))

                tiles(dve, v_first, v_step)

            def final(b):
                c = Chain(dve, final_dve, 5, b.index)
                dve.wait_ge(final_in[b.parity], b.half * 48 + 48)
                wait(dve, final_used, b.index(1, 0))
                combine(c, b, G[1], final_used)
                c.end()

            for p in range(2):
                final(Batch(0, p))
            with dve.Fori(1, NB // 2) as i:
                for p in range(2):
                    final(Batch(i, p))


def kernel(**inputs):
    import numpy as np
    import concourse.bacc as bacc
    from concourse.bass_utils import run_bass_kernel_spmd

    a = {k: np.asarray(v) for k, v in inputs.items()}

    def chunks(w):
        e, r, m = w.shape
        return w.reshape(e, r // P, P, m).transpose(0, 2, 1, 3).reshape(e, P, -1)

    def columns(v):
        return v.reshape(E, -1, P).transpose(0, 2, 1)

    arrays = {
        "x": a["L0_attn_x"].reshape(N, D),
        "c_t": np.stack([a["L0_c"].T, a["L1_c"].T]),
        "wmod": np.stack([a["L0_wmod"], a["L1_wmod"]]),
        "wqkv": np.stack([np.concatenate([a["L0_attn_w_q"].T, a["L0_attn_w_k"].T, a["L0_attn_w_v"].T], axis=1),
                          a["L1_attn_w_attn"]]),
        "wo": np.stack([a["L0_attn_w_o"].T, a["L1_attn_w_proj"]]),
        "router": np.stack([a["L0_ffn_router_w"].T, a["L1_ffn_gate_w"]]),
        "gate_b": np.repeat(a["L1_ffn_gate_b"][None], P, axis=0),
        "exp0": np.concatenate([chunks(a["L0_ffn_w1"]), chunks(a["L0_ffn_w2"])], axis=2),
        "exp1": np.concatenate([chunks(a["L1_ffn_w1"]), chunks(a["L1_ffn_w2"]), chunks(a["L1_ffn_wg"]), chunks(a["L1_ffn_w3"]),
                                columns(a["L1_ffn_b1"]), columns(a["L1_ffn_b2"]), columns(a["L1_ffn_bg"]),
                                np.repeat(a["L1_ffn_b3"][:, None], P, axis=1)], axis=2),
    }
    arrays = {k: np.ascontiguousarray(v) for k, v in arrays.items()}
    nc = bacc.Bacc("TRN2", target_bir_lowering=False, num_devices=1)
    args = [nc.dram_tensor(k, v.shape, mybir.dt.from_np(v.dtype), kind="ExternalInput").ap() for k, v in arrays.items()]
    out = nc.dram_tensor("out", (N, D), mybir.dt.float32, kind="ExternalOutput").ap()
    adaln_kernel(nc, *args, out)
    r = run_bass_kernel_spmd(nc, [arrays], core_ids=[0])
    return r.results[0]["out"].reshape(NB, S, D)
```

```python
import concourse.bass as bass
from concourse import mybir
from contextlib import ExitStack

NB, S, D, H, HD = 32, 256, 128, 16, 8
P = 128
TB = S // P
NT = NB * TB
N = NB * S
E = 8
ST = 256
NJ = (2 * N + E * (ST - 1)) // ST
HI = NJ * ST // P
CAP = int(1.25 * N / E * 2)
FF0, FF1 = 512, 256
EPS, QK_EPS = 1e-5, 1.1920929e-07
SOFTCAP = 50.0
QK_SCALE = HD ** -0.5
SLOT = (32, 64)
MAGIC = 0x5F3759DF
MASKED = -1e30
EMPTY = 1 << 20


class Batch:

    def __init__(self, half, parity):
        self.half, self.parity = half, parity

    def index(self, factor=1, offset=0):
        return self.half * (2 * factor) + (self.parity * factor + offset)

    def plus(self, n):
        return Batch(self.half + (self.parity + n) // 2, (self.parity + n) % 2)

    def exists(self):
        return not isinstance(self.half, int) or 0 <= self.index() < NB


class Tile:

    def __init__(self, quarter, phase):
        self.quarter, self.phase = quarter, phase

    def index(self, factor=1, offset=0):
        return self.quarter * (4 * factor) + (self.phase * factor + offset)

    def ahead(self, n):
        return Tile(self.quarter + (self.phase + n) // 4, (self.phase + n) % 4)


def wait(eng, sem, value):
    if not isinstance(value, int) or value > 0:
        eng.wait_ge(sem, value)


def passed(eng, counter):
    eng.sem_inc(counter, 1)


class Chain:

    def __init__(self, eng, sem, steps, turn):
        self.eng, self.sem, self.steps, self.turn, self.n = eng, sem, steps, turn, 0

    def link(self, *instructions):
        for ins in instructions:
            ins.then_inc(self.sem, 1)
        self.n += len(instructions)
        assert self.n <= self.steps, self.n
        self.eng.wait_ge(self.sem, self.turn(self.steps, self.n))

    def end(self):
        assert self.n == self.steps, (self.n, self.steps)


def adaln_kernel(nc, x, c_t, wmod, wqkv, wo, router, gate_b, exp0, exp1, out):
    f32, bf16, f16, i32 = (mybir.dt.float32, mybir.dt.bfloat16, mybir.dt.float16, mybir.dt.int32)
    ALU, ACT, AX = mybir.AluOpType, mybir.ActivationFunctionType, mybir.AxisListType
    ds = bass.ds
    W_E = (exp0.shape[2], exp1.shape[2])

    with ExitStack() as ctx:
        def sb(name, shape, dt=f32):
            return ctx.enter_context(nc.sbuf_tensor(name, shape, dt))

        def sem(name):
            return ctx.enter_context(nc.semaphore(name))

        def dram(name, shape, dt=f32):
            return nc.dram_tensor(name, shape, dt, kind="Internal").ap()

        mod_dram = dram("mod_dram", [2 * NB, 6 * D])
        h_dram = [dram(f"h_dram{l}", [N, D]) for l in range(2)]
        y_dram = [dram("y_dram0", [NJ * ST, D]), dram("y_dram1", [2 * N, D])]

        X = sb("X", [P, NT * D])
        Xt = X[:, :]
        LG = [sb(f"LG{l}", [P, NT * E]) for l in range(2)]
        G = [sb(f"G{l}", [P, 2 * NT]) for l in range(2)]
        wqkv_sb = sb("wqkv_sb", [P, 2, 3 * D])
        wo_sb = sb("wo_sb", [P, 2, D])
        router_sb = sb("router_sb", [P, 2, E])
        gate_b_sb = sb("gate_b_sb", [P, E])
        identf = sb("identf", [P, P])
        identb = sb("identb", [P, P], bf16)
        identh = sb("identh", [P, P], f16)
        causal = sb("causal", [P, P], bf16)
        ps = ctx.enter_context(nc.psum_tensor("ps", [P, 8, 512], f32))

        modF = [sb(f"modF{i}", [P, 2 * D]) for i in range(2)]
        modB = [sb(f"modB{i}", [P, 3 * D]) for i in range(2)]
        modG = [sb(f"modG{i}", [P, D]) for i in range(2)]
        yin = [sb(f"yin{i}", [P, 2, 2, D]) for i in range(2)]
        ycomb = sb("ycomb", [P, 2, D])
        stF = sb("stF", [P, 2, 6])
        mvF = sb("mvF", [P, 2, 2])
        roots = sb("roots", [P, 4, 4 + 64])
        hF = [sb(f"hF{i}", [P, 2, D]) for i in range(2)]
        hT = sb("hT", [P, 2, D])
        qkv = [sb(f"qkv{i}", [P, 2, 3 * D]) for i in range(2)]
        qk2 = sb("qk2", [P, 512])
        qk3 = sb("qk3", [P, 512])
        pieces = sb("pieces", [P, 3, 512], bf16)
        ms = sb("ms", [P, 64])
        Qx = sb("Qx", [P, 2 * H * 64], bf16)
        Kx = sb("Kx", [P, 2 * H * 64], bf16)
        QT = [sb(f"QT{i}", [P, 8 * S], bf16) for i in range(2)]
        QTa = sb("QTa", [P, 8 * S], bf16)
        KT = [sb(f"KT{i}", [P, 2 * 8 * S], bf16) for i in range(2)]
        Vx = [sb(f"Vx{i}", [P, 2, H, 32]) for i in range(2)]
        tanh = [sb(f"tanh{i}", [P, 1024]) for i in range(2)]
        probs_all = sb("probs_all", [P, 2 * 3072])
        probs = [probs_all[:, i * 3072:(i + 1) * 3072] for i in range(2)]
        oT = [sb(f"oT{i}", [P, 1024]) for i in range(2)]
        rec = sb("rec", [P, 2, H])
        y = sb("y", [P, 2, D])
        yT = sb("yT", [P, 2, D])
        attn = sb("attn", [P, 2, D])
        stB = sb("stB", [P, 2, 6])
        mvB = sb("mvB", [P, 2, 2])
        hB = [sb(f"hB{i}", [P, 2, D]) for i in range(2)]
        h2T = sb("h2T", [P, 2, D])
        mxr = sb("mxr", [P, 4, 2 * H])

        iota_i = sb("iota_i", [P, 2 * NT + HI + NJ + 3 * E], i32)
        iota_f = sb("iota_f", [P, 2 * NT + HI + NJ + 3 * E])
        lane, block_no, tile_no, expert_no, row_no, pair_no = (
            iota_f[:, 0:P], iota_f[:, P:P + HI], iota_f[:, P + HI:P + HI + NJ],
            iota_f[:, P + HI + NJ:P + HI + NJ + E], iota_f[:, P + HI + NJ + E:P + HI + NJ + E + 1], iota_f[:, 0:P])
        lane_b, block_b = sb("lane_b", [P, P], bf16), sb("block_b", [P, HI], bf16)
        pair_base = sb("pair_base", [P, 2 * NT])
        before = sb("before", [P, P], bf16)
        onesb = sb("onesb", [P, P], bf16)
        chosen = sb("chosen", [P, 2, E, NT], bf16)
        rt = [tanh[0], tanh[1], oT[0], oT[1], QTa[:, :].bitcast(f32)]
        small = sb("small", [P, 8, 2 * E])
        top = sb("top", [P, 6, NT])
        slots = sb("slots", [P, 5, 2 * NT])
        eid = sb("eid", [P, NJ], i32)
        permA = [sb(f"permA{i}", [P, 8, P], bf16) for i in range(2)]
        permB = [sb(f"permB{i}", [P, 8, 2, HI], bf16) for i in range(2)]
        inv = sb("inv", [P, 4, HI])
        gat_i, sca_i = sb("gat_i", [P, HI], i32), sb("sca_i", [P, HI], i32)

        we = [probs_all[:, i * 1536:i * 1536 + max(W_E)] for i in range(4)]
        idx = [sb(f"idx{i}", [P, 4], i32) for i in range(4)]
        yidx = [sb(f"yidx{i}", [P, 4], i32) for i in range(2)]
        xg = [sb(f"xg{i}", [P, 2, D]) for i in range(4)]
        xT = [sb(f"xT{i}", [P, ST]) for i in range(2)]
        hid = tanh
        hz = [oT[i][:, 0:512] for i in range(2)]
        yo = [sb(f"yo{i}", [P, 2, D]) for i in range(4)]

        setup_dma, setup_pool, setup_pe, setup_dve, setup_act = (
            sem("setup_dma"), sem("setup_pool"), sem("setup_pe"), sem("setup_dve"), sem("setup_act"))

        final_dve = sem("final_dve")
        final_used, final_in, stored = sem("final_used"), [sem("final_in0"), sem("final_in1")], sem("stored")
        dve_passed, pool_passed = sem("dve_passed"), sem("pool_passed")

        L = [{}, {}]
        for l in range(2):
            names = {}
            own = (("qk_psum", "tanh_done", "hidden_ready"),
                   ("slots_act", "tq_psum", "tk_psum", "qa_ready", "k_ready", "max_psum", "max_done", "m_ready",
                    "up_act", "z_ready", "mid_psum", "s_ready"))[l]
            for name in own + ("norm_dve", "roots_dve", "front_dve", "front_pool", "xn_ready", "h_ready", "hT_psum", "hT_ready", "qkv_psum",
                               "qkv_ready", "slots_ready", "qk_ready", "v_ready", "score_psum", "exp_done", "masked",
                               "pv_psum", "o_ready", "ot_psum", "y_ready", "yT_psum", "yT_ready", "proj_psum",
                               "back_dve", "x1_ready", "back_pool", "xn2_ready", "h2_ready", "h2T_psum", "h2T_ready",
                               "router_psum", "logits_ready",
                               "route_dve", "gate_exp", "onehot_ready", "prefix_psum", "perm_ready",
                               "perm_used", "index_ready", "index_copied", "xT_psum", "xT_ready", "up_psum",
                               "down_psum", "y_out"):
                names[name] = sem(f"{name}{l}")
            for name, n in (("front_in", 2), ("modB_in", 2), ("h2_out", 2), ("weights_in", 4), ("gathered", 4), ("scattered", 4)):
                names[name] = [sem(f"{name}{l}{i}") for i in range(n)]
            L[l] = names
        L[1]["yidx_copied"], L[1]["scatter_index"] = sem("yidx_copied"), sem("scatter_index")
        L[1]["y_in"] = [sem(f"y_in{i}") for i in range(2)]

        NORM = (4, 10)
        ROOTS = (14, 13)
        FRONT = (9, 13)
        BACK = 7
        QK_STEPS = (5, 1)
        PIECES_DONE = 5
        PIECES = ((0, 0, 3), (1, 3 * HD, 2), (2, 5 * HD, 1))
        BIAS = 1280
        SCATTER = (16, 32)
        ROUTE = (64, 64)

        block = ctx.enter_context(nc.Block())

        def steps(eng, step):
            def run(b):
                def stage(n, work, *args):
                    if b.plus(n).exists():
                        work(b.plus(n), *args)
                step(b, stage)

            for k in range(-4, 3):
                run(Batch(k // 2, k % 2))
            with eng.Fori(1, NB // 2 - 3) as i:
                run(Batch(i, 1))
                run(Batch(i + 1, 0))
            for k in range(NB - 5, NB + 2):
                run(Batch(k // 2, k % 2))

        def tiles(eng, before_first, step):
            before_first()
            step(Tile(0, 0), True, True, True, True, False)
            for r in range(1, 5):
                step(Tile(r // 4, r % 4), True, True, True, True, True)
            with eng.Fori(1, (NJ - 4) // 4) as i:
                for r in range(1, 5):
                    step(Tile(i + r // 4, r % 4), True, True, True, True, True)
            for k in range(4 * ((NJ - 4) // 4) + 1, NJ + 1):
                step(Tile(k // 4, k % 4), k + 3 < NJ, k + 1 < NJ, k + 2 < NJ, k < NJ, True)

        def heads(l):
            return P // SLOT[l]

        def chunk_blocks(c):
            half, kind = c // 3, c % 3
            if kind < 2:
                return [(i * S, S, half * 8 + kind * 4 + i, 0, 0) for i in range(4)]
            return [(i * P, P, half * 8 + i, 1, P) for i in range(8)]

        @block.sync
        def _(sp):
            sp.dma_start(wqkv_sb[:, :, :], wqkv.rearrange("l p n -> p l n")).then_inc(setup_dma, 16)
            sp.dma_start(wo_sb[:, :, :], wo.rearrange("l p n -> p l n")).then_inc(setup_dma, 16)
            sp.dma_start(router_sb[:, :, :], router.rearrange("l p n -> p l n")).then_inc(setup_dma, 16)
            sp.dma_start(gate_b_sb[:, :], gate_b).then_inc(setup_dma, 16)
            sp.dma_start(probs[0][:, 0:1536].rearrange("p (l n) -> p l n", l=2),
                         wmod.rearrange("l p n -> p l n")).then_inc(setup_dma, 16)
            sp.dma_start(tanh[0][:, 0:2 * NB].rearrange("p (l n) -> p l n", l=2),
                         c_t.rearrange("l p n -> p l n")).then_inc(setup_dma, 16)
            sp.wait_ge(setup_dve, 12)
            for l in range(2):
                sp.dma_start(mod_dram[l * NB:(l + 1) * NB, :], probs[1][0:NB, l * 768:(l + 1) * 768]).then_inc(setup_dma, 16)
            sp.wait_ge(setup_dma, 128)

            def rows(l, b, first, n):
                return mod_dram[ds(b.index(1, l * NB), 1), first:first + n].to_broadcast([P, n])

            for l in range(2):
                q = L[l]

                def front_loads(b):
                    wait(sp, q["h_ready"], b.index(1, -1))
                    if l == 0:
                        sp.dma_start(Xt[:, ds(b.index(S), S)].rearrange("p (t c) -> p t c", t=2),
                                     x[ds(b.index(S), S), :].rearrange("(t p) c -> p t c", p=P)).then_inc(q["front_in"][b.parity], 16)
                    else:
                        sp.dma_start(modG[b.parity][:, :], rows(0, b, 5 * D, D)).then_inc(q["front_in"][b.parity], 16)
                    sp.dma_start(modF[b.parity][:, :], rows(l, b, 0, 2 * D)).then_inc(q["front_in"][b.parity], 16)

                def back_loads(b):
                    wait(sp, q["h2_ready"], b.index(1, -1))
                    sp.dma_start(modB[b.parity][:, :], rows(l, b, 2 * D, 3 * D)).then_inc(q["modB_in"][b.parity], 16)

                def back_stores(b):
                    sp.wait_ge(q["h2_ready"], b.index(1, 1))
                    sp.dma_start(h_dram[l][ds(b.index(S), S), :].rearrange("(t p) c -> p t c", p=P),
                                 hB[b.parity][:, :, :]).then_inc(q["h2_out"][b.parity], 16)

                def step(b, stage):
                    stage(4, front_loads)
                    stage(0, back_loads)
                    stage(-2, back_stores)

                steps(sp, step)
                for i in range(2):
                    sp.wait_ge(q["h2_out"][i], 16 * (NB // 2))
                exp = (exp0, exp1)[l]
                sp.wait_ge(q["index_ready"], 2)

                def weights(j):
                    wait(sp, q["y_out"], j.index(1, -3))
                    e = sp.value_load(eid[0:1, ds(j.index(), 1)], min_val=0, max_val=E - 1)
                    sp.dma_start(we[j.phase][:, 0:W_E[l]], exp[ds(e, 1), :, :].rearrange("e p n -> p (e n)")).then_inc(q["weights_in"][j.phase], 16)

                def store_y(j):
                    sp.wait_ge(q["y_out"], j.index(1, 1))
                    sp.dma_start(y_dram[0][ds(j.index(ST), ST), :].rearrange("(s p) c -> p s c", p=P),
                                 yo[j.phase][:, :, :]).then_inc(q["scattered"][j.phase], 16)

                def w_first():
                    for r in range(3):
                        weights(Tile(0, r))

                def w_step(j, ahead, up, transposed, mid, down):
                    if down and l == 0:
                        store_y(j.ahead(-1))
                    if ahead:
                        weights(j.ahead(3))

                tiles(sp, w_first, w_step)
                for r in range(4):
                    sp.wait_ge(q["scattered"][r], SCATTER[l] * len(range(r, NJ, 4)))

            q = L[1]

            def final_loads(b):
                wait(sp, final_used, b.index(1, -1))
                for k in range(2):
                    sp.dma_start(yin[b.parity][:, k, :, :],
                                 y_dram[1][ds(b.index(S, k * N), S), :].rearrange("(t p) c -> p t c", p=P)).then_inc(final_in[b.parity], 16)
                sp.dma_start(modG[b.parity][:, :], rows(1, b, 5 * D, D)).then_inc(final_in[b.parity], 16)

            def store(b):
                sp.wait_ge(final_used, b.index(1, 1))
                sp.dma_start(out[ds(b.index(S), S), :].rearrange("(t p) c -> p t c", p=P),
                             Xt[:, ds(b.index(S), S)].rearrange("p (t c) -> p t c", t=2)).then_inc(stored, 16)

            final_loads(Batch(0, 0))
            final_loads(Batch(0, 1))
            with sp.Fori(0, NB // 2 - 1) as i:
                for p in range(2):
                    final_loads(Batch(i + 1, p))
                    store(Batch(i, p))
            for p in range(2):
                store(Batch(NB // 2 - 1, p))
            sp.wait_ge(stored, 16 * NB)


        @block.gpsimd
        def _(pool):
            def one(ins):
                ins.then_inc(setup_pool, 1)

            one(nc.gpsimd.memset(identf[:, :], 0.0))
            one(nc.gpsimd.memset(identb[:, :], 0.0))
            one(nc.gpsimd.memset(identh[:, :], 0.0))
            one(nc.gpsimd.memset(causal[:, :], 0.0))
            pool.wait_ge(setup_pool, 4)
            for m in (identf, identb, identh):
                one(nc.gpsimd.affine_select(out=m[:, :], in_=m[:, :], compare_op=ALU.not_equal, fill=1.0,
                                            base=0, pattern=[[-1, P]], channel_multiplier=1))
            one(nc.gpsimd.affine_select(out=causal[:, :], in_=causal[:, :], compare_op=ALU.is_ge, fill=MASKED,
                                        base=0, pattern=[[-1, P]], channel_multiplier=1))
            for i in range(2):
                one(nc.gpsimd.memset(Vx[i][:, :, :, :], 0.0))
                one(nc.gpsimd.memset(KT[i][:, :].bitcast(f32), 0.0))
            one(nc.gpsimd.memset(Qx[:, :].bitcast(f32), 0.0))
            one(nc.gpsimd.memset(Kx[:, :].bitcast(f32), 0.0))
            pool.wait_ge(setup_pool, 14)
            for i in range(2):
                one(nc.gpsimd.memset(Vx[i][:, :, :, HD:HD + 1], 1.0))
            one(nc.gpsimd.iota(iota_i[:, 0:P], [[1, P]], base=0, channel_multiplier=0))
            one(nc.gpsimd.iota(iota_i[:, P:P + HI], [[1, HI]], base=0, channel_multiplier=0))
            one(nc.gpsimd.iota(iota_i[:, P + HI:P + HI + NJ], [[1, NJ]], base=0, channel_multiplier=0))
            one(nc.gpsimd.iota(iota_i[:, P + HI + NJ:P + HI + NJ + E], [[1, E]], base=-E, channel_multiplier=0))
            one(nc.gpsimd.iota(iota_i[:, P + HI + NJ + E:P + HI + NJ + 2 * E], [[0, E]], base=1, channel_multiplier=1))
            one(nc.gpsimd.memset(onesb[:, :], 1.0))
            one(nc.gpsimd.memset(before[:, :], 1.0))
            pool.wait_ge(setup_pool, 23)
            one(nc.gpsimd.affine_select(out=before[:, :], in_=before[:, :], compare_op=ALU.is_gt, fill=0.0,
                                        base=0, pattern=[[1, P]], channel_multiplier=-1))
            pool.wait_ge(setup_pool, 24)

            for l in range(2):
                q = L[l]

                def front(b):
                    pool.wait_ge(q["xn_ready"], b.index(2, 2))
                    pool.wait_ge(q["front_in"][b.parity], b.half * 32 + 32)
                    c = Chain(pool, q["front_pool"], 1, b.index)
                    for_all = hF[b.parity][:, :, :]
                    c.link(nc.gpsimd.tensor_tensor(for_all, for_all, modF[b.parity][:, D:2 * D].unsqueeze(1).to_broadcast([P, 2, D]), ALU.mult))
                    nc.gpsimd.tensor_tensor(for_all, for_all, modF[b.parity][:, 0:D].unsqueeze(1).to_broadcast([P, 2, D]),
                                            ALU.add).then_inc(q["h_ready"], 1)
                    c.end()

                def values(b):
                    pool.wait_ge(q["qkv_ready"], b.index(2, 2))
                    wait(pool, q["pv_psum"], b.index(2, -2))
                    passed(pool, pool_passed)
                    nc.gpsimd.tensor_copy(Vx[b.parity][:, :, :, 0:HD],
                                          qkv[b.parity][:, :, 2 * D:3 * D].rearrange("p t (h d) -> p t h d", h=H)).then_inc(q["v_ready"], 1)

                def mask(b, c):
                    pool.wait_ge(q["exp_done"], b.index(6, c + 1))
                    half, kind = c // 3, c % 3
                    v = probs[half][:, kind * 1024:(kind + 1) * 1024]
                    v = v.rearrange("p (h n) -> p h n", h=4 if kind < 2 else 8)[:, :, 0:P]
                    passed(pool, pool_passed)
                    nc.gpsimd.affine_select(out=v, in_=v, compare_op=ALU.is_ge, fill=0.0, base=0,
                                            pattern=[[0, v.shape[1]], [1, P]], channel_multiplier=-1).then_inc(q["masked"], 1)

                def back(b):
                    pool.wait_ge(q["xn2_ready"], b.index(2, 2))
                    c = Chain(pool, q["back_pool"], 1, b.index)
                    v = hB[b.parity][:, :, :]
                    c.link(nc.gpsimd.tensor_tensor(v, v, modB[b.parity][:, 2 * D:3 * D].unsqueeze(1).to_broadcast([P, 2, D]), ALU.mult))
                    nc.gpsimd.tensor_tensor(v, v, modB[b.parity][:, D:2 * D].unsqueeze(1).to_broadcast([P, 2, D]),
                                            ALU.add).then_inc(q["h2_ready"], 1)
                    c.end()

                def gather_y(b):
                    wait(pool, q["xn_ready"], b.index(2, -2))
                    passed(pool, pool_passed)
                    for k in range(2):
                        nc.gpsimd.tensor_copy(yidx[b.parity][:, 2 * k:2 * k + 2],
                                              slots[:, 1, ds(b.index(2, k * NT), 2)].bitcast(i32)).then_inc(q["yidx_copied"], 1)
                    pool.wait_ge(q["yidx_copied"], b.index(2, 2))
                    passed(pool, pool_passed)
                    for k in range(2):
                        for t in range(2):
                            nc.gpsimd.indirect_dma_start(
                                out=yin[b.parity][:, k, t, :], out_offset=None, in_=y_dram[0][:, :],
                                in_offset=bass.IndirectOffsetOnAxis(yidx[b.parity][:, 2 * k + t:2 * k + t + 1], 0)).then_inc(q["y_in"][b.parity], 16)

                def step(b, stage):
                    if l == 1:
                        stage(4, gather_y)
                    stage(0, mask, 0)
                    stage(0, mask, 1)
                    stage(1, values)
                    stage(3, front)
                    stage(0, mask, 2)
                    stage(-2, back)
                    stage(0, mask, 3)
                    stage(0, mask, 4)
                    stage(0, mask, 5)

                if l == 1:
                    for r in range(4):
                        pool.wait_ge(L[0]["scattered"][r], SCATTER[0] * len(range(r, NJ, 4)))
                steps(pool, step)
                pool.wait_ge(q["index_ready"], 2)
                for i in range(2):
                    pool.wait_ge(q["h2_out"][i], 16 * (NB // 2))

                def gather(j):
                    wait(pool, q["xT_psum"], j.index(1, -3))
                    passed(pool, pool_passed)
                    nc.gpsimd.tensor_copy(idx[j.phase][:, 0:2], gat_i[:, ds(j.index(2), 2)]).then_inc(q["index_copied"], 1)
                    pool.wait_ge(q["index_copied"], j.index(1, 1))
                    passed(pool, pool_passed)
                    for s_ in range(2):
                        nc.gpsimd.indirect_dma_start(
                            out=xg[j.phase][:, s_, :], out_offset=None, in_=h_dram[l][:, :],
                            in_offset=bass.IndirectOffsetOnAxis(idx[j.phase][:, s_:s_ + 1], 0)).then_inc(q["gathered"][j.phase], 16)

                def scatter(j):
                    wait(pool, q["scattered"][j.phase], j.quarter * SCATTER[l])
                    passed(pool, pool_passed)
                    nc.gpsimd.tensor_copy(idx[j.phase][:, 2:4], sca_i[:, ds(j.index(2), 2)]).then_inc(q["scatter_index"], 1)
                    pool.wait_ge(q["scatter_index"], j.index(1, 1))
                    pool.wait_ge(q["y_out"], j.index(1, 1))
                    passed(pool, pool_passed)
                    for s_ in range(2):
                        nc.gpsimd.indirect_dma_start(
                            out=y_dram[l][:, :], out_offset=bass.IndirectOffsetOnAxis(idx[j.phase][:, 2 + s_:3 + s_], 0),
                            in_=yo[j.phase][:, s_, :], in_offset=None,
                            bounds_check=2 * N - 1, oob_is_err=False).then_inc(q["scattered"][j.phase], 16)

                def g_first():
                    for r in range(3):
                        gather(Tile(0, r))

                def g_step(j, ahead, up, transposed, mid, down):
                    if ahead:
                        gather(j.ahead(3))
                    if down and l == 1:
                        scatter(j.ahead(-1))

                if l == 0:
                    pool.wait_ge(q["logits_ready"], NB)
                    for v in (KT[0], KT[1], Qx, Kx):
                        one(nc.gpsimd.memset(v[:, :].bitcast(f32), 0.0))
                    pool.wait_ge(setup_pool, 28)
                    for piece in range(3):
                        at = 6 * HD + piece
                        one(nc.gpsimd.memset(Kx[:, :].rearrange("p (h n) -> p h n", n=64)[:, :, at:at + 1], 1.0))

                tiles(pool, g_first, g_step)

        @block.scalar
        def _(act):
            act.wait_ge(setup_dma, 96)
            nc.scalar.activation(tanh[1][:, 0:2 * NB], tanh[0][:, 0:2 * NB], ACT.Silu).then_inc(setup_act, 1)

            for l in range(2):
                q = L[l]

                def copy_h(b):
                    act.wait_ge(q["hT_psum"], b.index(1, 1))
                    wait(act, q["qkv_psum"], b.index(2, 0))
                    nc.scalar.activation(hT[:, :, :], ps[:, 4, 0:S].rearrange("p (t c) -> p t c", t=2), ACT.Copy).then_inc(q["hT_ready"], 1)

                def copy_qkv(b):
                    wait(act, q["slots_ready"], b.index(1, -1))
                    wait(act, q["v_ready"], b.index(1, -1))
                    for t in range(2):
                        act.wait_ge(q["qkv_psum"], b.index(2, t + 1))
                        nc.scalar.activation(qkv[b.parity][:, t, :], ps[:, 4 + t, 0:3 * D], ACT.Copy).then_inc(q["qkv_ready"], 1)

                def fill_q(b):
                    act.wait_ge(q["front_dve"], b.index(FRONT[1], PIECES_DONE))
                    v = Qx[:, :].rearrange("p (th n) -> p th n", n=64)
                    wait(act, q["tq_psum"], b.index(2, 0))
                    for piece, at, n in PIECES:
                        src = pieces[:, piece, :].rearrange("p (t q) -> p t q", t=2)[:, :, 0:P]
                        for t in range(2):
                            nc.scalar.activation(
                                v[:, t * H:(t + 1) * H, at:at + n * HD].rearrange("p h (s d) -> p h s d", s=n),
                                src[:, t, :].rearrange("p (h d) -> p h d", h=H).unsqueeze(2).to_broadcast([P, H, n, HD]),
                                ACT.Copy).then_inc(q["slots_act"], 1)

                def softmax(b, c):
                    act.wait_ge(q["score_psum"], b.index(6, c + 1))
                    src = ps[:, 2 * (c % 2):2 * (c % 2) + 2, :].rearrange("p a b -> p (a b)")
                    half, kind = c // 3, c % 3
                    dst = probs[half][:, kind * 1024:(kind + 1) * 1024]
                    wait(act, q["pv_psum"], b.index(2, half - 1))
                    if l == 0:
                        wait(act, q["exp_done"], b.index(6, c - 1))
                        nc.scalar.activation(tanh[c % 2][:, :], src, ACT.Tanh, scale=QK_SCALE / SOFTCAP).then_inc(q["tanh_done"], 1)
                        act.wait_ge(q["tanh_done"], b.index(6, c + 1))
                        nc.scalar.activation(dst, tanh[c % 2][:, :], ACT.Exp, scale=SOFTCAP).then_inc(q["exp_done"], 1)
                    else:
                        nc.scalar.activation(dst, src, ACT.Exp, scale=QK_SCALE).then_inc(q["exp_done"], 1)

                def copy_o(b, half):
                    act.wait_ge(q["pv_psum"], b.index(2, half + 1))
                    wait(act, q["ot_psum"], b.index(2, -2))
                    nc.scalar.activation(oT[b.parity][:, half * 512:(half + 1) * 512], ps[:, 6, :], ACT.Copy).then_inc(q["o_ready"], 1)

                def copy_y(b):
                    act.wait_ge(q["yT_psum"], b.index(1, 1))
                    wait(act, q["proj_psum"], b.index(1, 0))
                    nc.scalar.activation(yT[:, :, :], ps[:, 7, 0:S].rearrange("p (t c) -> p t c", t=2), ACT.Copy).then_inc(q["yT_ready"], 1)

                def copy_h2(b):
                    act.wait_ge(q["h2T_psum"], b.index(1, 1))
                    wait(act, q["router_psum"], b.index(1, 0))
                    nc.scalar.activation(h2T[:, :, :], ps[:, 7, 0:S].rearrange("p (t c) -> p t c", t=2), ACT.Copy).then_inc(q["h2T_ready"], 1)

                def step(b, stage):
                    stage(0, softmax, 0)
                    stage(2, copy_h)
                    stage(-1, copy_o, 1)
                    if l == 0:
                        stage(0, softmax, 1)
                    stage(2, copy_qkv)
                    if l == 1:
                        stage(1, fill_q)
                        stage(0, softmax, 1)
                    stage(0, softmax, 2)
                    stage(-1, copy_y)
                    stage(0, softmax, 3)
                    stage(0, copy_o, 0)
                    stage(-2, copy_h2)
                    stage(0, softmax, 4)
                    stage(0, softmax, 5)

                steps(act, step)
                act.wait_ge(q["onehot_ready"], 3)
                nc.scalar.activation(top[:, 5, :], top[:, 4, :], ACT.Exp).then_inc(q["gate_exp"], 1)

                def pair(j):
                    return ps[:, 2 + 2 * (j.phase % 2):4 + 2 * (j.phase % 2), :].rearrange("p a b -> p (a b)")

                def a_step(j, ahead, up, transposed, mid, down):
                    if l == 0:
                        if up:
                            hidden(j.ahead(1))
                    else:
                        if up:
                            biased(j.ahead(1))
                        if mid:
                            gated(j)

                def hidden(j):
                    act.wait_ge(q["up_psum"], j.index(1, 1))
                    wait(act, q["down_psum"], j.index(1, -1))
                    nc.scalar.activation(hid[j.phase % 2][:, :], pair(j), ACT.Gelu).then_inc(q["hidden_ready"], 1)

                def biased(j):
                    act.wait_ge(q["up_psum"], j.index(1, 1))
                    wait(act, q["z_ready"], j.index(2, -2))
                    w = we[j.phase]
                    for f in range(2):
                        nc.scalar.activation(hid[j.phase % 2][:, f * ST:(f + 1) * ST], pair(j)[:, f * ST:(f + 1) * ST], ACT.Identity,
                                             bias=w[:, BIAS + f:BIAS + f + 1]).then_inc(q["up_act"], 1)

                def gated(j):
                    act.wait_ge(q["mid_psum"], j.index(1, 1))
                    wait(act, q["down_psum"], j.index(1, -1))
                    w = we[j.phase]
                    for f in range(2):
                        nc.scalar.activation(hid[j.phase % 2][:, 512 + f * ST:512 + (f + 1) * ST], ps[:, 6, f * ST:(f + 1) * ST], ACT.Silu,
                                             bias=w[:, BIAS + 4 + f:BIAS + 5 + f]).then_inc(q["s_ready"], 1)

                tiles(act, (lambda: hidden(Tile(0, 0))) if l == 0 else (lambda: biased(Tile(0, 0))), a_step)

        @block.tensor
        def _(pe):
            pe.wait_ge(setup_pool, 16)
            pe.wait_ge(setup_act, 1)
            for l in range(2):
                sc = tanh[1][:, l * NB:(l + 1) * NB]
                wm = probs[0][:, l * 768:(l + 1) * 768]
                nc.tensor.matmul(ps[0:NB, 2 * l, :], sc, wm[:, 0:512], start=True, stop=True)
                nc.tensor.matmul(ps[0:NB, 2 * l + 1, 0:256], sc, wm[:, 512:768], start=True, stop=True).then_inc(setup_pe, 1)
            pe.wait_ge(setup_dve, 12)
            for l in range(2):
                q = L[l]
                nh = heads(l)
                ng = H // nh
                dt = f16 if l == 0 else bf16
                ident = identh if l == 0 else identb

                def transposed_h(b):
                    pe.wait_ge(q["h_ready"], b.index(1, 1))
                    wait(pe, q["qkv_ready"], b.index(2, 0))
                    wait(pe, q["qk_ready"], b.index(QK_STEPS[l], -QK_STEPS[l]))
                    for t in range(2):
                        last = nc.tensor.transpose(ps[:, 4, t * P:(t + 1) * P], hF[b.parity][:, t, :], identf[:, :])
                    last.then_inc(q["hT_psum"], 1)

                def qkv_products(b):
                    pe.wait_ge(q["hT_ready"], b.index(1, 1))
                    for t in range(2):
                        nc.tensor.matmul(ps[:, 4 + t, 0:3 * D], hT[:, t, :], wqkv_sb[:, l, :], start=True, stop=True).then_inc(q["qkv_psum"], 1)

                def projections_copied(b):
                    if b.plus(1).exists():
                        pe.wait_ge(q["qkv_ready"], b.index(2, 4))

                def transposed_qk(b):
                    pe.wait_ge(q["slots_ready"], b.index(1, 1))
                    projections_copied(b)
                    for i, src in enumerate((Qx, Kx)):
                        v = src[:, 0:2 * H * SLOT[l]].bitcast(dt)
                        dst = ps[:, 4 + i, :].bitcast(dt)
                        for g in range(ng):
                            for t in range(2):
                                at = (t * H + g * nh) * SLOT[l]
                                last = nc.tensor.transpose(dst[:, g * S + t * P:g * S + (t + 1) * P], v[:, at:at + P], ident[:, :])
                        last.then_inc(q["qk_psum"], 1)

                def slots_transposed(b, src, first, done):
                    v = src[:, 0:2 * H * SLOT[1]]
                    dst = ps[:, 4:6, :].rearrange("p a b -> p (a b)").bitcast(bf16)
                    for g in range(ng):
                        for t in range(2):
                            at = (t * H + g * nh) * SLOT[1]
                            last = nc.tensor.transpose(dst[:, g * S + t * P:g * S + (t + 1) * P], v[:, at:at + P], ident[:, :])
                    last.then_inc(done, 1)

                def transposed_q(b):
                    pe.wait_ge(q["slots_act"], b.index(6, 6))
                    projections_copied(b)
                    slots_transposed(b, Qx, 0, q["tq_psum"])

                def transposed_k(b):
                    pe.wait_ge(q["slots_ready"], b.index(1, 1))
                    pe.wait_ge(q["qa_ready"], b.index(1, 1))
                    slots_transposed(b, Kx, 0, q["tk_psum"])

                def max_scores(b, m):
                    bank = 4 + m % 2
                    if m < 2:
                        pe.wait_ge(q["k_ready"], b.index(2, 2))
                    else:
                        pe.wait_ge(q["max_done"], b.index(12, m - 1))
                    kv = KT[b.parity][:, :]
                    if m < 8:
                        blocks = [(i * S, S, 2 * m + i, 1) for i in range(2)]
                    else:
                        blocks = [(i * P, P, 4 * (m - 8) + i, 0) for i in range(4)]
                    for col, n, h, qt in blocks:
                        g, i = h // nh, h % nh
                        nc.tensor.matmul(ps[:, bank, col:col + n], QTa[:, g * S + qt * P:g * S + qt * P + P],
                                         kv[:, (i * ng + g) * S:(i * ng + g) * S + n], start=True, stop=False)
                        last = nc.tensor.matmul(ps[:, bank, col + n - P:col + n], identb[:, :], causal[:, :], start=False, stop=True)
                    last.then_inc(q["max_psum"], 1)

                def transposed_qm(b):
                    pe.wait_ge(q["m_ready"], b.index(1, 1))
                    slots_transposed(b, Qx, 0, q["tq_psum"])

                def scores(b, c):
                    wait(pe, q["tanh_done"] if l == 0 else q["exp_done"], b.index(6, c - 1))
                    if c == 0:
                        pe.wait_ge(q["qk_ready"], b.index(QK_STEPS[l], QK_STEPS[l]))
                    flat = ps[:, 2 * (c % 2):2 * (c % 2) + 2, :].rearrange("p a b -> p (a b)")
                    qv, kv = QT[b.parity][:, 0:ng * S].bitcast(dt), KT[b.parity][:, 0:nh * ng * S].bitcast(dt)
                    for col, n, h, kt, q0 in chunk_blocks(c):
                        g, i = h // nh, h % nh
                        last = nc.tensor.matmul(flat[:, col:col + n],
                                                kv[:, (i * ng + g) * S + kt * P:(i * ng + g) * S + kt * P + P],
                                                qv[:, g * S + q0:g * S + q0 + n], start=True, stop=True)
                    last.then_inc(q["score_psum"], 1)

                def values(b, half):
                    pe.wait_ge(q["masked"], b.index(6, 3 * (half + 1)))
                    if half == 0:
                        pe.wait_ge(q["v_ready"], b.index(1, 1))
                    wait(pe, q["o_ready"], b.index(2, half))
                    pr = probs[half]
                    for g in range(2):
                        for kt in range(2):
                            for i in range(4):
                                h = half * 8 + g * 4 + i
                                o = ps[32 * i:32 * i + 32, 6, g * S:(g + 1) * S]
                                v = Vx[b.parity][:, kt, h, :]
                                if kt == 0:
                                    nc.tensor.matmul(o, v, pr[:, g * 1024 + i * S:g * 1024 + (i + 1) * S], start=True, stop=False)
                                else:
                                    last = nc.tensor.matmul(o[:, P:S], v, pr[:, 2048 + (g * 4 + i) * P:2048 + (g * 4 + i + 1) * P],
                                                            start=False, stop=True)
                    last.then_inc(q["pv_psum"], 1)

                def transposed_o(b, t):
                    pe.wait_ge(q["o_ready"], b.index(2, 2))
                    if t == 0:
                        wait(pe, q["x1_ready"], b.index(1, 0))
                        wait(pe, q["logits_ready"], b.index(1, -1))
                    else:
                        pe.wait_ge(q["y_ready"], b.index(2, 1))
                    for g in range(4):
                        last = nc.tensor.transpose(ps[:, 7, g * P:(g + 1) * P], oT[b.parity][:, g * S + t * P:g * S + (t + 1) * P], identf[:, :])
                    last.then_inc(q["ot_psum"], 1)

                def transposed_y(b):
                    pe.wait_ge(q["y_ready"], b.index(2, 2))
                    for t in range(2):
                        last = nc.tensor.transpose(ps[:, 7, t * P:(t + 1) * P], y[:, t, :], identf[:, :])
                    last.then_inc(q["yT_psum"], 1)

                def projection(b):
                    pe.wait_ge(q["yT_ready"], b.index(1, 1))
                    for t in range(2):
                        last = nc.tensor.matmul(ps[:, 7, S + t * P:S + (t + 1) * P], yT[:, t, :], wo_sb[:, l, :], start=True, stop=True)
                    last.then_inc(q["proj_psum"], 1)

                def transposed_h2(b):
                    pe.wait_ge(q["h2_ready"], b.index(1, 1))
                    if not isinstance(b.half, int) or b.index() < NB - 1:
                        pe.wait_ge(q["x1_ready"], b.index(1, 2))
                    for t in range(2):
                        last = nc.tensor.transpose(ps[:, 7, t * P:(t + 1) * P], hB[b.parity][:, t, :], identf[:, :])
                    last.then_inc(q["h2T_psum"], 1)

                def router_logits(b):
                    pe.wait_ge(q["h2T_ready"], b.index(1, 1))
                    for t in range(2):
                        last = nc.tensor.matmul(ps[:, 7, S + t * E:S + (t + 1) * E], h2T[:, t, :], router_sb[:, l, :], start=True, stop=True)
                    last.then_inc(q["router_psum"], 1)

                def maxima(b, first, end):
                    for m in range(first, end):
                        max_scores(b, m)

                def step(b, stage):
                    stage(0, scores, 0)
                    stage(2, transposed_h)
                    stage(-1, values, 1)
                    stage(-1, transposed_o, 0)
                    stage(0, scores, 1)
                    stage(2, qkv_products)
                    if l == 0:
                        stage(-1, transposed_o, 1)
                        stage(0, scores, 2)
                        stage(-1, transposed_y)
                        stage(1, transposed_qk)
                        stage(-1, projection)
                        stage(0, scores, 3)
                        stage(0, values, 0)
                        stage(-2, transposed_h2)
                        stage(0, scores, 4)
                        stage(-2, router_logits)
                        stage(0, scores, 5)
                    else:
                        stage(1, transposed_q)
                        stage(0, scores, 2)
                        stage(-1, transposed_o, 1)
                        stage(1, transposed_k)
                        stage(-1, transposed_y)
                        stage(1, maxima, 0, 3)
                        stage(-1, projection)
                        stage(0, scores, 3)
                        stage(1, maxima, 3, 6)
                        stage(0, values, 0)
                        stage(-2, transposed_h2)
                        stage(1, maxima, 6, 9)
                        stage(-2, router_logits)
                        stage(0, scores, 4)
                        stage(1, maxima, 9, 12)
                        stage(0, scores, 5)
                        stage(1, transposed_qm)

                steps(pe, step)
                pe.wait_ge(q["onehot_ready"], 2)
                for k in range(2):
                    rhs = chosen[:, k, :, :].rearrange("p e t -> p (e t)")
                    nc.tensor.matmul(ps[:, k, :], before[:, :], rhs, start=True, stop=True)
                    nc.tensor.matmul(ps[:, 2 + k, :], onesb[:, :], rhs, start=True, stop=True).then_inc(q["prefix_psum"], 1)

                def invert(g, start, stop):
                    pe.wait_ge(q["perm_ready"], g.index(1, 1))
                    a_, b_ = permA[g.parity], permB[g.parity]
                    for r in range(8):
                        last = nc.tensor.matmul(ps[:, 4, 0:2 * HI], a_[:, r, :], b_[:, r, :, :].rearrange("p a b -> p (a b)"),
                                                start=start and r == 0, stop=stop and r == 7)
                    last.then_inc(q["perm_used"], 1)

                groups = 2 * NT // 8
                invert(Batch(0, 0), True, False)
                invert(Batch(0, 1), False, False)
                with pe.Fori(1, groups // 2 - 1) as i:
                    invert(Batch(i, 0), False, False)
                    invert(Batch(i, 1), False, False)
                invert(Batch(groups // 2 - 1, 0), False, False)
                invert(Batch(groups // 2 - 1, 1), False, True)

                def pair(j):
                    return ps[:, 2 + 2 * (j.phase % 2):4 + 2 * (j.phase % 2), :].rearrange("p a b -> p (a b)")

                def transposed_x(j):
                    pe.wait_ge(q["gathered"][j.phase], j.quarter * 32 + 32)
                    wait(pe, q["xT_ready"], j.index(1, -1))
                    for s_ in range(2):
                        last = nc.tensor.transpose(ps[:, j.phase % 2, s_ * P:(s_ + 1) * P], xg[j.phase][:, s_, :], identf[:, :])
                    last.then_inc(q["xT_psum"], 1)

                def up_products(j):
                    pe.wait_ge(q["xT_ready"], j.index(1, 1))
                    pe.wait_ge(q["weights_in"][j.phase], j.quarter * 16 + 16)
                    if l == 0:
                        wait(pe, q["hidden_ready"], j.index(1, -1))
                    else:
                        wait(pe, q["z_ready"], j.index(2, -2))
                    o = pair(j)
                    for f in range(4):
                        last = nc.tensor.matmul(o[:, f * ST:(f + 1) * ST], we[j.phase][:, f * P:(f + 1) * P], xT[j.phase % 2][:, :],
                                                start=True, stop=True)
                    last.then_inc(q["up_psum"], 1)

                def mid_products(j):
                    pe.wait_ge(q["z_ready"], j.index(2, 2))
                    wait(pe, q["s_ready"], j.index(2, 0))
                    for g in range(2):
                        for f in range(2):
                            at = 512 + f * FF1 + g * P
                            last = nc.tensor.matmul(ps[:, 6, g * ST:(g + 1) * ST], we[j.phase][:, at:at + P],
                                                    hz[j.phase % 2][:, f * ST:(f + 1) * ST], start=f == 0, stop=f == 1)
                    last.then_inc(q["mid_psum"], 1)

                def down_products(j):
                    if l == 0:
                        pe.wait_ge(q["hidden_ready"], j.index(1, 1))
                    else:
                        pe.wait_ge(q["s_ready"], j.index(2, 2))
                    wait(pe, q["y_out"], j.index(1, 0))
                    bank = 6 + j.phase % 2 if l == 0 else 7
                    nf, w0, h0 = (4, 512, 0) if l == 0 else (2, 1024, 512)
                    for s_ in range(2):
                        for f in range(nf):
                            last = nc.tensor.matmul(ps[:, bank, s_ * P:(s_ + 1) * P],
                                                    hid[j.phase % 2][:, h0 + f * ST + s_ * P:h0 + f * ST + (s_ + 1) * P],
                                                    we[j.phase][:, w0 + f * P:w0 + (f + 1) * P], start=f == 0, stop=f == nf - 1)
                    last.then_inc(q["down_psum"], 1)

                def p_first():
                    transposed_x(Tile(0, 0))
                    up_products(Tile(0, 0))
                    transposed_x(Tile(0, 1))

                def p_step(j, ahead, up, transposed, mid, down):
                    if up:
                        up_products(j.ahead(1))
                    if transposed:
                        transposed_x(j.ahead(2))
                    if mid and l == 1:
                        mid_products(j)
                    if down:
                        down_products(j.ahead(-1))

                tiles(pe, p_first, p_step)

        @block.vector
        def _(dve):
            V = nc.vector
            m = probs[1][0:NB, 0:1536].rearrange("p (l s c) -> p l s c", l=2, s=6)
            tmp = probs[1][0:NB, 2048:2048 + 512].rearrange("p (l s c) -> p l s c", l=2, s=2)
            n = 0

            def link(ins):
                nonlocal n
                ins.then_inc(setup_dve, 1)
                n += 1
                dve.wait_ge(setup_dve, n)

            dve.wait_ge(setup_pe, 2)
            for l in range(2):
                link(V.tensor_copy(probs[1][0:NB, l * 768:(l + 1) * 768],
                                   ps[0:NB, 2 * l:2 * l + 2, :].rearrange("p a b -> p (a b)")[:, 0:768]))
            for l in range(2):
                sc = m[:, l, 1:5:3, :]
                link(V.tensor_scalar(sc, sc, 1.0, None, ALU.add))
                g = m[:, l, 2:6:3, :]
                sign = tmp[:, l, :, :]
                link(V.tensor_scalar(sign, g, 0.0, 2.0, ALU.is_ge, ALU.mult))
                link(V.tensor_scalar(sign, sign, 1.0, None, ALU.subtract))
                link(V.scalar_tensor_tensor(g, g, -1.0, g, ALU.mult, ALU.max))
                link(V.scalar_tensor_tensor(g, g, 0.25, sign, ALU.max, ALU.mult))

            def rsqrt(c, *sources):
                n = 4 + 64 * (len(sources) > 2)
                r, v, i0, a = [roots[:, i, 0:n] for i in range(4)]
                c.link(*[V.tensor_scalar(roots[:, 1, at:at + w], src, k, eps, ALU.mult, ALU.add) for src, k, eps, at, w in sources])
                c.link(V.tensor_scalar(i0.bitcast(i32), v.bitcast(i32), 1, None, ALU.arith_shift_right))
                c.link(V.tensor_scalar(r.bitcast(i32), i0.bitcast(i32), -1.0, float(MAGIC), ALU.mult, ALU.add))
                for _ in range(3):
                    c.link(V.tensor_tensor(a, r, r, ALU.mult))
                    c.link(V.scalar_tensor_tensor(a, a, -0.5, v, ALU.mult, ALU.mult))
                    c.link(V.scalar_tensor_tensor(r, a, 1.5, r, ALU.add, ALU.mult))

            def combine(c, b, gates, last=None):
                y0, y1 = yin[b.parity][:, 0], yin[b.parity][:, 1]
                gate = [[gates[:, ds(b.index(2, k * NT + t), 1)] for t in range(2)] for k in range(2)]
                c.link(*[V.tensor_scalar(ycomb[:, t, :], y0[:, t, :], gate[0][t], None, ALU.mult) for t in range(2)])
                c.link(*[V.scalar_tensor_tensor(ycomb[:, t, :], y1[:, t, :], gate[1][t], ycomb[:, t, :], ALU.mult, ALU.add) for t in range(2)])
                c.link(V.tensor_tensor(ycomb[:, :, :], ycomb[:, :, :], modG[b.parity][:, :].unsqueeze(1).to_broadcast([P, 2, D]), ALU.mult))
                xb = Xt[:, ds(b.index(S), S)]
                ins = V.tensor_tensor(xb, xb, ycomb[:, :, :].rearrange("p t c -> p (t c)"), ALU.add)
                if last is None:
                    c.link(ins)
                else:
                    ins.then_inc(last, 1)

            dve.wait_ge(setup_pool, 24)
            link(V.tensor_copy(iota_f[:, 0:P + HI + NJ + 2 * E], iota_i[:, 0:P + HI + NJ + 2 * E]))
            link(V.tensor_copy(lane_b[:, :], lane))
            link(V.tensor_copy(block_b[:, :], block_no))
            for v in (ms[:, :], mvF[:, :, :], mvB[:, :, :]):
                link(V.memset(v, 1.0))
            link(V.tensor_scalar(pair_base[:, :], lane, float(P), None, ALU.mult))

            for l in range(2):
                q = L[l]
                nh = heads(l)
                ng = H // nh
                dt = f16 if l == 0 else bf16

                def statistics(c, b, st, mv):
                    passed(dve, dve_passed)
                    c.link(*[V.bn_stats(st[:, t, :], Xt[:, ds(b.index(S, t * D), D)]) for t in range(2)])
                    passed(dve, dve_passed)
                    c.link(*[V.bn_aggr(mv[:, t, :], st[:, t, :]) for t in range(2)])

                def normalize(b, mv, at, dst, done):
                    for t in range(2):
                        V.tensor_scalar(dst[:, t, :], Xt[:, ds(b.index(S, t * D), D)], mv[:, t, 0:1], roots[:, 0, at + t:at + t + 1],
                                        ALU.subtract, ALU.mult).then_inc(done, 1)
                    dve.wait_ge(done, b.index(2, 2))

                def step_roots(b):
                    c = Chain(dve, q["roots_dve"], ROOTS[l], lambda steps_, n_: b.index(steps_, 4 * steps_ + n_))
                    sources = [(mvF[:, :, 1], 1.0, EPS, 0, 2), (mvB[:, :, 1], 1.0, EPS, 2, 2)]
                    if l == 0:
                        sources.append((ms[:, :], 1.0 / HD, QK_EPS, 4, 64))
                    rsqrt(c, *sources)
                    c.end()

                chain = {}

                def front_statistics(b):
                    c = Chain(dve, q["norm_dve"], NORM[l], b.index)
                    if l == 0:
                        dve.wait_ge(q["front_in"][b.parity], b.half * 32 + 32)
                    else:
                        dve.wait_ge(q["y_in"][b.parity], b.half * 64 + 64)
                        dve.wait_ge(q["front_in"][b.parity], b.half * 32 + 32)
                        combine(c, b, G[0])
                    statistics(c, b, stF, mvF)
                    c.end()

                def front_norm(b):
                    wait(dve, q["hT_psum"], b.index(1, -1))
                    normalize(b, mvF, 0, hF[b.parity], q["xn_ready"])

                def back_norm(b):
                    wait(dve, q["h2_out"][b.parity], b.half * 16)
                    wait(dve, q["h2T_psum"], b.index(1, -1))
                    normalize(b, mvB, 2, hB[b.parity], q["xn2_ready"])

                def mean_squares(b):
                    c = chain["f"] = Chain(dve, q["front_dve"], FRONT[l], b.index)
                    dve.wait_ge(q["qkv_ready"], b.index(2, 2))
                    c.link(V.tensor_tensor(qk2[:, :].rearrange("p (t n) -> p t n", t=2), qkv[b.parity][:, :, 0:2 * D],
                                           qkv[b.parity][:, :, 0:2 * D], ALU.mult))
                    c.link(V.reduce_sum(ms[:, :], qk2[:, :].rearrange("p (h d) -> p h d", d=HD), AX.X))

                def front_slots(b):
                    c = chain["f"] = chain["f"] if l == 0 else Chain(dve, q["front_dve"], FRONT[l], b.index)
                    dve.wait_ge(q["qkv_ready"], b.index(2, 2))
                    qk = qkv[b.parity][:, :, 0:2 * D]
                    v2 = lambda t: t[:, :].rearrange("p (t n) -> p t n", t=2)
                    if l == 0:
                        c.link(V.tensor_tensor(qk2[:, :].rearrange("p (t h d) -> p t h d", t=2, d=HD),
                                               qk.rearrange("p t (h d) -> p t h d", d=HD),
                                               roots[:, 0, 4:68].rearrange("p (t h) -> p t h", t=2).unsqueeze(3).to_broadcast([P, 2, 2 * H, HD]), ALU.mult))
                        wait(dve, q["qk_psum"], b.index(2, 0))
                        s = qk2[:, :].rearrange("p (t s h d) -> p t s h d", t=2, s=2, h=H)
                        xs = [t_[:, 0:2 * H * SLOT[0]].bitcast(f16).rearrange("p (t h n) -> p t h n", t=2, h=H) for t_ in (Qx, Kx)]
                        c.link(*[V.tensor_copy(xs[i][:, :, :, 0:HD], s[:, :, i]) for i in range(2)])
                        low = (2 * HD, HD)
                        high = (HD, 2 * HD)
                        for i in range(2):
                            V.tensor_tensor(xs[i][:, :, :, low[i]:low[i] + HD], s[:, :, i], xs[i][:, :, :, 0:HD], ALU.subtract).then_inc(q["front_dve"], 1)
                        for i in range(2):
                            V.tensor_copy(xs[i][:, :, :, high[i]:high[i] + HD], xs[i][:, :, :, 0:HD]).then_inc(q["front_dve"], 1)
                        c.n += 4
                        dve.wait_ge(q["front_dve"], b.index(FRONT[l], c.n))
                        dve.sem_inc(q["slots_ready"], 1)
                        c.end()
                    else:
                        pc = [v2(pieces[:, i, :]) for i in range(3)]
                        wait(dve, q["slots_act"], b.index(6, 0))
                        c.link(V.tensor_copy(pc[0], qk))
                        c.link(V.tensor_tensor(v2(qk2), qk, pc[0], ALU.subtract))
                        c.link(V.tensor_copy(pc[1], v2(qk2)))
                        c.link(V.tensor_tensor(v2(qk3), v2(qk2), pc[1], ALU.subtract))
                        c.link(V.tensor_copy(pc[2], v2(qk3)))
                        assert c.n == PIECES_DONE
                        wait(dve, q["tk_psum"], b.index(1, 0))
                        for at, piece in enumerate((0, 1, 2, 0, 1, 0)):
                            last = V.tensor_copy(Kx[:, :].rearrange("p (t h n) -> p t h n", t=2, h=H)[:, :, :, at * HD:(at + 1) * HD],
                                                 pieces[:, piece, :].rearrange("p (t s h d) -> p t s h d", t=2, s=2, h=H)[:, :, 1])
                        last.then_inc(q["slots_ready"], 1)

                def front_copies(b):
                    words = ng * S // 2
                    dve.wait_ge(q["qk_psum"], b.index(2, 1))
                    wait(dve, q["score_psum"], b.index(6, -6))
                    V.tensor_copy(QT[b.parity][:, 0:ng * S].bitcast(i32), ps[:, 4, 0:words].bitcast(i32)).then_inc(q["qk_ready"], 1)
                    dve.wait_ge(q["qk_psum"], b.index(2, 2))
                    n = SLOT[l]
                    for i in range(nh):
                        V.tensor_copy(KT[b.parity][i * n:(i + 1) * n, i * ng * S:(i + 1) * ng * S].bitcast(i32),
                                      ps[i * n:(i + 1) * n, 5, 0:words].bitcast(i32)).then_inc(q["qk_ready"], 1)

                def front_copies1(b):
                    both = ps[:, 4:6, :].rearrange("p a b -> p (a b)").bitcast(i32)
                    dve.wait_ge(q["tq_psum"], b.index(2, 1))
                    wait(dve, q["max_psum"], b.index(12, 0))
                    V.tensor_copy(QTa[:, :].bitcast(i32), both).then_inc(q["qa_ready"], 1)
                    dve.wait_ge(q["tk_psum"], b.index(1, 1))
                    wait(dve, q["score_psum"], b.index(6, -6))
                    n = SLOT[1]
                    for i in range(2):
                        V.tensor_copy(KT[b.parity][i * n:(i + 1) * n, i * ng * S:(i + 1) * ng * S].bitcast(i32),
                                      both[i * n:(i + 1) * n, :]).then_inc(q["k_ready"], 1)

                def maxima(b, first, end):
                    for m in range(first, end):
                        dve.wait_ge(q["max_psum"], b.index(12, m + 1))
                        bank = ps[:, 4 + m % 2, :]
                        if m < 8:
                            ins = V.reduce_max(mxr[:, 0, H + 2 * m:H + 2 * m + 2], bank.rearrange("p (h n) -> p h n", h=2), AX.X)
                        else:
                            ins = V.reduce_max(mxr[:, 0, 4 * (m - 8):4 * (m - 8) + 4], bank.rearrange("p (h n) -> p h n", h=4), AX.X)
                        ins.then_inc(q["max_done"], 1)

                def fill_maxima(b):
                    c = chain["f"]
                    dve.wait_ge(q["max_done"], b.index(12, 12))
                    piece = [Qx[:, :].rearrange("p (h n) -> p h n", n=64)[:, :, 6 * HD + i] for i in range(3)]
                    c.link(V.tensor_scalar(mxr[:, 1, :], mxr[:, 0, :], -1.0, None, ALU.mult))
                    for i in range(2):
                        c.link(V.tensor_copy(piece[i], mxr[:, 1 + i, :]))
                        c.link(V.tensor_tensor(mxr[:, 2 + i, :], mxr[:, 1 + i, :], piece[i], ALU.subtract))
                    V.tensor_copy(piece[2], mxr[:, 3, :]).then_inc(q["m_ready"], 1)

                def copy_qm(b):
                    c = chain["f"]
                    both = ps[:, 4:6, :].rearrange("p a b -> p (a b)").bitcast(i32)
                    piece = [Qx[:, :].rearrange("p (h n) -> p h n", n=64)[:, :, 6 * HD + i] for i in range(3)]
                    dve.wait_ge(q["tq_psum"], b.index(2, 2))
                    V.tensor_copy(QT[b.parity][:, :].bitcast(i32), both).then_inc(q["qk_ready"], 1)
                    for i in range(3):
                        V.memset(piece[i], 0.0).then_inc(q["front_dve"], 1)
                    c.n += 3
                    dve.wait_ge(q["front_dve"], b.index(FRONT[1], c.n))
                    c.end()

                def back_values(b, t):
                    if t == 0:
                        chain["b"] = Chain(dve, q["back_dve"], BACK, b.index)
                        wait(dve, q["yT_psum"], b.index(1, 0))
                    c = chain["b"]
                    dve.wait_ge(q["ot_psum"], b.index(2, t + 1))
                    o = ps[:, 7, :].rearrange("p (h n) -> p h n", n=32)
                    c.link(V.reciprocal(rec[:, t, :], o[:, :, HD]))
                    V.tensor_tensor(y[:, t, :].rearrange("p (h d) -> p h d", d=HD), o[:, :, 0:HD],
                                    rec[:, t, :].unsqueeze(2).to_broadcast([P, H, HD]), ALU.mult).then_inc(q["y_ready"], 1)

                def back_residual(b):
                    c = chain["b"]
                    dve.wait_ge(q["proj_psum"], b.index(1, 1))
                    dve.wait_ge(q["modB_in"][b.parity], b.half * 16 + 16)
                    c.link(V.tensor_tensor(attn[:, :, :], ps[:, 7, S:2 * S].rearrange("p (t c) -> p t c", t=2),
                                           modB[b.parity][:, 0:D].unsqueeze(1).to_broadcast([P, 2, D]), ALU.mult))
                    xb = Xt[:, ds(b.index(S), S)]
                    V.tensor_tensor(xb, xb, attn[:, :, :].rearrange("p t c -> p (t c)"), ALU.add).then_inc(q["x1_ready"], 1)
                    dve.wait_ge(q["x1_ready"], b.index(1, 1))
                    statistics(c, b, stB, mvB)
                    c.end()

                def back_logits(b):
                    dve.wait_ge(q["router_psum"], b.index(1, 1))
                    V.tensor_copy(LG[l][:, ds(b.index(2 * E), 2 * E)], ps[:, 7, S:S + 2 * E]).then_inc(q["logits_ready"], 1)

                def step(b, stage):
                    if l == 0:
                        stage(1, mean_squares)
                    else:
                        stage(1, front_slots)
                    stage(3, front_statistics)
                    step_roots(b)
                    stage(-1, back_values, 0)
                    stage(-2, back_norm)
                    stage(3, front_norm)
                    if l == 0:
                        stage(-1, back_values, 1)
                        stage(1, front_slots)
                        stage(-1, back_residual)
                        stage(1, front_copies)
                        stage(-2, back_logits)
                    else:
                        stage(1, front_copies1)
                        stage(-1, back_values, 1)
                        stage(1, maxima, 0, 6)
                        stage(-1, back_residual)
                        stage(1, maxima, 6, 12)
                        stage(1, fill_maxima)
                        stage(-2, back_logits)
                        stage(1, copy_qm)

                steps(dve, step)
                dve.wait_ge(q["logits_ready"], NB)

                c = Chain(dve, q["route_dve"], ROUTE[l], lambda steps_, n_: n_)
                te = lambda v: v.rearrange("p (t e) -> p t e", e=E)
                w = [te(rt[i][:, 0:NT * E]) for i in range(5)]
                lg = te(LG[l][:, :])
                tb = lambda v: v.unsqueeze(2).to_broadcast([P, NT, E])
                eb = lambda v: v.unsqueeze(1).to_broadcast([P, NT, E])
                if l == 1:
                    c.link(V.tensor_tensor(lg, lg, eb(gate_b_sb[:, :]), ALU.add))
                for k in range(2):
                    c.link(V.reduce_max(top[:, k, :], lg, AX.X))
                    c.link(V.tensor_tensor(w[0], lg, tb(top[:, k, :]), ALU.is_equal))
                    c.link(V.tensor_tensor(w[0], w[0], eb(expert_no), ALU.mult))
                    c.link(V.tensor_reduce(top[:, 2 + k, :], w[0], AX.X, ALU.min))
                    c.link(V.tensor_tensor(w[1 + k], eb(expert_no), tb(top[:, 2 + k, :]), ALU.is_equal))
                    V.tensor_copy(chosen[:, k, :, :].rearrange("p e t -> p t e"), w[1 + k]).then_inc(q["onehot_ready"], 1)
                    if k == 0:
                        c.link(V.scalar_tensor_tensor(lg, w[1], -3.0e38, lg, ALU.mult, ALU.add))
                V.tensor_tensor(top[:, 4, :], top[:, 1, :], top[:, 0, :], ALU.subtract).then_inc(q["onehot_ready"], 1)
                dve.wait_ge(q["gate_exp"], 1)
                g0, g1 = G[l][:, 0:NT], G[l][:, NT:2 * NT]
                c.link(V.tensor_scalar(g1, top[:, 5, :], 1.0, None, ALU.add))
                c.link(V.reciprocal(g0, g1))
                c.link(V.tensor_tensor(g1, top[:, 5, :], g0, ALU.mult))

                c.link(V.memset(rt[3][:, :], 1.0))
                c.link(V.memset(rt[3][:, :].rearrange("p (g t) -> p g t", t=NT)[:, :, 0:1], 0.0))
                dve.wait_ge(q["prefix_psum"], 2)
                c.link(V.tensor_copy(rt[2][:, :], ps[:, 2:4, :].rearrange("p a b -> p (a b)")))
                c.link(V.tensor_tensor_scan(rt[1][:, :], rt[3][:, :], rt[2][:, :], 0.0, ALU.mult, ALU.add))
                c.link(V.tensor_tensor(rt[0][:, :], rt[1][:, :], rt[2][:, :], ALU.subtract))
                c.link(V.tensor_tensor(rt[0][:, :], rt[0][:, :], ps[:, 0:2, :].rearrange("p a b -> p (a b)"), ALU.add))
                count = small[:, 0, :]
                ket = lambda v: v.rearrange("p (k e t) -> p k e t", k=2, e=E)
                oh = chosen[:, :, :, :].rearrange("p k e t -> p (k e t)")
                kt = lambda v: v.rearrange("p (k t) -> p k t", k=2)
                if l == 0:
                    c.link(V.tensor_tensor(rt[4][:, :], rt[0][:, :], oh, ALU.mult))
                    c.link(V.reduce_sum(kt(slots[:, 0, :]), ket(rt[4][:, :]).rearrange("p k e t -> p k t e"), AX.X))
                    c.link(V.tensor_scalar(slots[:, 0, :], slots[:, 0, :], float(CAP), None, ALU.is_lt))
                    c.link(V.tensor_tensor(G[0][:, :], G[0][:, :], slots[:, 0, :], ALU.mult))
                c.link(V.tensor_copy(count, rt[1][:, :].rearrange("p (g t) -> p g t", t=NT)[:, :, NT - 1]))
                n_e, n_i, tiles_f, ends, base = (small[:, 1, 0:E], small[:, 2, 0:E].bitcast(i32), small[:, 3, 0:E],
                                                 small[:, 4, 0:E], small[:, 5, :])
                c.link(V.tensor_tensor(n_e, count[:, 0:E], count[:, E:2 * E], ALU.add))
                c.link(V.tensor_scalar(n_e, n_e, float(ST - 1), None, ALU.add))
                c.link(V.tensor_copy(n_i, n_e))
                c.link(V.tensor_scalar(n_i, n_i, ST.bit_length() - 1, None, ALU.arith_shift_right))
                c.link(V.tensor_copy(tiles_f, n_i))
                c.link(V.memset(small[:, 6, 0:E], 1.0))
                c.link(V.tensor_tensor_scan(ends, small[:, 6, 0:E], tiles_f, 0.0, ALU.mult, ALU.add))
                c.link(V.tensor_tensor(base[:, 0:E], ends, tiles_f, ALU.subtract))
                c.link(V.tensor_scalar(base[:, 0:E], base[:, 0:E], float(ST), None, ALU.mult))
                c.link(V.tensor_tensor(base[:, E:2 * E], base[:, 0:E], count[:, 0:E], ALU.add))
                c.link(V.tensor_tensor(rt[0][:, :].rearrange("p (g t) -> p g t", t=NT), rt[0][:, :].rearrange("p (g t) -> p g t", t=NT),
                                       base.unsqueeze(2).to_broadcast([P, 2 * E, NT]), ALU.add))
                c.link(V.tensor_tensor(rt[4][:, :], rt[0][:, :], oh, ALU.mult))
                c.link(V.reduce_sum(kt(slots[:, 0, :]), ket(rt[4][:, :]).rearrange("p k e t -> p k t e"), AX.X))
                slot_i, part_i = slots[:, 1, :].bitcast(i32), slots[:, 2, :].bitcast(i32)
                c.link(V.tensor_copy(slot_i, slots[:, 0, :]))
                c.link(V.tensor_scalar(part_i, slot_i, P - 1, None, ALU.bitwise_and))
                c.link(V.tensor_copy(slots[:, 3, :], part_i))
                c.link(V.tensor_scalar(part_i, slot_i, P.bit_length() - 1, None, ALU.arith_shift_right))
                c.link(V.tensor_copy(slots[:, 4, :], part_i))
                v = rt[4][:, 0:NJ * E].rearrange("p (j e) -> p j e", e=E)
                c.link(V.tensor_tensor(v, ends.unsqueeze(1).to_broadcast([P, NJ, E]), tile_no.unsqueeze(2).to_broadcast([P, NJ, E]), ALU.is_le))
                c.link(V.reduce_sum(inv[:, 0, 0:NJ], v, AX.X))
                c.link(V.tensor_scalar(inv[:, 0, 0:NJ], inv[:, 0, 0:NJ], float(E - 1), None, ALU.min))
                V.tensor_copy(eid[:, :], inv[:, 0, 0:NJ]).then_inc(q["index_ready"], 1)

                def factors(g):
                    wait(dve, q["perm_used"], g.index(1, -1))
                    for r in range(8):
                        at = g.index(8, r)
                        low_, high_ = slots[:, 3, ds(at, 1)], slots[:, 4, ds(at, 1)]
                        V.tensor_scalar(permA[g.parity][:, r, :], lane_b[:, :], low_, None, ALU.is_equal)
                        V.tensor_scalar(permB[g.parity][:, r, 0, :], block_b[:, :], high_, row_no, ALU.is_equal, ALU.mult)
                        last = V.tensor_scalar(permB[g.parity][:, r, 1, :], block_b[:, :], high_, pair_base[:, ds(at, 1)], ALU.is_equal, ALU.mult)
                    last.then_inc(q["perm_ready"], 1)

                factors(Batch(0, 0))
                factors(Batch(0, 1))
                with dve.Fori(1, NT // 8) as i:
                    factors(Batch(i, 0))
                    factors(Batch(i, 1))
                dve.wait_ge(q["perm_used"], NT // 4)
                c.link(V.tensor_copy(inv[:, 0:2, :], ps[:, 4, 0:2 * HI].rearrange("p (a b) -> p a b", a=2)))
                c.link(V.tensor_tensor(inv[:, 0, :], inv[:, 0, :], inv[:, 1, :], ALU.add))
                c.link(V.tensor_scalar(inv[:, 1, :], inv[:, 0, :], 0.0, float(EMPTY), ALU.is_equal, ALU.mult))
                c.link(V.tensor_scalar(inv[:, 2, :], inv[:, 0, :], 1.0, 0.0, ALU.subtract, ALU.max))
                c.link(V.scalar_tensor_tensor(inv[:, 1, :], inv[:, 2, :], 0.0, inv[:, 1, :], ALU.add, ALU.add))
                c.link(V.tensor_copy(sca_i[:, :], inv[:, 1, :]))
                c.link(V.tensor_copy(gat_i[:, :], inv[:, 2, :]))
                V.tensor_scalar(gat_i[:, :], gat_i[:, :], N - 1, None, ALU.bitwise_and).then_inc(q["index_ready"], 1)
                assert c.n <= ROUTE[l], c.n

                def copy_x(j):
                    dve.wait_ge(q["xT_psum"], j.index(1, 1))
                    wait(dve, q["up_psum"], j.index(1, -1))
                    V.tensor_copy(xT[j.phase % 2][:, :], ps[:, j.phase % 2, 0:ST]).then_inc(q["xT_ready"], 1)

                def product(j):
                    dve.wait_ge(q["up_act"], j.index(2, 2))
                    wait(dve, q["mid_psum"], j.index(1, -1))
                    up = ps[:, 2 + 2 * (j.phase % 2):4 + 2 * (j.phase % 2), :].rearrange("p a b -> p (a b)")
                    for f in range(2):
                        V.scalar_tensor_tensor(hz[j.phase % 2][:, f * ST:(f + 1) * ST], up[:, 512 + f * ST:512 + (f + 1) * ST],
                                               we[j.phase][:, BIAS + 2 + f:BIAS + 3 + f], hid[j.phase % 2][:, f * ST:(f + 1) * ST],
                                               ALU.add, ALU.mult).then_inc(q["z_ready"], 1)

                def copy_y(j):
                    dve.wait_ge(q["down_psum"], j.index(1, 1))
                    wait(dve, q["scattered"][j.phase], j.quarter * SCATTER[l])
                    if l == 0:
                        ins = V.tensor_copy(yo[j.phase][:, :, :], ps[:, 6 + j.phase % 2, 0:2 * P].rearrange("p (s c) -> p s c", s=2))
                    else:
                        ins = V.tensor_tensor(yo[j.phase][:, :, :], ps[:, 7, 0:2 * P].rearrange("p (s c) -> p s c", s=2),
                                              we[j.phase][:, BIAS + 6:BIAS + 6 + D].unsqueeze(1).to_broadcast([P, 2, D]), ALU.add)
                    ins.then_inc(q["y_out"], 1)

                def v_first():
                    copy_x(Tile(0, 0))
                    if l == 1:
                        product(Tile(0, 0))
                    copy_x(Tile(0, 1))

                def v_step(j, ahead, up, transposed, mid, down):
                    if transposed:
                        copy_x(j.ahead(2))
                    if up and l == 1:
                        product(j.ahead(1))
                    if down:
                        copy_y(j.ahead(-1))

                tiles(dve, v_first, v_step)

            def final(b):
                c = Chain(dve, final_dve, 5, b.index)
                dve.wait_ge(final_in[b.parity], b.half * 48 + 48)
                wait(dve, final_used, b.index(1, 0))
                combine(c, b, G[1], final_used)
                c.end()

            for p in range(2):
                final(Batch(0, p))
            with dve.Fori(1, NB // 2) as i:
                for p in range(2):
                    final(Batch(i, p))


def kernel(**inputs):
    import numpy as np
    import concourse.bacc as bacc
    from concourse.bass_utils import run_bass_kernel_spmd

    a = {k: np.asarray(v) for k, v in inputs.items()}

    def chunks(w):
        e, r, m = w.shape
        return w.reshape(e, r // P, P, m).transpose(0, 2, 1, 3).reshape(e, P, -1)

    def columns(v):
        return v.reshape(E, -1, P).transpose(0, 2, 1)

    arrays = {
        "x": a["L0_attn_x"].reshape(N, D),
        "c_t": np.stack([a["L0_c"].T, a["L1_c"].T]),
        "wmod": np.stack([a["L0_wmod"], a["L1_wmod"]]),
        "wqkv": np.stack([np.concatenate([a["L0_attn_w_q"].T, a["L0_attn_w_k"].T, a["L0_attn_w_v"].T], axis=1),
                          a["L1_attn_w_attn"]]),
        "wo": np.stack([a["L0_attn_w_o"].T, a["L1_attn_w_proj"]]),
        "router": np.stack([a["L0_ffn_router_w"].T, a["L1_ffn_gate_w"]]),
        "gate_b": np.repeat(a["L1_ffn_gate_b"][None], P, axis=0),
        "exp0": np.concatenate([chunks(a["L0_ffn_w1"]), chunks(a["L0_ffn_w2"])], axis=2),
        "exp1": np.concatenate([chunks(a["L1_ffn_w1"]), chunks(a["L1_ffn_w2"]), chunks(a["L1_ffn_wg"]), chunks(a["L1_ffn_w3"]),
                                columns(a["L1_ffn_b1"]), columns(a["L1_ffn_b2"]), columns(a["L1_ffn_bg"]),
                                np.repeat(a["L1_ffn_b3"][:, None], P, axis=1)], axis=2),
    }
    arrays = {k: np.ascontiguousarray(v) for k, v in arrays.items()}
    nc = bacc.Bacc("TRN2", target_bir_lowering=False, num_devices=1)
    args = [nc.dram_tensor(k, v.shape, mybir.dt.from_np(v.dtype), kind="ExternalInput").ap() for k, v in arrays.items()]
    out = nc.dram_tensor("out", (N, D), mybir.dt.float32, kind="ExternalOutput").ap()
    adaln_kernel(nc, *args, out)
    r = run_bass_kernel_spmd(nc, [arrays], core_ids=[0])
    return r.results[0]["out"].reshape(NB, S, D)
```

```python
import concourse.bass as bass
from concourse import mybir
from contextlib import ExitStack

NB, S, D, H, HD = 32, 256, 128, 16, 8
P = 128
TB = S // P
NT = NB * TB
N = NB * S
E = 8
ST = 256
NJ = (2 * N + E * (ST - 1)) // ST
HI = NJ * ST // P
CAP = int(1.25 * N / E * 2)
FF0, FF1 = 512, 256
EPS, QK_EPS = 1e-5, 1.1920929e-07
SOFTCAP = 50.0
QK_SCALE = HD ** -0.5
SLOT = (32, 64)
MAGIC = 0x5F3759DF
MASKED = -1e30
EMPTY = 1 << 20


class Batch:

    def __init__(self, half, parity):
        self.half, self.parity = half, parity

    def index(self, factor=1, offset=0):
        return self.half * (2 * factor) + (self.parity * factor + offset)

    def plus(self, n):
        return Batch(self.half + (self.parity + n) // 2, (self.parity + n) % 2)

    def exists(self):
        return not isinstance(self.half, int) or 0 <= self.index() < NB


class Tile:

    def __init__(self, quarter, phase):
        self.quarter, self.phase = quarter, phase

    def index(self, factor=1, offset=0):
        return self.quarter * (4 * factor) + (self.phase * factor + offset)

    def ahead(self, n):
        return Tile(self.quarter + (self.phase + n) // 4, (self.phase + n) % 4)


def wait(eng, sem, value):
    if not isinstance(value, int) or value > 0:
        eng.wait_ge(sem, value)


def passed(eng, counter):
    eng.sem_inc(counter, 1)


class Chain:

    def __init__(self, eng, sem, steps, turn):
        self.eng, self.sem, self.steps, self.turn, self.n = eng, sem, steps, turn, 0

    def link(self, *instructions, of=0):
        for ins in instructions:
            ins.then_inc(self.sem, 1)
        if of > len(instructions):
            self.eng.sem_inc(self.sem, of - len(instructions))
        self.n += max(len(instructions), of)
        assert self.n <= self.steps, self.n
        self.eng.wait_ge(self.sem, self.turn(self.steps, self.n))

    def end(self):
        assert self.n == self.steps, (self.n, self.steps)


def adaln_kernel(nc, x, c_t, wmod, wqkv, wo, router, gate_b, exp0, exp1, out):
    f32, bf16, f16, i32 = (mybir.dt.float32, mybir.dt.bfloat16, mybir.dt.float16, mybir.dt.int32)
    ALU, ACT, AX = mybir.AluOpType, mybir.ActivationFunctionType, mybir.AxisListType
    ds = bass.ds
    W_E = (exp0.shape[2], exp1.shape[2])

    with ExitStack() as ctx:
        def sb(name, shape, dt=f32):
            return ctx.enter_context(nc.sbuf_tensor(name, shape, dt))

        def sem(name):
            return ctx.enter_context(nc.semaphore(name))

        def dram(name, shape, dt=f32):
            return nc.dram_tensor(name, shape, dt, kind="Internal").ap()

        mod_dram = dram("mod_dram", [2 * NB, 6 * D])
        h_dram = [dram(f"h_dram{l}", [N, D]) for l in range(2)]
        y_dram = [dram("y_dram0", [NJ * ST, D]), dram("y_dram1", [2 * N, D])]

        X = sb("X", [P, NT * D])
        Xt = X[:, :]
        LG = [sb(f"LG{l}", [P, NT * E]) for l in range(2)]
        G = [sb(f"G{l}", [P, 2 * NT]) for l in range(2)]
        wqkv_sb = sb("wqkv_sb", [P, 2, 3 * D])
        wo_sb = sb("wo_sb", [P, 2, D])
        router_sb = sb("router_sb", [P, 2, E])
        gate_b_sb = sb("gate_b_sb", [P, E])
        identf = sb("identf", [P, P])
        identb = sb("identb", [P, P], bf16)
        identh = sb("identh", [P, P], f16)
        causal = sb("causal", [P, P], bf16)
        ps = ctx.enter_context(nc.psum_tensor("ps", [P, 8, 512], f32))

        modF = [sb(f"modF{i}", [P, 2 * D]) for i in range(2)]
        modB = [sb(f"modB{i}", [P, 3 * D]) for i in range(2)]
        modG = [sb(f"modG{i}", [P, D]) for i in range(2)]
        yin = [sb(f"yin{i}", [P, 2, 2, D]) for i in range(2)]
        ycomb = sb("ycomb", [P, 2, D])
        stF = sb("stF", [P, 2, 6])
        mvF = sb("mvF", [P, 2, 2])
        roots = sb("roots", [P, 4, 4 + 64])
        hF = [sb(f"hF{i}", [P, 2, D]) for i in range(2)]
        hT = sb("hT", [P, 2, D])
        qkv = [sb(f"qkv{i}", [P, 2, 3 * D]) for i in range(2)]
        qk2 = sb("qk2", [P, 512])
        pieces = sb("pieces", [P, 3, 512], bf16)
        ms = sb("ms", [P, 64])
        Qx = sb("Qx", [P, 2 * H * 64], bf16)
        Kx = sb("Kx", [P, 2 * H * 64], bf16)
        QT = [sb(f"QT{i}", [P, 8 * S], bf16) for i in range(2)]
        QTa = sb("QTa", [P, 8 * S], bf16)
        KT = [sb(f"KT{i}", [P, 2 * 8 * S], bf16) for i in range(2)]
        Vx = [sb(f"Vx{i}", [P, 2, H, 32]) for i in range(2)]
        tanh = [sb(f"tanh{i}", [P, 1024]) for i in range(2)]
        probs_all = sb("probs_all", [P, 2 * 3072])
        probs = [probs_all[:, i * 3072:(i + 1) * 3072] for i in range(2)]
        oT = [sb(f"oT{i}", [P, 1024]) for i in range(2)]
        rec = sb("rec", [P, 2, H])
        y = sb("y", [P, 2, D])
        yT = sb("yT", [P, 2, D])
        attn = sb("attn", [P, 2, D])
        stB = sb("stB", [P, 2, 6])
        mvB = sb("mvB", [P, 2, 2])
        hB = [sb(f"hB{i}", [P, 2, D]) for i in range(2)]
        h2T = sb("h2T", [P, 2, D])
        mxr = sb("mxr", [P, 3, 2 * H])

        iota_i = sb("iota_i", [P, 2 * NT + HI + NJ + 3 * E], i32)
        iota_f = sb("iota_f", [P, 2 * NT + HI + NJ + 3 * E])
        lane, block_no, tile_no, expert_no, row_no, pair_no = (
            iota_f[:, 0:P], iota_f[:, P:P + HI], iota_f[:, P + HI:P + HI + NJ],
            iota_f[:, P + HI + NJ:P + HI + NJ + E], iota_f[:, P + HI + NJ + E:P + HI + NJ + E + 1], iota_f[:, 0:P])
        lane_b, block_b = sb("lane_b", [P, P], bf16), sb("block_b", [P, HI], bf16)
        pair_base = sb("pair_base", [P, 2 * NT])
        before = sb("before", [P, P], bf16)
        onesb = sb("onesb", [P, P], bf16)
        chosen = sb("chosen", [P, 2, E, NT], bf16)
        rt = [tanh[0], tanh[1], oT[0], oT[1], QTa[:, :].bitcast(f32)]
        small = sb("small", [P, 8, 2 * E])
        top = sb("top", [P, 6, NT])
        slots = sb("slots", [P, 5, 2 * NT])
        eid = sb("eid", [P, NJ], i32)
        permA = [sb(f"permA{i}", [P, 8, P], bf16) for i in range(2)]
        permB = [sb(f"permB{i}", [P, 8, 2, HI], bf16) for i in range(2)]
        inv = sb("inv", [P, 4, HI])
        gat_i, sca_i = sb("gat_i", [P, HI], i32), sb("sca_i", [P, HI], i32)

        we = [probs_all[:, i * 1536:i * 1536 + max(W_E)] for i in range(4)]
        idx = [sb(f"idx{i}", [P, 4], i32) for i in range(4)]
        yidx = [sb(f"yidx{i}", [P, 4], i32) for i in range(2)]
        xg = [sb(f"xg{i}", [P, 2, D]) for i in range(4)]
        xT = [sb(f"xT{i}", [P, ST]) for i in range(2)]
        hid = tanh
        hz = [oT[i][:, 0:512] for i in range(2)]
        yo = [sb(f"yo{i}", [P, 2, D]) for i in range(4)]

        yfin = [yin[0][:, :, :, :], yin[1][:, :, :, :]] + [QT[i][:, 0:8 * D].bitcast(f32).rearrange("p (k t c) -> p k t c", k=2, t=2)
                                                           for i in range(2)]
        gfin = [modG[0][:, :], modG[1][:, :], modF[0][:, 0:D], modF[1][:, 0:D]]

        setup_dma, setup_pool, setup_pe, setup_dve, setup_act = (
            sem("setup_dma"), sem("setup_pool"), sem("setup_pe"), sem("setup_dve"), sem("setup_act"))

        final_dve = sem("final_dve")
        final_scaled = sem("final_scaled")
        final_used, final_in, stored = sem("final_used"), [sem(f"final_in{i}") for i in range(4)], sem("stored")
        route_dve, gate_exp = sem("route_dve"), sem("gate_exp")
        dve_passed, pool_passed = sem("dve_passed"), sem("pool_passed")

        L = [{}, {}]
        for l in range(2):
            names = {}
            own = (("qk_psum", "tanh_done", "hidden_ready"),
                   ("pieces_dve", "slots_act", "tq_psum", "tk_psum", "qa_ready", "k_ready", "max_psum", "max_done", "m_ready",
                    "up_act", "z_ready", "mid_psum", "s_ready"))[l]
            for name in own + ("roots_dve", "front_dve", "front_pool", "xn_ready", "h_ready", "hT_psum", "hT_ready", "qkv_psum",
                               "qkv_ready", "slots_ready", "qk_ready", "v_ready", "score_psum", "exp_done", "masked",
                               "pv_psum", "o_ready", "ot_psum", "y_ready", "yT_psum", "yT_ready", "proj_psum",
                               "back_dve", "attn_ready", "x1_ready", "back_pool", "xn2_ready", "h2_ready", "h2T_psum", "h2T_ready",
                               "router_psum", "logits_ready",
                               "onehot_ready", "prefix_psum", "perm_ready", "perm_scaled",
                               "perm_used", "index_ready", "index_copied", "xT_psum", "xT_ready", "up_psum",
                               "down_psum", "y_out"):
                names[name] = sem(f"{name}{l}")
            for name, n in (("front_in", 2), ("modB_in", 2), ("h2_out", 2), ("scattered", 4)):
                names[name] = [sem(f"{name}{l}{i}") for i in range(n)]
            L[l] = names
        L[1]["yidx_copied"], L[1]["scatter_index"] = sem("yidx_copied"), sem("scatter_index")
        for name in ("weights_in", "gathered"):
            L[0][name] = L[1][name] = [sem(f"{name}{i}") for i in range(4)]
        L[1]["combined"] = sem("combined")
        L[1]["y_in"] = [sem(f"y_in{i}") for i in range(2)]

        ROOTS = (22, 21)
        FRONT = (9, 7)
        PIECES = 4
        BACK = 2
        QK_STEPS = (5, 2)
        Q_SLOTS = ((0, 0, 3), (1, 3 * HD, 2), (2, 5 * HD, 1))
        BIAS = 1280
        SCATTER = (16, 32)
        ROUTE = 64

        block = ctx.enter_context(nc.Block())

        def steps(eng, step):
            def run(b):
                def stage(n, work, *args):
                    if b.plus(n).exists():
                        work(b.plus(n), *args)
                step(b, stage)

            for k in range(-4, 5):
                run(Batch(k // 2, k % 2))
            with eng.Fori(2, NB // 2 - 3) as i:
                run(Batch(i, 1))
                run(Batch(i + 1, 0))
            for k in range(NB - 5, NB + 3):
                run(Batch(k // 2, k % 2))

        def tiles(eng, before_first, step):
            before_first()
            step(Tile(0, 0), True, True, True, True, False)
            for r in range(1, 5):
                step(Tile(r // 4, r % 4), True, True, True, True, True)
            with eng.Fori(1, (NJ - 4) // 4) as i:
                for r in range(1, 5):
                    step(Tile(i + r // 4, r % 4), True, True, True, True, True)
            for k in range(4 * ((NJ - 4) // 4) + 1, NJ + 1):
                step(Tile(k // 4, k % 4), k + 3 < NJ, k + 1 < NJ, k + 2 < NJ, k < NJ, True)

        def fours(eng, step):
            for p in range(4):
                step(Tile(0, p))
            with eng.Fori(1, NB // 4) as i:
                for p in range(4):
                    step(Tile(i, p))

        def loads(l, j):
            return j.quarter + (1 + l * len(range(j.phase, NJ, 4)))

        def heads(l):
            return P // SLOT[l]

        def chunk_blocks(c):
            half, kind = c // 3, c % 3
            if kind < 2:
                return [(i * S, S, half * 8 + kind * 4 + i, 0, 0) for i in range(4)]
            return [(i * P, P, half * 8 + i, 1, P) for i in range(8)]

        @block.sync
        def _(sp):
            sp.dma_start(wqkv_sb[:, :, :], wqkv.rearrange("l p n -> p l n")).then_inc(setup_dma, 16)
            sp.dma_start(wo_sb[:, :, :], wo.rearrange("l p n -> p l n")).then_inc(setup_dma, 16)
            sp.dma_start(router_sb[:, :, :], router.rearrange("l p n -> p l n")).then_inc(setup_dma, 16)
            sp.dma_start(gate_b_sb[:, :], gate_b).then_inc(setup_dma, 16)
            sp.dma_start(probs[0][:, 0:1536].rearrange("p (l n) -> p l n", l=2),
                         wmod.rearrange("l p n -> p l n")).then_inc(setup_dma, 16)
            sp.dma_start(tanh[0][:, 0:2 * NB].rearrange("p (l n) -> p l n", l=2),
                         c_t.rearrange("l p n -> p l n")).then_inc(setup_dma, 16)
            sp.wait_ge(setup_dve, 12)
            for l in range(2):
                sp.dma_start(mod_dram[l * NB:(l + 1) * NB, :], probs[1][0:NB, l * 768:(l + 1) * 768]).then_inc(setup_dma, 16)
            sp.wait_ge(setup_dma, 128)

            def rows(l, b, first, n):
                return mod_dram[ds(b.index(1, l * NB), 1), first:first + n].to_broadcast([P, n])

            for l in range(2):
                q = L[l]

                def front_loads(b):
                    wait(sp, q["h_ready"], b.index(1, -1))
                    if l == 0:
                        sp.dma_start(Xt[:, ds(b.index(S), S)].rearrange("p (t c) -> p t c", t=2),
                                     x[ds(b.index(S), S), :].rearrange("(t p) c -> p t c", p=P)).then_inc(q["front_in"][b.parity], 16)
                    else:
                        sp.dma_start(modG[b.parity][:, :], rows(0, b, 5 * D, D)).then_inc(q["front_in"][b.parity], 16)
                    sp.dma_start(modF[b.parity][:, :], rows(l, b, 0, 2 * D)).then_inc(q["front_in"][b.parity], 16)

                def back_loads(b):
                    wait(sp, q["h2_ready"], b.index(1, -1))
                    sp.dma_start(modB[b.parity][:, :], rows(l, b, 2 * D, 3 * D)).then_inc(q["modB_in"][b.parity], 16)

                def back_stores(b):
                    sp.wait_ge(q["h2_ready"], b.index(1, 1))
                    sp.dma_start(h_dram[l][ds(b.index(S), S), :].rearrange("(t p) c -> p t c", p=P),
                                 hB[b.parity][:, :, :]).then_inc(q["h2_out"][b.parity], 16)

                def step(b, stage):
                    stage(4, front_loads)
                    stage(0, back_loads)
                    stage(-2, back_stores)

                steps(sp, step)
                for i in range(2):
                    sp.wait_ge(q["h2_out"][i], 16 * (NB // 2))
                exp = (exp0, exp1)[l]
                sp.wait_ge(q["index_ready"], 2)

                def weights(j):
                    e = sp.value_load(eid[0:1, ds(j.index(), 1)], min_val=0, max_val=E - 1)
                    wait(sp, q["down_psum" if l == 0 else "y_out"], j.index(1, -3))
                    sp.dma_start(we[j.phase][:, 0:W_E[l]], exp[ds(e, 1), :, :].rearrange("e p n -> p (e n)")).then_inc(q["weights_in"][j.phase], 16)

                def store_y(j):
                    sp.wait_ge(q["y_out"], j.index(1, 1))
                    sp.dma_start(y_dram[0][ds(j.index(ST), ST), :].rearrange("(s p) c -> p s c", p=P),
                                 yo[j.phase][:, :, :]).then_inc(q["scattered"][j.phase], 16)

                def w_first():
                    for r in range(3):
                        weights(Tile(0, r))

                def w_step(j, ahead, up, transposed, mid, down):
                    if ahead:
                        weights(j.ahead(3))
                    if down and l == 0:
                        store_y(j.ahead(-1))

                tiles(sp, w_first, w_step)
                for r in range(4):
                    sp.wait_ge(q["scattered"][r], SCATTER[l] * len(range(r, NJ, 4)))

            q = L[1]

            def final_loads(b):
                wait(sp, final_used, b.index(1, -3))
                rows_ = y_dram[1].rearrange("(k n) c -> n k c", k=2)[ds(b.index(S), S), :, :]
                for t in range(2):
                    sp.dma_start(yfin[b.phase][:, :, t, :], rows_[t * P:(t + 1) * P, :, :]).then_inc(final_in[b.phase], 16)
                sp.dma_start(gfin[b.phase], mod_dram[ds(b.index(1, NB), 1), 5 * D:6 * D].to_broadcast([P, D])).then_inc(final_in[b.phase], 16)

            fours(sp, final_loads)
            sp.wait_ge(stored, 16 * NB)


        @block.gpsimd
        def _(pool):
            def one(ins):
                ins.then_inc(setup_pool, 1)

            one(nc.gpsimd.memset(identf[:, :], 0.0))
            one(nc.gpsimd.memset(identb[:, :], 0.0))
            one(nc.gpsimd.memset(identh[:, :], 0.0))
            one(nc.gpsimd.memset(causal[:, :], 0.0))
            pool.wait_ge(setup_pool, 4)
            for m in (identf, identb, identh):
                one(nc.gpsimd.affine_select(out=m[:, :], in_=m[:, :], compare_op=ALU.not_equal, fill=1.0,
                                            base=0, pattern=[[-1, P]], channel_multiplier=1))
            one(nc.gpsimd.affine_select(out=causal[:, :], in_=causal[:, :], compare_op=ALU.is_ge, fill=MASKED,
                                        base=0, pattern=[[-1, P]], channel_multiplier=1))
            for i in range(2):
                one(nc.gpsimd.memset(Vx[i][:, :, :, :], 0.0))
                one(nc.gpsimd.memset(KT[i][:, :].bitcast(f32), 0.0))
            one(nc.gpsimd.memset(Qx[:, :].bitcast(f32), 0.0))
            one(nc.gpsimd.memset(Kx[:, :].bitcast(f32), 0.0))
            pool.wait_ge(setup_pool, 14)
            for i in range(2):
                one(nc.gpsimd.memset(Vx[i][:, :, :, HD:HD + 1], 1.0))
            one(nc.gpsimd.iota(iota_i[:, 0:P], [[1, P]], base=0, channel_multiplier=0))
            one(nc.gpsimd.iota(iota_i[:, P:P + HI], [[1, HI]], base=0, channel_multiplier=0))
            one(nc.gpsimd.iota(iota_i[:, P + HI:P + HI + NJ], [[1, NJ]], base=0, channel_multiplier=0))
            one(nc.gpsimd.iota(iota_i[:, P + HI + NJ:P + HI + NJ + E], [[1, E]], base=-E, channel_multiplier=0))
            one(nc.gpsimd.iota(iota_i[:, P + HI + NJ + E:P + HI + NJ + 2 * E], [[0, E]], base=1, channel_multiplier=1))
            one(nc.gpsimd.memset(onesb[:, :], 1.0))
            one(nc.gpsimd.memset(before[:, :], 1.0))
            pool.wait_ge(setup_pool, 23)
            one(nc.gpsimd.affine_select(out=before[:, :], in_=before[:, :], compare_op=ALU.is_gt, fill=0.0,
                                        base=0, pattern=[[1, P]], channel_multiplier=-1))
            pool.wait_ge(setup_pool, 24)

            for l in range(2):
                q = L[l]

                def front(b):
                    pool.wait_ge(q["xn_ready"], b.index(2, 2))
                    pool.wait_ge(q["front_in"][b.parity], b.half * 32 + 32)
                    c = Chain(pool, q["front_pool"], 1, b.index)
                    for_all = hF[b.parity][:, :, :]
                    c.link(nc.gpsimd.tensor_tensor(for_all, for_all, modF[b.parity][:, D:2 * D].unsqueeze(1).to_broadcast([P, 2, D]), ALU.mult))
                    nc.gpsimd.tensor_tensor(for_all, for_all, modF[b.parity][:, 0:D].unsqueeze(1).to_broadcast([P, 2, D]),
                                            ALU.add).then_inc(q["h_ready"], 1)
                    c.end()

                def values(b):
                    pool.wait_ge(q["qkv_ready"], b.index(2, 2))
                    wait(pool, q["pv_psum"], b.index(2, -2))
                    passed(pool, pool_passed)
                    nc.gpsimd.tensor_copy(Vx[b.parity][:, :, :, 0:HD],
                                          qkv[b.parity][:, :, 2 * D:3 * D].rearrange("p t (h d) -> p t h d", h=H)).then_inc(q["v_ready"], 1)

                def mask(b, c):
                    pool.wait_ge(q["exp_done"], b.index(6, c + 1))
                    half, kind = c // 3, c % 3
                    v = probs[half][:, kind * 1024:(kind + 1) * 1024]
                    v = v.rearrange("p (h n) -> p h n", h=4 if kind < 2 else 8)[:, :, 0:P]
                    passed(pool, pool_passed)
                    nc.gpsimd.affine_select(out=v, in_=v, compare_op=ALU.is_ge, fill=0.0, base=0,
                                            pattern=[[0, v.shape[1]], [1, P]], channel_multiplier=-1).then_inc(q["masked"], 1)

                def residual(b):
                    pool.wait_ge(q["attn_ready"], b.index(1, 1))
                    xb = Xt[:, ds(b.index(S), S)]
                    nc.gpsimd.tensor_tensor(xb, xb, attn[:, :, :].rearrange("p t c -> p (t c)"), ALU.add).then_inc(q["x1_ready"], 1)

                def back(b):
                    pool.wait_ge(q["xn2_ready"], b.index(2, 2))
                    c = Chain(pool, q["back_pool"], 1, b.index)
                    v = hB[b.parity][:, :, :]
                    c.link(nc.gpsimd.tensor_tensor(v, v, modB[b.parity][:, 2 * D:3 * D].unsqueeze(1).to_broadcast([P, 2, D]), ALU.mult))
                    nc.gpsimd.tensor_tensor(v, v, modB[b.parity][:, D:2 * D].unsqueeze(1).to_broadcast([P, 2, D]),
                                            ALU.add).then_inc(q["h2_ready"], 1)
                    c.end()

                def gather_y(b):
                    wait(pool, q["combined"], b.index(4, -4))
                    passed(pool, pool_passed)
                    for k in range(2):
                        nc.gpsimd.tensor_copy(yidx[b.parity][:, 2 * k:2 * k + 2],
                                              slots[:, 1, ds(b.index(2, k * NT), 2)].bitcast(i32)).then_inc(q["yidx_copied"], 1)
                    pool.wait_ge(q["yidx_copied"], b.index(2, 2))
                    passed(pool, pool_passed)
                    for k in range(2):
                        for t in range(2):
                            nc.gpsimd.indirect_dma_start(
                                out=yin[b.parity][:, k, t, :], out_offset=None, in_=y_dram[0][:, :],
                                in_offset=bass.IndirectOffsetOnAxis(yidx[b.parity][:, 2 * k + t:2 * k + t + 1], 0)).then_inc(q["y_in"][b.parity], 16)

                def combine_y(b):
                    pool.wait_ge(q["y_in"][b.parity], b.half * 64 + 64)
                    pool.wait_ge(q["front_in"][b.parity], b.half * 32 + 32)
                    c = Chain(pool, q["combined"], 4, b.index)
                    both = yin[b.parity][:, :, :, :]
                    gates = G[0][:, :].rearrange("p (k t) -> p k t", k=2)[:, :, ds(b.index(2), 2)]
                    c.link(nc.gpsimd.tensor_tensor(both, both, gates.unsqueeze(3).to_broadcast([P, 2, 2, D]), ALU.mult))
                    c.link(nc.gpsimd.tensor_tensor(ycomb[:, :, :], both[:, 0], both[:, 1], ALU.add))
                    c.link(nc.gpsimd.tensor_tensor(ycomb[:, :, :], ycomb[:, :, :], modG[b.parity][:, :].unsqueeze(1).to_broadcast([P, 2, D]), ALU.mult))
                    xb = Xt[:, ds(b.index(S), S)]
                    c.link(nc.gpsimd.tensor_tensor(xb, xb, ycomb[:, :, :].rearrange("p t c -> p (t c)"), ALU.add))
                    c.end()

                def step(b, stage):
                    if l == 0:
                        stage(0, mask, 0)
                        stage(0, mask, 1)
                        stage(1, values)
                        stage(3, front)
                        stage(0, mask, 2)
                        stage(-2, back)
                        stage(0, mask, 3)
                        stage(0, mask, 4)
                        stage(-1, residual)
                        stage(0, mask, 5)
                    else:
                        stage(4, gather_y)
                        stage(0, mask, 0)
                        stage(0, mask, 1)
                        stage(1, values)
                        stage(0, mask, 2)
                        stage(-2, back)
                        stage(3, front)
                        stage(0, mask, 3)
                        stage(4, combine_y)
                        stage(0, mask, 4)
                        stage(-1, residual)
                        stage(0, mask, 5)

                if l == 1:
                    for r in range(4):
                        pool.wait_ge(L[0]["scattered"][r], SCATTER[0] * len(range(r, NJ, 4)))
                steps(pool, step)
                if l == 0:
                    pool.wait_ge(q["logits_ready"], NB)
                    for v in (KT[0], KT[1], Qx, Kx):
                        one(nc.gpsimd.memset(v[:, :].bitcast(f32), 0.0))
                    pool.wait_ge(setup_pool, 28)
                    for piece in range(3):
                        at = 6 * HD + piece
                        one(nc.gpsimd.memset(Kx[:, :].rearrange("p (h n) -> p h n", n=64)[:, :, at:at + 1], 1.0))

                pool.wait_ge(q["index_ready"], 2)
                for i in range(2):
                    pool.wait_ge(q["h2_out"][i], 16 * (NB // 2))

                def gather(j):
                    wait(pool, q["xT_psum"], j.index(1, -3))
                    passed(pool, pool_passed)
                    nc.gpsimd.tensor_copy(idx[j.phase][:, 0:2], gat_i[:, ds(j.index(2), 2)]).then_inc(q["index_copied"], 1)
                    pool.wait_ge(q["index_copied"], j.index(1, 1))
                    passed(pool, pool_passed)
                    for s_ in range(2):
                        nc.gpsimd.indirect_dma_start(
                            out=xg[j.phase][:, s_, :], out_offset=None, in_=h_dram[l][:, :],
                            in_offset=bass.IndirectOffsetOnAxis(idx[j.phase][:, s_:s_ + 1], 0)).then_inc(q["gathered"][j.phase], 16)

                def scatter(j):
                    wait(pool, q["scattered"][j.phase], j.quarter * SCATTER[l])
                    passed(pool, pool_passed)
                    nc.gpsimd.tensor_copy(idx[j.phase][:, 2:4], sca_i[:, ds(j.index(2), 2)]).then_inc(q["scatter_index"], 1)
                    pool.wait_ge(q["scatter_index"], j.index(1, 1))
                    pool.wait_ge(q["y_out"], j.index(1, 1))
                    passed(pool, pool_passed)
                    for s_ in range(2):
                        nc.gpsimd.indirect_dma_start(
                            out=y_dram[l][:, :], out_offset=bass.IndirectOffsetOnAxis(idx[j.phase][:, 2 + s_:3 + s_], 0),
                            in_=yo[j.phase][:, s_, :], in_offset=None,
                            bounds_check=2 * N - 1, oob_is_err=False).then_inc(q["scattered"][j.phase], 16)

                def g_first():
                    for r in range(3):
                        gather(Tile(0, r))

                def g_step(j, ahead, up, transposed, mid, down):
                    if ahead:
                        gather(j.ahead(3))
                    if down and l == 1:
                        scatter(j.ahead(-1))

                tiles(pool, g_first, g_step)

        @block.scalar
        def _(act):
            act.wait_ge(setup_dma, 96)
            nc.scalar.activation(tanh[1][:, 0:2 * NB], tanh[0][:, 0:2 * NB], ACT.Silu).then_inc(setup_act, 1)

            for l in range(2):
                q = L[l]

                def copy_h(b):
                    act.wait_ge(q["hT_psum"], b.index(1, 1))
                    wait(act, q["qkv_psum"], b.index(2, 0))
                    nc.scalar.activation(hT[:, :, :], ps[:, 4, 0:S].rearrange("p (t c) -> p t c", t=2), ACT.Copy).then_inc(q["hT_ready"], 1)

                def copy_qkv(b):
                    wait(act, q["slots_ready"], b.index(1, -1))
                    wait(act, q["v_ready"], b.index(1, -1))
                    for t in range(2):
                        act.wait_ge(q["qkv_psum"], b.index(2, t + 1))
                        nc.scalar.activation(qkv[b.parity][:, t, :], ps[:, 4 + t, 0:3 * D], ACT.Copy).then_inc(q["qkv_ready"], 1)

                def fill_q(b):
                    act.wait_ge(q["slots_ready"], b.index(1, 1))
                    v = Qx[:, :].rearrange("p (th n) -> p th n", n=64)
                    wait(act, q["tq_psum"], b.index(2, 0))
                    for piece, at, n in Q_SLOTS:
                        src = pieces[:, piece, :].rearrange("p (t q) -> p t q", t=2)[:, :, 0:P]
                        for t in range(2):
                            nc.scalar.activation(
                                v[:, t * H:(t + 1) * H, at:at + n * HD].rearrange("p h (s d) -> p h s d", s=n),
                                src[:, t, :].rearrange("p (h d) -> p h d", h=H).unsqueeze(2).to_broadcast([P, H, n, HD]),
                                ACT.Copy).then_inc(q["slots_act"], 1)

                def fill_k(b):
                    act.wait_ge(q["slots_ready"], b.index(1, 1))
                    wait(act, q["tk_psum"], b.index(1, 0))
                    v = Kx[:, :].rearrange("p (th n) -> p th n", n=64)
                    for at, n in ((0, 3), (3, 2), (5, 1)):
                        for t in range(2):
                            src = pieces[:, 0:n, t * 2 * D + D:t * 2 * D + 2 * D].rearrange("p n (h d) -> p h n d", h=H)
                            nc.scalar.activation(v[:, t * H:(t + 1) * H, at * HD:(at + n) * HD].rearrange("p h (n d) -> p h n d", n=n),
                                                 src, ACT.Copy).then_inc(q["slots_act"], 1)

                def copy_qm(b):
                    act.wait_ge(q["tq_psum"], b.index(2, 2))
                    wait(act, q["score_psum"], b.index(6, -6))
                    nc.scalar.activation(QT[b.parity][:, 4 * S:8 * S], ps[:, 5, :].bitcast(bf16), ACT.Copy).then_inc(q["qk_ready"], 1)

                def copy_k(b):
                    act.wait_ge(q["tk_psum"], b.index(1, 1))
                    wait(act, q["score_psum"], b.index(6, -6))
                    n = SLOT[1]
                    nc.scalar.activation(KT[b.parity][n:2 * n, 8 * S:16 * S], ps[n:2 * n, 4:6, :].rearrange("p a b -> p (a b)").bitcast(bf16),
                                         ACT.Copy).then_inc(q["k_ready"], 1)

                def softmax(b, c):
                    act.wait_ge(q["score_psum"], b.index(6, c + 1))
                    src = ps[:, 2 * (c % 2):2 * (c % 2) + 2, :].rearrange("p a b -> p (a b)")
                    half, kind = c // 3, c % 3
                    dst = probs[half][:, kind * 1024:(kind + 1) * 1024]
                    wait(act, q["pv_psum"], b.index(2, half - 1))
                    if l == 0:
                        wait(act, q["exp_done"], b.index(6, c - 1))
                        nc.scalar.activation(tanh[c % 2][:, :], src, ACT.Tanh, scale=QK_SCALE / SOFTCAP).then_inc(q["tanh_done"], 1)
                        act.wait_ge(q["tanh_done"], b.index(6, c + 1))
                        nc.scalar.activation(dst, tanh[c % 2][:, :], ACT.Exp, scale=SOFTCAP).then_inc(q["exp_done"], 1)
                    else:
                        nc.scalar.activation(dst, src, ACT.Exp, scale=QK_SCALE).then_inc(q["exp_done"], 1)

                def copy_o(b, half):
                    act.wait_ge(q["pv_psum"], b.index(2, half + 1))
                    wait(act, q["ot_psum"], b.index(2, -2))
                    nc.scalar.activation(oT[b.parity][:, half * 512:(half + 1) * 512], ps[:, 6, :], ACT.Copy).then_inc(q["o_ready"], 1)

                def copy_y(b):
                    act.wait_ge(q["yT_psum"], b.index(1, 1))
                    wait(act, q["proj_psum"], b.index(1, 0))
                    nc.scalar.activation(yT[:, :, :], ps[:, 7, 0:S].rearrange("p (t c) -> p t c", t=2), ACT.Copy).then_inc(q["yT_ready"], 1)

                def copy_h2(b):
                    act.wait_ge(q["h2T_psum"], b.index(1, 1))
                    wait(act, q["router_psum"], b.index(1, 0))
                    nc.scalar.activation(h2T[:, :, :], ps[:, 7, 0:S].rearrange("p (t c) -> p t c", t=2), ACT.Copy).then_inc(q["h2T_ready"], 1)

                def step(b, stage):
                    if l == 0:
                        stage(0, softmax, 0)
                        stage(2, copy_h)
                        stage(0, softmax, 1)
                        stage(-1, copy_o, 1)
                        stage(0, softmax, 2)
                        stage(2, copy_qkv)
                        stage(0, softmax, 3)
                        stage(0, softmax, 4)
                        stage(-1, copy_y)
                        stage(0, softmax, 5)
                        stage(0, copy_o, 0)
                        stage(-2, copy_h2)
                    else:
                        stage(2, copy_h)
                        stage(1, fill_q)
                        stage(2, copy_qkv)
                        stage(0, softmax, 0)
                        stage(-1, copy_o, 1)
                        stage(1, fill_k)
                        stage(0, softmax, 1)
                        stage(1, copy_k)
                        stage(0, softmax, 2)
                        stage(0, softmax, 3)
                        stage(-1, copy_y)
                        stage(0, softmax, 4)
                        stage(-2, copy_h2)
                        stage(0, softmax, 5)
                        stage(1, copy_qm)
                        stage(0, copy_o, 0)

                steps(act, step)
                act.wait_ge(q["onehot_ready"], 3)
                nc.scalar.activation(top[:, 5, :], top[:, 4, :], ACT.Exp).then_inc(gate_exp, 1)

                def scaled(g):
                    hot = QT[g.parity][:, 0:8 * HI].rearrange("p (r n) -> p r n", r=8)
                    act.wait_ge(q["perm_ready"], g.index(2, 1))
                    wait(act, q["perm_used"], g.index(1, -1))
                    for r in range(8):
                        last = nc.scalar.activation(permB[g.parity][:, r, 1, :], hot[:, r, :], ACT.Copy,
                                                    scale=pair_base[:, ds(g.index(8, r), 1)])
                    last.then_inc(q["perm_scaled"], 1)

                scaled(Batch(0, 0))
                scaled(Batch(0, 1))
                with act.Fori(1, NT // 8) as i:
                    scaled(Batch(i, 0))
                    scaled(Batch(i, 1))

                def pair(j):
                    return ps[:, 2 + 2 * (j.phase % 2):4 + 2 * (j.phase % 2), :].rearrange("p a b -> p (a b)")

                def a_step(j, ahead, up, transposed, mid, down):
                    if l == 0:
                        if up:
                            hidden(j.ahead(1))
                    else:
                        if up:
                            biased(j.ahead(1))
                        if mid:
                            gated(j)

                def hidden(j):
                    act.wait_ge(q["up_psum"], j.index(1, 1))
                    wait(act, q["down_psum"], j.index(1, -1))
                    nc.scalar.activation(hid[j.phase % 2][:, :], pair(j), ACT.Gelu).then_inc(q["hidden_ready"], 1)

                def biased(j):
                    act.wait_ge(q["up_psum"], j.index(1, 1))
                    wait(act, q["z_ready"], j.index(2, -2))
                    w = we[j.phase]
                    for f in range(2):
                        nc.scalar.activation(hid[j.phase % 2][:, f * ST:(f + 1) * ST], pair(j)[:, f * ST:(f + 1) * ST], ACT.Identity,
                                             bias=w[:, BIAS + f:BIAS + f + 1]).then_inc(q["up_act"], 1)

                def gated(j):
                    act.wait_ge(q["mid_psum"], j.index(1, 1))
                    wait(act, q["down_psum"], j.index(1, -1))
                    w = we[j.phase]
                    for f in range(2):
                        nc.scalar.activation(hid[j.phase % 2][:, 512 + f * ST:512 + (f + 1) * ST], ps[:, 6, f * ST:(f + 1) * ST], ACT.Silu,
                                             bias=w[:, BIAS + 4 + f:BIAS + 5 + f]).then_inc(q["s_ready"], 1)

                tiles(act, (lambda: hidden(Tile(0, 0))) if l == 0 else (lambda: biased(Tile(0, 0))), a_step)

            def final_scale(b):
                act.wait_ge(final_in[b.phase], b.quarter * 48 + 48)
                for k in range(2):
                    for t in range(2):
                        v = yfin[b.phase][:, k, t, :]
                        last = nc.scalar.activation(v, v, ACT.Copy, scale=G[1][:, ds(b.index(2, k * NT + t), 1)])
                last.then_inc(final_scaled, 1)

            def final_store(b):
                act.wait_ge(final_used, b.index(1, 1))
                nc.scalar.dma_start(out[ds(b.index(S), S), :].rearrange("(t p) c -> p t c", p=P),
                                    Xt[:, ds(b.index(S), S)].rearrange("p (t c) -> p t c", t=2)).then_inc(stored, 16)

            def final_step(b):
                final_scale(b)
                if not isinstance(b.quarter, int) or b.index() > 0:
                    final_store(b.ahead(-1))

            fours(act, final_step)
            final_store(Tile(NB // 4 - 1, 3))

        @block.tensor
        def _(pe):
            pe.wait_ge(setup_act, 1)
            for l in range(2):
                sc = tanh[1][:, l * NB:(l + 1) * NB]
                wm = probs[0][:, l * 768:(l + 1) * 768]
                nc.tensor.matmul(ps[0:NB, 2 * l, :], sc, wm[:, 0:512], start=True, stop=True)
                nc.tensor.matmul(ps[0:NB, 2 * l + 1, 0:256], sc, wm[:, 512:768], start=True, stop=True).then_inc(setup_pe, 1)
            pe.wait_ge(setup_dve, 12)
            for l in range(2):
                q = L[l]
                nh = heads(l)
                ng = H // nh
                dt = f16 if l == 0 else bf16
                ident = identh if l == 0 else identb

                def transposed_h(b):
                    pe.wait_ge(q["h_ready"], b.index(1, 1))
                    wait(pe, q["qkv_ready"], b.index(2, 0))
                    wait(pe, q["qk_ready"], b.index(QK_STEPS[l], -QK_STEPS[l]))
                    for t in range(2):
                        last = nc.tensor.transpose(ps[:, 4, t * P:(t + 1) * P], hF[b.parity][:, t, :], identf[:, :])
                    last.then_inc(q["hT_psum"], 1)

                def qkv_products(b):
                    pe.wait_ge(q["hT_ready"], b.index(1, 1))
                    for t in range(2):
                        nc.tensor.matmul(ps[:, 4 + t, 0:3 * D], hT[:, t, :], wqkv_sb[:, l, :], start=True, stop=True).then_inc(q["qkv_psum"], 1)

                def projections_copied(b):
                    if b.plus(1).exists():
                        pe.wait_ge(q["qkv_ready"], b.index(2, 4))

                def transposed_qk(b):
                    pe.wait_ge(q["slots_ready"], b.index(1, 1))
                    projections_copied(b)
                    for i, src in enumerate((Qx, Kx)):
                        v = src[:, 0:2 * H * SLOT[l]].bitcast(dt)
                        dst = ps[:, 4 + i, :].bitcast(dt)
                        for g in range(ng):
                            for t in range(2):
                                at = (t * H + g * nh) * SLOT[l]
                                last = nc.tensor.transpose(dst[:, g * S + t * P:g * S + (t + 1) * P], v[:, at:at + P], ident[:, :])
                        last.then_inc(q["qk_psum"], 1)

                def slots_transposed(b, src, first, done):
                    v = src[:, 0:2 * H * SLOT[1]]
                    dst = ps[:, 4:6, :].rearrange("p a b -> p (a b)").bitcast(bf16)
                    for g in range(ng):
                        for t in range(2):
                            at = (t * H + g * nh) * SLOT[1]
                            last = nc.tensor.transpose(dst[:, g * S + t * P:g * S + (t + 1) * P], v[:, at:at + P], ident[:, :])
                    last.then_inc(done, 1)

                def transposed_q(b):
                    pe.wait_ge(q["slots_act"], b.index(12, 6))
                    projections_copied(b)
                    slots_transposed(b, Qx, 0, q["tq_psum"])

                def transposed_k(b):
                    pe.wait_ge(q["slots_act"], b.index(12, 12))
                    pe.wait_ge(q["qa_ready"], b.index(1, 1))
                    slots_transposed(b, Kx, 0, q["tk_psum"])

                def max_scores(b, m):
                    bank = 4 + m % 2
                    if m < 2:
                        pe.wait_ge(q["k_ready"], b.index(2, 2))
                    else:
                        pe.wait_ge(q["max_done"], b.index(12, m - 1))
                    kv = KT[b.parity][:, :]
                    if m < 8:
                        blocks = [(i * S, S, 2 * m + i, 1) for i in range(2)]
                    else:
                        blocks = [(i * P, P, 4 * (m - 8) + i, 0) for i in range(4)]
                    for col, n, h, qt in blocks:
                        g, i = h // nh, h % nh
                        nc.tensor.matmul(ps[:, bank, col:col + n], QTa[:, g * S + qt * P:g * S + qt * P + P],
                                         kv[:, (i * ng + g) * S:(i * ng + g) * S + n], start=True, stop=False)
                        last = nc.tensor.matmul(ps[:, bank, col + n - P:col + n], identb[:, :], causal[:, :], start=False, stop=True)
                    last.then_inc(q["max_psum"], 1)

                def transposed_qm(b):
                    pe.wait_ge(q["m_ready"], b.index(1, 1))
                    slots_transposed(b, Qx, 0, q["tq_psum"])

                def scores(b, c):
                    wait(pe, q["tanh_done"] if l == 0 else q["exp_done"], b.index(6, c - 1))
                    if c == 0:
                        pe.wait_ge(q["qk_ready"], b.index(QK_STEPS[l], QK_STEPS[l]))
                    flat = ps[:, 2 * (c % 2):2 * (c % 2) + 2, :].rearrange("p a b -> p (a b)")
                    qv, kv = QT[b.parity][:, 0:ng * S].bitcast(dt), KT[b.parity][:, 0:nh * ng * S].bitcast(dt)
                    for col, n, h, kt, q0 in chunk_blocks(c):
                        g, i = h // nh, h % nh
                        last = nc.tensor.matmul(flat[:, col:col + n],
                                                kv[:, (i * ng + g) * S + kt * P:(i * ng + g) * S + kt * P + P],
                                                qv[:, g * S + q0:g * S + q0 + n], start=True, stop=True)
                    last.then_inc(q["score_psum"], 1)

                def values(b, half):
                    pe.wait_ge(q["masked"], b.index(6, 3 * (half + 1)))
                    if half == 0:
                        pe.wait_ge(q["v_ready"], b.index(1, 1))
                    wait(pe, q["o_ready"], b.index(2, half))
                    pr = probs[half]
                    for g in range(2):
                        for kt in range(2):
                            for i in range(4):
                                h = half * 8 + g * 4 + i
                                o = ps[32 * i:32 * i + 32, 6, g * S:(g + 1) * S]
                                v = Vx[b.parity][:, kt, h, :]
                                if kt == 0:
                                    nc.tensor.matmul(o, v, pr[:, g * 1024 + i * S:g * 1024 + (i + 1) * S], start=True, stop=False)
                                else:
                                    last = nc.tensor.matmul(o[:, P:S], v, pr[:, 2048 + (g * 4 + i) * P:2048 + (g * 4 + i + 1) * P],
                                                            start=False, stop=True)
                    last.then_inc(q["pv_psum"], 1)

                def transposed_o(b, t):
                    pe.wait_ge(q["o_ready"], b.index(2, 2))
                    if t == 0:
                        wait(pe, q["attn_ready"], b.index(1, 0))
                        wait(pe, q["logits_ready"], b.index(1, -1))
                    else:
                        pe.wait_ge(q["y_ready"], b.index(2, 1))
                    for g in range(4):
                        last = nc.tensor.transpose(ps[:, 7, g * P:(g + 1) * P], oT[b.parity][:, g * S + t * P:g * S + (t + 1) * P], identf[:, :])
                    last.then_inc(q["ot_psum"], 1)

                def transposed_y(b):
                    pe.wait_ge(q["y_ready"], b.index(2, 2))
                    for t in range(2):
                        last = nc.tensor.transpose(ps[:, 7, t * P:(t + 1) * P], y[:, t, :], identf[:, :])
                    last.then_inc(q["yT_psum"], 1)

                def projection(b):
                    pe.wait_ge(q["yT_ready"], b.index(1, 1))
                    for t in range(2):
                        last = nc.tensor.matmul(ps[:, 7, S + t * P:S + (t + 1) * P], yT[:, t, :], wo_sb[:, l, :], start=True, stop=True)
                    last.then_inc(q["proj_psum"], 1)

                def transposed_h2(b):
                    pe.wait_ge(q["h2_ready"], b.index(1, 1))
                    if not isinstance(b.half, int) or b.index() < NB - 1:
                        pe.wait_ge(q["attn_ready"], b.index(1, 2))
                    for t in range(2):
                        last = nc.tensor.transpose(ps[:, 7, t * P:(t + 1) * P], hB[b.parity][:, t, :], identf[:, :])
                    last.then_inc(q["h2T_psum"], 1)

                def router_logits(b):
                    pe.wait_ge(q["h2T_ready"], b.index(1, 1))
                    for t in range(2):
                        last = nc.tensor.matmul(ps[:, 7, S + t * E:S + (t + 1) * E], h2T[:, t, :], router_sb[:, l, :], start=True, stop=True)
                    last.then_inc(q["router_psum"], 1)

                def maxima(b, first, end):
                    for m in range(first, end):
                        max_scores(b, m)

                def step(b, stage):
                    if l == 0:
                        stage(0, scores, 0)
                        stage(-3, router_logits)
                        stage(2, transposed_h)
                        stage(0, scores, 1)
                        stage(-1, values, 1)
                        stage(0, scores, 2)
                        stage(-1, transposed_o, 0)
                        stage(2, qkv_products)
                        stage(0, scores, 3)
                        stage(-1, transposed_o, 1)
                        stage(0, scores, 4)
                        stage(1, transposed_qk)
                        stage(-1, transposed_y)
                        stage(0, scores, 5)
                        stage(-1, projection)
                        stage(0, values, 0)
                        stage(-2, transposed_h2)
                    else:
                        stage(2, transposed_h)
                        stage(0, scores, 0)
                        stage(2, qkv_products)
                        stage(0, scores, 1)
                        stage(-1, values, 1)
                        stage(1, transposed_q)
                        stage(-1, transposed_o, 0)
                        stage(0, scores, 2)
                        stage(1, transposed_k)
                        stage(0, scores, 3)
                        stage(1, maxima, 0, 2)
                        stage(-1, transposed_o, 1)
                        stage(1, maxima, 2, 4)
                        stage(-1, transposed_y)
                        stage(1, maxima, 4, 6)
                        stage(-1, projection)
                        stage(1, maxima, 6, 8)
                        stage(0, scores, 4)
                        stage(1, maxima, 8, 10)
                        stage(-2, transposed_h2)
                        stage(1, maxima, 10, 12)
                        stage(0, scores, 5)
                        stage(0, values, 0)
                        stage(1, transposed_qm)
                        stage(-2, router_logits)

                steps(pe, step)
                pe.wait_ge(q["onehot_ready"], 2)
                for k in range(2):
                    rhs = chosen[:, k, :, :].rearrange("p e t -> p (e t)")
                    nc.tensor.matmul(ps[:, k, :], before[:, :], rhs, start=True, stop=True)
                    nc.tensor.matmul(ps[:, 2 + k, :], onesb[:, :], rhs, start=True, stop=True).then_inc(q["prefix_psum"], 1)

                def invert(g, start, stop):
                    pe.wait_ge(q["perm_ready"], g.index(2, 2))
                    pe.wait_ge(q["perm_scaled"], g.index(1, 1))
                    a_, b_ = permA[g.parity], permB[g.parity]
                    for r in range(8):
                        last = nc.tensor.matmul(ps[:, 4, 0:2 * HI], a_[:, r, :], b_[:, r, :, :].rearrange("p a b -> p (a b)"),
                                                start=start and r == 0, stop=stop and r == 7)
                    last.then_inc(q["perm_used"], 1)

                groups = 2 * NT // 8
                invert(Batch(0, 0), True, False)
                invert(Batch(0, 1), False, False)
                with pe.Fori(1, groups // 2 - 1) as i:
                    invert(Batch(i, 0), False, False)
                    invert(Batch(i, 1), False, False)
                invert(Batch(groups // 2 - 1, 0), False, False)
                invert(Batch(groups // 2 - 1, 1), False, True)

                def pair(j):
                    return ps[:, 2 + 2 * (j.phase % 2):4 + 2 * (j.phase % 2), :].rearrange("p a b -> p (a b)")

                def transposed_x(j):
                    pe.wait_ge(q["gathered"][j.phase], loads(l, j) * 32)
                    wait(pe, q["xT_ready"], j.index(1, -1))
                    for s_ in range(2):
                        last = nc.tensor.transpose(ps[:, j.phase % 2, s_ * P:(s_ + 1) * P], xg[j.phase][:, s_, :], identf[:, :])
                    last.then_inc(q["xT_psum"], 1)

                def up_products(j):
                    pe.wait_ge(q["xT_ready"], j.index(1, 1))
                    pe.wait_ge(q["weights_in"][j.phase], loads(l, j) * 16)
                    if l == 0:
                        wait(pe, q["hidden_ready"], j.index(1, -1))
                    else:
                        wait(pe, q["z_ready"], j.index(2, -2))
                    o = pair(j)
                    for f in range(4):
                        last = nc.tensor.matmul(o[:, f * ST:(f + 1) * ST], we[j.phase][:, f * P:(f + 1) * P], xT[j.phase % 2][:, :],
                                                start=True, stop=True)
                    last.then_inc(q["up_psum"], 1)

                def mid_products(j):
                    pe.wait_ge(q["z_ready"], j.index(2, 2))
                    wait(pe, q["s_ready"], j.index(2, 0))
                    for g in range(2):
                        for f in range(2):
                            at = 512 + f * FF1 + g * P
                            last = nc.tensor.matmul(ps[:, 6, g * ST:(g + 1) * ST], we[j.phase][:, at:at + P],
                                                    hz[j.phase % 2][:, f * ST:(f + 1) * ST], start=f == 0, stop=f == 1)
                    last.then_inc(q["mid_psum"], 1)

                def down_products(j):
                    if l == 0:
                        pe.wait_ge(q["hidden_ready"], j.index(1, 1))
                    else:
                        pe.wait_ge(q["s_ready"], j.index(2, 2))
                    wait(pe, q["y_out"], j.index(1, 0))
                    bank = 6 + j.phase % 2 if l == 0 else 7
                    nf, w0, h0 = (4, 512, 0) if l == 0 else (2, 1024, 512)
                    for s_ in range(2):
                        for f in range(nf):
                            last = nc.tensor.matmul(ps[:, bank, s_ * P:(s_ + 1) * P],
                                                    hid[j.phase % 2][:, h0 + f * ST + s_ * P:h0 + f * ST + (s_ + 1) * P],
                                                    we[j.phase][:, w0 + f * P:w0 + (f + 1) * P], start=f == 0, stop=f == nf - 1)
                    last.then_inc(q["down_psum"], 1)

                def p_first():
                    transposed_x(Tile(0, 0))
                    up_products(Tile(0, 0))
                    transposed_x(Tile(0, 1))

                def p_step(j, ahead, up, transposed, mid, down):
                    if up:
                        up_products(j.ahead(1))
                    if transposed:
                        transposed_x(j.ahead(2))
                    if mid and l == 1:
                        mid_products(j)
                    if down:
                        down_products(j.ahead(-1))

                tiles(pe, p_first, p_step)

        @block.vector
        def _(dve):
            V = nc.vector
            m = probs[1][0:NB, 0:1536].rearrange("p (l s c) -> p l s c", l=2, s=6)
            tmp = probs[1][0:NB, 2048:2048 + 512].rearrange("p (l s c) -> p l s c", l=2, s=2)
            n = 0

            def link(ins):
                nonlocal n
                ins.then_inc(setup_dve, 1)
                n += 1
                dve.wait_ge(setup_dve, n)

            dve.wait_ge(setup_pe, 2)
            for l in range(2):
                link(V.tensor_copy(probs[1][0:NB, l * 768:(l + 1) * 768],
                                   ps[0:NB, 2 * l:2 * l + 2, :].rearrange("p a b -> p (a b)")[:, 0:768]))
            for l in range(2):
                sc = m[:, l, 1:5:3, :]
                link(V.tensor_scalar(sc, sc, 1.0, None, ALU.add))
                g = m[:, l, 2:6:3, :]
                sign = tmp[:, l, :, :]
                link(V.tensor_scalar(sign, g, 0.0, 2.0, ALU.is_ge, ALU.mult))
                link(V.tensor_scalar(sign, sign, 1.0, None, ALU.subtract))
                link(V.scalar_tensor_tensor(g, g, -1.0, g, ALU.mult, ALU.max))
                link(V.scalar_tensor_tensor(g, g, 0.25, sign, ALU.max, ALU.mult))

            def rsqrt(c, *sources):
                n = 4 + 64 * (len(sources) > 2)
                r, v, i0, a = [roots[:, i, 0:n] for i in range(4)]
                c.link(*[V.tensor_scalar(roots[:, 1, at:at + w], src, k, eps, ALU.mult, ALU.add) for src, k, eps, at, w in sources])
                c.link(V.tensor_scalar(i0.bitcast(i32), v.bitcast(i32), 1, None, ALU.arith_shift_right))
                c.link(V.tensor_scalar(r.bitcast(i32), i0.bitcast(i32), -1.0, float(MAGIC), ALU.mult, ALU.add))
                for _ in range(3):
                    c.link(V.tensor_tensor(a, r, r, ALU.mult))
                    c.link(V.scalar_tensor_tensor(a, a, -0.5, v, ALU.mult, ALU.mult))
                    c.link(V.scalar_tensor_tensor(r, a, 1.5, r, ALU.add, ALU.mult))

            dve.wait_ge(setup_pool, 24)
            link(V.tensor_copy(iota_f[:, 0:P + HI + NJ + 2 * E], iota_i[:, 0:P + HI + NJ + 2 * E]))
            link(V.tensor_copy(lane_b[:, :], lane))
            link(V.tensor_copy(block_b[:, :], block_no))
            for v in (ms[:, :], mvF[:, :, :], mvB[:, :, :]):
                link(V.memset(v, 1.0))
            link(V.tensor_scalar(pair_base[:, :], lane, float(P), None, ALU.mult))

            for l in range(2):
                q = L[l]
                nh = heads(l)
                ng = H // nh
                dt = f16 if l == 0 else bf16

                def normalize(b, mv, at, dst, done):
                    for t in range(2):
                        V.tensor_scalar(dst[:, t, :], Xt[:, ds(b.index(S, t * D), D)], mv[:, t, 0:1], roots[:, 0, at + t:at + t + 1],
                                        ALU.subtract, ALU.mult).then_inc(done, 1)
                    dve.wait_ge(done, b.index(2, 2))

                def step_roots(b):
                    c = Chain(dve, q["roots_dve"], ROOTS[l], lambda steps_, n_: b.index(steps_, 4 * steps_ + n_))
                    norms = []
                    if b.plus(3).exists():
                        f = b.plus(3)
                        if l == 0:
                            dve.wait_ge(q["front_in"][f.parity], f.half * 32 + 32)
                        else:
                            dve.wait_ge(q["combined"], f.index(4, 4))
                        norms += [(f, stF, mvF, t) for t in range(2)]
                    if b.plus(-2).exists():
                        dve.wait_ge(q["x1_ready"], b.plus(-2).index(1, 1))
                        norms += [(b.plus(-2), stB, mvB, t) for t in range(2)]
                    passed(dve, dve_passed)
                    c.link(*[V.bn_stats(st[:, t, :], Xt[:, ds(n.index(S, t * D), D)]) for n, st, mv, t in norms], of=4)
                    passed(dve, dve_passed)
                    c.link(*[V.bn_aggr(mv[:, t, :], st[:, t, :]) for n, st, mv, t in norms], of=4)
                    sources = [(mvF[:, :, 1], 1.0, EPS, 0, 2), (mvB[:, :, 1], 1.0, EPS, 2, 2)]
                    if l == 0:
                        sources.append((ms[:, :], 1.0 / HD, QK_EPS, 4, 64))
                    rsqrt(c, *sources)
                    c.end()

                chain = {}

                def front_norm(b):
                    wait(dve, q["hT_psum"], b.index(1, -1))
                    normalize(b, mvF, 0, hF[b.parity], q["xn_ready"])

                def back_norm(b):
                    wait(dve, q["h2_out"][b.parity], b.half * 16)
                    wait(dve, q["h2T_psum"], b.index(1, -1))
                    normalize(b, mvB, 2, hB[b.parity], q["xn2_ready"])

                def mean_squares(b):
                    c = chain["f"] = Chain(dve, q["front_dve"], FRONT[l], b.index)
                    dve.wait_ge(q["qkv_ready"], b.index(2, 2))
                    c.link(V.tensor_tensor(qk2[:, :].rearrange("p (t n) -> p t n", t=2), qkv[b.parity][:, :, 0:2 * D],
                                           qkv[b.parity][:, :, 0:2 * D], ALU.mult))
                    c.link(V.reduce_sum(ms[:, :], qk2[:, :].rearrange("p (h d) -> p h d", d=HD), AX.X))

                def front_slots(b):
                    c = chain["f"]
                    qk = qkv[b.parity][:, :, 0:2 * D]
                    c.link(V.tensor_tensor(qk2[:, :].rearrange("p (t h d) -> p t h d", t=2, d=HD),
                                           qk.rearrange("p t (h d) -> p t h d", d=HD),
                                           roots[:, 0, 4:68].rearrange("p (t h) -> p t h", t=2).unsqueeze(3).to_broadcast([P, 2, 2 * H, HD]), ALU.mult))
                    wait(dve, q["qk_psum"], b.index(2, 0))
                    s = qk2[:, :].rearrange("p (t s h d) -> p t s h d", t=2, s=2, h=H)
                    xs = [t_[:, 0:2 * H * SLOT[0]].bitcast(f16).rearrange("p (t h n) -> p t h n", t=2, h=H) for t_ in (Qx, Kx)]
                    c.link(*[V.tensor_copy(xs[i][:, :, :, 0:HD], s[:, :, i]) for i in range(2)])
                    low = (2 * HD, HD)
                    high = (HD, 2 * HD)
                    for i in range(2):
                        V.tensor_tensor(xs[i][:, :, :, low[i]:low[i] + HD], s[:, :, i], xs[i][:, :, :, 0:HD], ALU.subtract).then_inc(q["front_dve"], 1)
                    for i in range(2):
                        V.tensor_copy(xs[i][:, :, :, high[i]:high[i] + HD], xs[i][:, :, :, 0:HD]).then_inc(q["front_dve"], 1)
                    c.n += 4
                    dve.wait_ge(q["front_dve"], b.index(FRONT[l], c.n))
                    dve.sem_inc(q["slots_ready"], 1)
                    c.end()

                def split(b, part):
                    qk = qkv[b.parity][:, :, 0:2 * D]
                    v2 = lambda t: t[:, :].rearrange("p (t n) -> p t n", t=2)
                    pc = [v2(pieces[:, i, :]) for i in range(3)]
                    c = Chain(dve, q["pieces_dve"], PIECES, b.index)
                    if part == 0:
                        dve.wait_ge(q["qkv_ready"], b.index(2, 2))
                        wait(dve, q["slots_act"], b.index(12, 0))
                        c.link(V.tensor_copy(pc[0], qk))
                        V.tensor_tensor(v2(qk2), qk, pc[0], ALU.subtract).then_inc(q["pieces_dve"], 1)
                    else:
                        c.n = 2
                        dve.wait_ge(q["pieces_dve"], b.index(PIECES, c.n))
                        c.link(V.tensor_copy(pc[1], v2(qk2)))
                        c.link(V.tensor_tensor(pc[2], v2(qk2), pc[1], ALU.subtract))
                        dve.sem_inc(q["slots_ready"], 1)
                        c.end()

                def front_copies(b):
                    words = ng * S // 2
                    dve.wait_ge(q["qk_psum"], b.index(2, 1))
                    wait(dve, q["score_psum"], b.index(6, -6))
                    V.tensor_copy(QT[b.parity][:, 0:ng * S].bitcast(i32), ps[:, 4, 0:words].bitcast(i32)).then_inc(q["qk_ready"], 1)
                    dve.wait_ge(q["qk_psum"], b.index(2, 2))
                    n = SLOT[l]
                    for i in range(nh):
                        V.tensor_copy(KT[b.parity][i * n:(i + 1) * n, i * ng * S:(i + 1) * ng * S].bitcast(i32),
                                      ps[i * n:(i + 1) * n, 5, 0:words].bitcast(i32)).then_inc(q["qk_ready"], 1)

                def copy_qa(b):
                    both = ps[:, 4:6, :].rearrange("p a b -> p (a b)").bitcast(i32)
                    dve.wait_ge(q["tq_psum"], b.index(2, 1))
                    wait(dve, q["max_psum"], b.index(12, 0))
                    V.tensor_copy(QTa[:, :].bitcast(i32), both).then_inc(q["qa_ready"], 1)

                def copy_k(b):
                    both = ps[:, 4:6, :].rearrange("p a b -> p (a b)").bitcast(i32)
                    dve.wait_ge(q["tk_psum"], b.index(1, 1))
                    wait(dve, q["score_psum"], b.index(6, -6))
                    n = SLOT[1]
                    V.tensor_copy(KT[b.parity][0:n, 0:ng * S].bitcast(i32), both[0:n, :]).then_inc(q["k_ready"], 1)

                def maxima(b, first, end):
                    for m in range(first, end):
                        dve.wait_ge(q["max_psum"], b.index(12, m + 1))
                        bank = ps[:, 4 + m % 2, :]
                        if m < 8:
                            ins = V.reduce_max(mxr[:, 0, H + 2 * m:H + 2 * m + 2], bank.rearrange("p (h n) -> p h n", h=2), AX.X)
                        else:
                            ins = V.reduce_max(mxr[:, 0, 4 * (m - 8):4 * (m - 8) + 4], bank.rearrange("p (h n) -> p h n", h=4), AX.X)
                        ins.then_inc(q["max_done"], 1)

                def fill_maxima(b):
                    c = chain["f"] = Chain(dve, q["front_dve"], FRONT[1], b.index)
                    dve.wait_ge(q["max_done"], b.index(12, 12))
                    piece = [Qx[:, :].rearrange("p (h n) -> p h n", n=64)[:, :, 6 * HD + i] for i in range(3)]
                    c.link(V.tensor_scalar(mxr[:, 1, :], mxr[:, 0, :], -1.0, None, ALU.mult))
                    c.link(V.tensor_copy(piece[0], mxr[:, 1, :]))
                    c.link(V.tensor_tensor(mxr[:, 2, :], mxr[:, 1, :], piece[0], ALU.subtract))
                    c.link(V.tensor_copy(piece[1], mxr[:, 2, :]))
                    V.tensor_tensor(piece[2], mxr[:, 2, :], piece[1], ALU.subtract).then_inc(q["m_ready"], 1)

                def copy_qm(b):
                    c = chain["f"]
                    both = ps[:, 4:6, :].rearrange("p a b -> p (a b)").bitcast(i32)
                    piece = [Qx[:, :].rearrange("p (h n) -> p h n", n=64)[:, :, 6 * HD + i] for i in range(3)]
                    dve.wait_ge(q["tq_psum"], b.index(2, 2))
                    V.tensor_copy(QT[b.parity][:, 0:4 * S].bitcast(i32), both[:, 0:512]).then_inc(q["qk_ready"], 1)
                    for i in range(3):
                        V.memset(piece[i], 0.0).then_inc(q["front_dve"], 1)
                    c.n += 3
                    dve.wait_ge(q["front_dve"], b.index(FRONT[1], c.n))
                    c.end()

                def back_values(b, t):
                    if t == 0:
                        chain["b"] = Chain(dve, q["back_dve"], BACK, b.index)
                        wait(dve, q["yT_psum"], b.index(1, 0))
                    c = chain["b"]
                    dve.wait_ge(q["ot_psum"], b.index(2, t + 1))
                    o = ps[:, 7, :].rearrange("p (h n) -> p h n", n=32)
                    c.link(V.reciprocal(rec[:, t, :], o[:, :, HD]))
                    V.tensor_tensor(y[:, t, :].rearrange("p (h d) -> p h d", d=HD), o[:, :, 0:HD],
                                    rec[:, t, :].unsqueeze(2).to_broadcast([P, H, HD]), ALU.mult).then_inc(q["y_ready"], 1)

                def back_residual(b):
                    c = chain["b"]
                    dve.wait_ge(q["proj_psum"], b.index(1, 1))
                    dve.wait_ge(q["modB_in"][b.parity], b.half * 16 + 16)
                    wait(dve, q["x1_ready"], b.index(1, 0))
                    V.tensor_tensor(attn[:, :, :], ps[:, 7, S:2 * S].rearrange("p (t c) -> p t c", t=2),
                                    modB[b.parity][:, 0:D].unsqueeze(1).to_broadcast([P, 2, D]), ALU.mult).then_inc(q["attn_ready"], 1)
                    c.end()

                def back_logits(b):
                    dve.wait_ge(q["router_psum"], b.index(1, 1))
                    V.tensor_copy(LG[l][:, ds(b.index(2 * E), 2 * E)], ps[:, 7, S:S + 2 * E]).then_inc(q["logits_ready"], 1)

                def step(b, stage):
                    if l == 0:
                        stage(1, mean_squares)
                        step_roots(b)
                        stage(-3, back_logits)
                        stage(-2, back_norm)
                        stage(3, front_norm)
                        stage(-1, back_values, 0)
                        stage(1, front_slots)
                        stage(-1, back_values, 1)
                        stage(1, front_copies)
                        stage(-1, back_residual)
                    else:
                        stage(1, split, 1)
                        step_roots(b)
                        stage(-3, back_logits)
                        stage(1, copy_qa)
                        stage(3, front_norm)
                        stage(-2, back_norm)
                        stage(-1, back_values, 0)
                        stage(1, copy_k)
                        stage(1, maxima, 0, 2)
                        stage(-1, back_values, 1)
                        stage(1, maxima, 2, 6)
                        stage(-1, back_residual)
                        stage(1, maxima, 6, 12)
                        stage(1, fill_maxima)
                        stage(2, split, 0)
                        stage(1, copy_qm)

                steps(dve, step)
                dve.wait_ge(q["logits_ready"], NB)

                c = Chain(dve, route_dve, ROUTE, lambda steps_, n_: l * steps_ + n_)
                te = lambda v: v.rearrange("p (t e) -> p t e", e=E)
                w = [te(rt[i][:, 0:NT * E]) for i in range(5)]
                lg = te(LG[l][:, :])
                tb = lambda v: v.unsqueeze(2).to_broadcast([P, NT, E])
                eb = lambda v: v.unsqueeze(1).to_broadcast([P, NT, E])
                if l == 1:
                    c.link(V.tensor_tensor(lg, lg, eb(gate_b_sb[:, :]), ALU.add))
                for k in range(2):
                    c.link(V.reduce_max(top[:, k, :], lg, AX.X))
                    c.link(V.tensor_tensor(w[0], lg, tb(top[:, k, :]), ALU.is_equal))
                    c.link(V.tensor_tensor(w[0], w[0], eb(expert_no), ALU.mult))
                    c.link(V.tensor_reduce(top[:, 2 + k, :], w[0], AX.X, ALU.min))
                    c.link(V.tensor_tensor(w[1 + k], eb(expert_no), tb(top[:, 2 + k, :]), ALU.is_equal))
                    V.tensor_copy(chosen[:, k, :, :].rearrange("p e t -> p t e"), w[1 + k]).then_inc(q["onehot_ready"], 1)
                    if k == 0:
                        c.link(V.scalar_tensor_tensor(lg, w[1], -3.0e38, lg, ALU.mult, ALU.add))
                V.tensor_tensor(top[:, 4, :], top[:, 1, :], top[:, 0, :], ALU.subtract).then_inc(q["onehot_ready"], 1)
                dve.wait_ge(gate_exp, l + 1)
                g0, g1 = G[l][:, 0:NT], G[l][:, NT:2 * NT]
                c.link(V.tensor_scalar(g1, top[:, 5, :], 1.0, None, ALU.add))
                c.link(V.reciprocal(g0, g1))
                c.link(V.tensor_tensor(g1, top[:, 5, :], g0, ALU.mult))

                c.link(V.memset(rt[3][:, :], 1.0))
                c.link(V.memset(rt[3][:, :].rearrange("p (g t) -> p g t", t=NT)[:, :, 0:1], 0.0))
                dve.wait_ge(q["prefix_psum"], 2)
                c.link(V.tensor_copy(rt[2][:, :], ps[:, 2:4, :].rearrange("p a b -> p (a b)")))
                c.link(V.tensor_tensor_scan(rt[1][:, :], rt[3][:, :], rt[2][:, :], 0.0, ALU.mult, ALU.add))
                c.link(V.tensor_tensor(rt[0][:, :], rt[1][:, :], rt[2][:, :], ALU.subtract))
                c.link(V.tensor_tensor(rt[0][:, :], rt[0][:, :], ps[:, 0:2, :].rearrange("p a b -> p (a b)"), ALU.add))
                count = small[:, 0, :]
                ket = lambda v: v.rearrange("p (k e t) -> p k e t", k=2, e=E)
                oh = chosen[:, :, :, :].rearrange("p k e t -> p (k e t)")
                kt = lambda v: v.rearrange("p (k t) -> p k t", k=2)
                if l == 0:
                    c.link(V.tensor_tensor(rt[4][:, :], rt[0][:, :], oh, ALU.mult))
                    c.link(V.reduce_sum(kt(slots[:, 0, :]), ket(rt[4][:, :]).rearrange("p k e t -> p k t e"), AX.X))
                    c.link(V.tensor_scalar(slots[:, 0, :], slots[:, 0, :], float(CAP), None, ALU.is_lt))
                    c.link(V.tensor_tensor(G[0][:, :], G[0][:, :], slots[:, 0, :], ALU.mult))
                c.link(V.tensor_copy(count, rt[1][:, :].rearrange("p (g t) -> p g t", t=NT)[:, :, NT - 1]))
                n_e, n_i, tiles_f, ends, base = (small[:, 1, 0:E], small[:, 2, 0:E].bitcast(i32), small[:, 3, 0:E],
                                                 small[:, 4, 0:E], small[:, 5, :])
                c.link(V.tensor_tensor(n_e, count[:, 0:E], count[:, E:2 * E], ALU.add))
                c.link(V.tensor_scalar(n_e, n_e, float(ST - 1), None, ALU.add))
                c.link(V.tensor_copy(n_i, n_e))
                c.link(V.tensor_scalar(n_i, n_i, ST.bit_length() - 1, None, ALU.arith_shift_right))
                c.link(V.tensor_copy(tiles_f, n_i))
                c.link(V.memset(small[:, 6, 0:E], 1.0))
                c.link(V.tensor_tensor_scan(ends, small[:, 6, 0:E], tiles_f, 0.0, ALU.mult, ALU.add))
                c.link(V.tensor_tensor(base[:, 0:E], ends, tiles_f, ALU.subtract))
                c.link(V.tensor_scalar(base[:, 0:E], base[:, 0:E], float(ST), None, ALU.mult))
                c.link(V.tensor_tensor(base[:, E:2 * E], base[:, 0:E], count[:, 0:E], ALU.add))
                c.link(V.tensor_tensor(rt[0][:, :].rearrange("p (g t) -> p g t", t=NT), rt[0][:, :].rearrange("p (g t) -> p g t", t=NT),
                                       base.unsqueeze(2).to_broadcast([P, 2 * E, NT]), ALU.add))
                c.link(V.tensor_tensor(rt[4][:, :], rt[0][:, :], oh, ALU.mult))
                c.link(V.reduce_sum(kt(slots[:, 0, :]), ket(rt[4][:, :]).rearrange("p k e t -> p k t e"), AX.X))
                slot_i, part_i = slots[:, 1, :].bitcast(i32), slots[:, 2, :].bitcast(i32)
                c.link(V.tensor_copy(slot_i, slots[:, 0, :]))
                c.link(V.tensor_scalar(part_i, slot_i, P - 1, None, ALU.bitwise_and))
                c.link(V.tensor_copy(slots[:, 3, :], part_i))
                c.link(V.tensor_scalar(part_i, slot_i, P.bit_length() - 1, None, ALU.arith_shift_right))
                c.link(V.tensor_copy(slots[:, 4, :], part_i))
                v = rt[4][:, 0:NJ * E].rearrange("p (j e) -> p j e", e=E)
                c.link(V.tensor_tensor(v, ends.unsqueeze(1).to_broadcast([P, NJ, E]), tile_no.unsqueeze(2).to_broadcast([P, NJ, E]), ALU.is_le))
                c.link(V.reduce_sum(inv[:, 0, 0:NJ], v, AX.X))
                c.link(V.tensor_scalar(inv[:, 0, 0:NJ], inv[:, 0, 0:NJ], float(E - 1), None, ALU.min))
                V.tensor_copy(eid[:, :], inv[:, 0, 0:NJ]).then_inc(q["index_ready"], 1)

                def factors(g):
                    hot = QT[g.parity][:, 0:8 * HI].rearrange("p (r n) -> p r n", r=8)
                    wait(dve, q["perm_scaled"], g.index(1, -1))
                    for r in range(8):
                        last = V.tensor_scalar(hot[:, r, :], block_b[:, :], slots[:, 4, ds(g.index(8, r), 1)], None, ALU.is_equal)
                    last.then_inc(q["perm_ready"], 1)
                    wait(dve, q["perm_used"], g.index(1, -1))
                    for r in range(8):
                        V.tensor_scalar(permA[g.parity][:, r, :], lane_b[:, :], slots[:, 3, ds(g.index(8, r), 1)], None, ALU.is_equal)
                    dve.wait_ge(q["perm_ready"], g.index(2, 1))
                    V.tensor_scalar(permB[g.parity][:, :, 0, :], hot, row_no, None, ALU.mult).then_inc(q["perm_ready"], 1)

                factors(Batch(0, 0))
                factors(Batch(0, 1))
                with dve.Fori(1, NT // 8) as i:
                    factors(Batch(i, 0))
                    factors(Batch(i, 1))
                dve.wait_ge(q["perm_used"], NT // 4)
                c.link(V.tensor_copy(inv[:, 0:2, :], ps[:, 4, 0:2 * HI].rearrange("p (a b) -> p a b", a=2)))
                c.link(V.tensor_tensor(inv[:, 0, :], inv[:, 0, :], inv[:, 1, :], ALU.add))
                c.link(V.tensor_scalar(inv[:, 1, :], inv[:, 0, :], 0.0, float(EMPTY), ALU.is_equal, ALU.mult))
                c.link(V.tensor_scalar(inv[:, 2, :], inv[:, 0, :], 1.0, 0.0, ALU.subtract, ALU.max))
                c.link(V.scalar_tensor_tensor(inv[:, 1, :], inv[:, 2, :], 0.0, inv[:, 1, :], ALU.add, ALU.add))
                c.link(V.tensor_copy(sca_i[:, :], inv[:, 1, :]))
                c.link(V.tensor_copy(gat_i[:, :], inv[:, 2, :]))
                V.tensor_scalar(gat_i[:, :], gat_i[:, :], N - 1, None, ALU.bitwise_and).then_inc(q["index_ready"], 1)
                dve.sem_inc(route_dve, ROUTE - c.n)

                def copy_x(j):
                    dve.wait_ge(q["xT_psum"], j.index(1, 1))
                    wait(dve, q["up_psum"], j.index(1, -1))
                    V.tensor_copy(xT[j.phase % 2][:, :], ps[:, j.phase % 2, 0:ST]).then_inc(q["xT_ready"], 1)

                def product(j):
                    dve.wait_ge(q["up_act"], j.index(2, 2))
                    wait(dve, q["mid_psum"], j.index(1, -1))
                    up = ps[:, 2 + 2 * (j.phase % 2):4 + 2 * (j.phase % 2), :].rearrange("p a b -> p (a b)")
                    for f in range(2):
                        V.scalar_tensor_tensor(hz[j.phase % 2][:, f * ST:(f + 1) * ST], up[:, 512 + f * ST:512 + (f + 1) * ST],
                                               we[j.phase][:, BIAS + 2 + f:BIAS + 3 + f], hid[j.phase % 2][:, f * ST:(f + 1) * ST],
                                               ALU.add, ALU.mult).then_inc(q["z_ready"], 1)

                def copy_y(j):
                    dve.wait_ge(q["down_psum"], j.index(1, 1))
                    wait(dve, q["scattered"][j.phase], j.quarter * SCATTER[l])
                    if l == 0:
                        ins = V.tensor_copy(yo[j.phase][:, :, :], ps[:, 6 + j.phase % 2, 0:2 * P].rearrange("p (s c) -> p s c", s=2))
                    else:
                        ins = V.tensor_tensor(yo[j.phase][:, :, :], ps[:, 7, 0:2 * P].rearrange("p (s c) -> p s c", s=2),
                                              we[j.phase][:, BIAS + 6:BIAS + 6 + D].unsqueeze(1).to_broadcast([P, 2, D]), ALU.add)
                    ins.then_inc(q["y_out"], 1)

                def v_first():
                    copy_x(Tile(0, 0))
                    if l == 1:
                        product(Tile(0, 0))
                    copy_x(Tile(0, 1))

                def v_step(j, ahead, up, transposed, mid, down):
                    if transposed:
                        copy_x(j.ahead(2))
                    if up and l == 1:
                        product(j.ahead(1))
                    if down:
                        copy_y(j.ahead(-1))

                tiles(dve, v_first, v_step)

            def final(b):
                c = Chain(dve, final_dve, 3, b.index)
                yb = yfin[b.phase]
                dve.wait_ge(final_in[b.phase], b.quarter * 48 + 48)
                dve.wait_ge(final_scaled, b.index(1, 1))
                c.link(V.tensor_tensor(yb[:, 0], yb[:, 0], yb[:, 1], ALU.add))
                c.link(V.tensor_tensor(yb[:, 0], yb[:, 0], gfin[b.phase].unsqueeze(1).to_broadcast([P, 2, D]), ALU.mult))
                xb = Xt[:, ds(b.index(S), S)]
                c.link(V.tensor_tensor(xb, xb, yb[:, 0].rearrange("p t c -> p (t c)"), ALU.add))
                c.end()
                dve.sem_inc(final_used, 1)

            fours(dve, final)


def kernel(**inputs):
    import numpy as np
    import concourse.bacc as bacc
    from concourse.bass_utils import run_bass_kernel_spmd

    a = {k: np.asarray(v) for k, v in inputs.items()}

    def chunks(w):
        e, r, m = w.shape
        return w.reshape(e, r // P, P, m).transpose(0, 2, 1, 3).reshape(e, P, -1)

    def columns(v):
        return v.reshape(E, -1, P).transpose(0, 2, 1)

    arrays = {
        "x": a["L0_attn_x"].reshape(N, D),
        "c_t": np.stack([a["L0_c"].T, a["L1_c"].T]),
        "wmod": np.stack([a["L0_wmod"], a["L1_wmod"]]),
        "wqkv": np.stack([np.concatenate([a["L0_attn_w_q"].T, a["L0_attn_w_k"].T, a["L0_attn_w_v"].T], axis=1),
                          a["L1_attn_w_attn"]]),
        "wo": np.stack([a["L0_attn_w_o"].T, a["L1_attn_w_proj"]]),
        "router": np.stack([a["L0_ffn_router_w"].T, a["L1_ffn_gate_w"]]),
        "gate_b": np.repeat(a["L1_ffn_gate_b"][None], P, axis=0),
        "exp0": np.concatenate([chunks(a["L0_ffn_w1"]), chunks(a["L0_ffn_w2"])], axis=2),
        "exp1": np.concatenate([chunks(a["L1_ffn_w1"]), chunks(a["L1_ffn_w2"]), chunks(a["L1_ffn_wg"]), chunks(a["L1_ffn_w3"]),
                                columns(a["L1_ffn_b1"]), columns(a["L1_ffn_b2"]), columns(a["L1_ffn_bg"]),
                                np.repeat(a["L1_ffn_b3"][:, None], P, axis=1)], axis=2),
    }
    arrays = {k: np.ascontiguousarray(v) for k, v in arrays.items()}
    nc = bacc.Bacc("TRN2", target_bir_lowering=False, num_devices=1)
    args = [nc.dram_tensor(k, v.shape, mybir.dt.from_np(v.dtype), kind="ExternalInput").ap() for k, v in arrays.items()]
    out = nc.dram_tensor("out", (N, D), mybir.dt.float32, kind="ExternalOutput").ap()
    adaln_kernel(nc, *args, out)
    r = run_bass_kernel_spmd(nc, [arrays], core_ids=[0])
    return r.results[0]["out"].reshape(NB, S, D)
```
